# Optimizing a Trainium2 kernel written in Bass

```python
import numpy as np
import jax
import jax.numpy as jnp

def _softmax(x, axis=-1):
    return jax.nn.softmax(x, axis=axis)

def _gelu(x):
    return jax.nn.gelu(x, approximate=True)

def _silu(x):
    return jax.nn.silu(x)

def _sigmoid(x):
    return jax.nn.sigmoid(x)

def _layernorm(x, axis=-1, eps=1e-05):
    m = jnp.mean(x, axis=axis, keepdims=True)
    v = jnp.var(x, axis=axis, keepdims=True)
    return (x - m) / jnp.sqrt(v + eps)

def _scatter_add(tgt, idx, src, axis=0):
    return tgt.at[idx].add(src)

def _segment_sum(src, seg, n):
    return jax.ops.segment_sum(src, seg, n)
kernel_name = 'mk_seq_preln_d1_jaxref_r8_6cd500'

def setup_inputs(seed: int=0):
    np.random.seed(seed)
    _w = jnp.asarray

    def _L0_attn_setup():
        import jax, jax.numpy as jnp
        import numpy as np
        import math
        E = 256
        H = 16
        HD = E // H // 2
        DEPTH = 12
        LAMBDA_INIT = 0.8 - 0.6 * math.exp(-0.3 * DEPTH)
        key = jax.random.key(seed)
        ks = jax.random.split(key, 9)
        s = 0.02
        return {'x': jax.random.normal(ks[0], (2, 256, E), jnp.float32), 'Wq': jax.random.normal(ks[1], (E, E), jnp.float32) * s, 'Wk': jax.random.normal(ks[2], (E, E), jnp.float32) * s, 'Wv': jax.random.normal(ks[3], (E, E), jnp.float32) * s, 'Wo': jax.random.normal(ks[4], (E, E), jnp.float32) * s, 'lq1': jax.random.normal(ks[5], (HD,), jnp.float32) * 0.1, 'lk1': jax.random.normal(ks[6], (HD,), jnp.float32) * 0.1, 'lq2': jax.random.normal(ks[7], (HD,), jnp.float32) * 0.1, 'lk2': jax.random.normal(ks[8], (HD,), jnp.float32) * 0.1}
    _L0_attn_in = _L0_attn_setup()

    def _L0_ffn_setup():
        import jax, jax.numpy as jnp
        import numpy as np
        HIDDEN = 256
        MOE_INTER = 128
        SHARED_INTER = 512
        N_EXPERTS = 16
        TOP_K = 2
        N_GROUP = 4
        TOPK_GROUP = 2
        NORM_TOPK_PROB = True
        ROUTED_SCALING = 1.0

        def relu2(x):
            r = jax.nn.relu(x)
            return r * r

        def _get_topk_indices(scores, e_bias):
            T, E = scores.shape
            s = scores + e_bias[None, :]
            gsz = E // N_GROUP
            group_scores = jax.lax.top_k(s.reshape(T, N_GROUP, gsz), 2)[0].sum(-1)
            group_idx = jax.lax.top_k(group_scores, TOPK_GROUP)[1]
            group_mask = jnp.zeros((T, N_GROUP), dtype=bool).at[jnp.arange(T)[:, None], group_idx].set(True)
            score_mask = jnp.repeat(group_mask, gsz, axis=1)
            masked = jnp.where(score_mask, s, 0.0)
            topk_indices = jax.lax.top_k(masked, TOP_K)[1]
            return jax.lax.stop_gradient(topk_indices)

        def _router(x_flat, router_weight, e_bias):
            logits = jnp.einsum('th,eh->te', x_flat.astype(jnp.float32), router_weight.astype(jnp.float32))
            scores = jax.nn.sigmoid(logits)
            topk_indices = _get_topk_indices(scores, e_bias)
            topk_weights = jnp.take_along_axis(scores, topk_indices, axis=1)
            if NORM_TOPK_PROB:
                topk_weights = topk_weights / (topk_weights.sum(-1, keepdims=True) + 1e-20)
            return (topk_indices, topk_weights * ROUTED_SCALING)
        key = jax.random.key(seed)
        ks = jax.random.split(key, 6)
        s = 0.02
        hidden_states = jax.random.normal(ks[0], (1, 256, HIDDEN), dtype=jnp.float32)
        router_weight = jax.random.normal(ks[1], (N_EXPERTS, HIDDEN), dtype=jnp.float32) * s
        e_bias = jnp.zeros((N_EXPERTS,), dtype=jnp.float32)
        w_up = jax.random.normal(ks[2], (N_EXPERTS, HIDDEN, MOE_INTER), dtype=jnp.float32) * s
        w_down = jax.random.normal(ks[3], (N_EXPERTS, MOE_INTER, HIDDEN), dtype=jnp.float32) * s
        shared_up = jax.random.normal(ks[4], (HIDDEN, SHARED_INTER), dtype=jnp.float32) * s
        shared_down = jax.random.normal(ks[5], (SHARED_INTER, HIDDEN), dtype=jnp.float32) * s
        return {'hidden_states': hidden_states, 'router_weight': router_weight, 'e_bias': e_bias, 'w_up': w_up, 'w_down': w_down, 'shared_up': shared_up, 'shared_down': shared_down}
    _L0_ffn_in = _L0_ffn_setup()
    _d = {'L0_attn_x': _L0_attn_in['x'], 'L0_attn_Wq': _L0_attn_in['Wq'], 'L0_attn_Wk': _L0_attn_in['Wk'], 'L0_attn_Wv': _L0_attn_in['Wv'], 'L0_attn_Wo': _L0_attn_in['Wo'], 'L0_attn_lq1': _L0_attn_in['lq1'], 'L0_attn_lk1': _L0_attn_in['lk1'], 'L0_attn_lq2': _L0_attn_in['lq2'], 'L0_attn_lk2': _L0_attn_in['lk2'], 'L0_ffn_router_weight': _L0_ffn_in['router_weight'], 'L0_ffn_e_bias': _L0_ffn_in['e_bias'], 'L0_ffn_w_up': _L0_ffn_in['w_up'], 'L0_ffn_w_down': _L0_ffn_in['w_down'], 'L0_ffn_shared_up': _L0_ffn_in['shared_up'], 'L0_ffn_shared_down': _L0_ffn_in['shared_down']}
    _x0 = _d['L0_attn_x']
    _d['L0_attn_x'] = jax.random.normal(jax.random.fold_in(jax.random.key(seed), 1), (4, 512, 256), dtype=_x0.dtype)
    del _x0
    return _d

def reference(L0_attn_x, L0_attn_Wq, L0_attn_Wk, L0_attn_Wv, L0_attn_Wo, L0_attn_lq1, L0_attn_lk1, L0_attn_lq2, L0_attn_lk2, L0_ffn_router_weight, L0_ffn_e_bias, L0_ffn_w_up, L0_ffn_w_down, L0_ffn_shared_up, L0_ffn_shared_down):

    def _L0_attn_ref(x, Wq, Wk, Wv, Wo, lq1, lk1, lq2, lk2):
        import jax, jax.numpy as jnp
        import numpy as np
        import math
        E = 256
        H = 16
        HD = E // H // 2
        DEPTH = 12
        LAMBDA_INIT = 0.8 - 0.6 * math.exp(-0.3 * DEPTH)
        b, t, e = x.shape
        scaling = HD ** (-0.5)
        q = (x @ Wq).reshape(b, t, 2 * H, HD).transpose(0, 2, 1, 3) * scaling
        k = (x @ Wk).reshape(b, t, 2 * H, HD).transpose(0, 2, 1, 3)
        v = (x @ Wv).reshape(b, t, H, 2 * HD).transpose(0, 2, 1, 3)
        scores = jnp.einsum('bhqd,bhkd->bhqk', q, k)
        causal = jnp.triu(jnp.full((t, t), -jnp.inf, dtype=jnp.float32), 1)
        aw = jax.nn.softmax((scores + causal).astype(jnp.float32), axis=-1)
        lam = jnp.exp(jnp.sum(lq1 * lk1)) - jnp.exp(jnp.sum(lq2 * lk2)) + LAMBDA_INIT
        aw = aw.reshape(b, H, 2, t, t)
        aw = aw[:, :, 0] - lam * aw[:, :, 1]
        attn = jnp.einsum('bhqk,bhkd->bhqd', aw, v)
        attn = attn * jax.lax.rsqrt(jnp.mean(attn * attn, axis=-1, keepdims=True) + 1e-05)
        attn = attn * (1.0 - LAMBDA_INIT)
        attn = attn.transpose(0, 2, 1, 3).reshape(b, t, H * 2 * HD)
        return attn @ Wo

    def _L0_ffn_ref(hidden_states, router_weight, e_bias, w_up, w_down, shared_up, shared_down):
        import jax, jax.numpy as jnp
        import numpy as np
        HIDDEN = 256
        MOE_INTER = 128
        SHARED_INTER = 512
        N_EXPERTS = 16
        TOP_K = 2
        N_GROUP = 4
        TOPK_GROUP = 2
        NORM_TOPK_PROB = True
        ROUTED_SCALING = 1.0

        def relu2(x):
            r = jax.nn.relu(x)
            return r * r

        def _get_topk_indices(scores, e_bias):
            T, E = scores.shape
            s = scores + e_bias[None, :]
            gsz = E // N_GROUP
            group_scores = jax.lax.top_k(s.reshape(T, N_GROUP, gsz), 2)[0].sum(-1)
            group_idx = jax.lax.top_k(group_scores, TOPK_GROUP)[1]
            group_mask = jnp.zeros((T, N_GROUP), dtype=bool).at[jnp.arange(T)[:, None], group_idx].set(True)
            score_mask = jnp.repeat(group_mask, gsz, axis=1)
            masked = jnp.where(score_mask, s, 0.0)
            topk_indices = jax.lax.top_k(masked, TOP_K)[1]
            return jax.lax.stop_gradient(topk_indices)

        def _router(x_flat, router_weight, e_bias):
            logits = jnp.einsum('th,eh->te', x_flat.astype(jnp.float32), router_weight.astype(jnp.float32))
            scores = jax.nn.sigmoid(logits)
            topk_indices = _get_topk_indices(scores, e_bias)
            topk_weights = jnp.take_along_axis(scores, topk_indices, axis=1)
            if NORM_TOPK_PROB:
                topk_weights = topk_weights / (topk_weights.sum(-1, keepdims=True) + 1e-20)
            return (topk_indices, topk_weights * ROUTED_SCALING)
        orig_shape = hidden_states.shape
        x = hidden_states.reshape(-1, HIDDEN)
        T = x.shape[0]
        topk_indices, topk_weights = _router(x, router_weight, e_bias)
        combine = jnp.zeros((T, N_EXPERTS), dtype=topk_weights.dtype).at[jnp.arange(T)[:, None], topk_indices].add(topk_weights)
        h1 = jnp.einsum('th,ehi->tei', x, w_up)
        a = relu2(h1) * combine[:, :, None]
        routed = jnp.einsum('tei,eih->th', a, w_down)
        shared = relu2(hidden_states @ shared_up) @ shared_down
        return routed.reshape(orig_shape) + shared
    x = L0_attn_x
    x = x + _L0_attn_ref(_layernorm(x, axis=-1), L0_attn_Wq, L0_attn_Wk, L0_attn_Wv, L0_attn_Wo, L0_attn_lq1, L0_attn_lk1, L0_attn_lq2, L0_attn_lk2)
    x = x + _L0_ffn_ref(_layernorm(x, axis=-1), L0_ffn_router_weight, L0_ffn_e_bias, L0_ffn_w_up, L0_ffn_w_down, L0_ffn_shared_up, L0_ffn_shared_down)
    return x

_drawn_inputs = setup_inputs


def setup_inputs(seed=0):
    import zlib

    import numpy as np

    out = dict(_drawn_inputs(seed))
    spreads = {'L0_ffn_e_bias': (0.0, 0.332)}
    factors = {'L0_attn_lq1': 8.0,
     'L0_attn_lk1': 8.0,
     'L0_attn_lq2': 7.392,
     'L0_attn_lk2': 6.792,
     'L0_ffn_router_weight': 4.368,
     'L0_ffn_w_up': 3.076,
     'L0_ffn_w_down': 2.812}
    for name, (base, spread) in spreads.items():
        noise = np.random.default_rng([zlib.crc32(name.encode()), seed]).standard_normal(out[name].shape)
        drawn = base * np.exp(spread * noise) if base else spread * noise
        out[name] = jnp.asarray(drawn.astype(out[name].dtype))
    for name, factor in factors.items():
        out[name] = (out[name] * factor).astype(out[name].dtype)
    return out
```

```python
import math
from contextlib import ExitStack
from collections import namedtuple

import concourse.bass as bass
from concourse import mybir

F32 = mybir.dt.float32
F32R = mybir.dt.float32r
BF16 = mybir.dt.bfloat16
ALU = mybir.AluOpType
ACT = mybir.ActivationFunctionType
AX = mybir.AxisListType

P = 128
LAMBDA_INIT = 0.8 - 0.6 * math.exp(-0.3 * 12)
EPS = 1e-5
GROUPS = 4
MASKED = -2.0e38
FAR = -1.0e30


class Shapes:
    pass


class Tensors:
    pass


def named(found):
    return namedtuple("Named", sorted(found))(**found)


def allocator(nc, stack, where, block=""):
    def tensor(name, shape, dt=F32):
        where[name] = stack.enter_context(nc.sbuf_tensor(block + name, list(shape), dt))

    def banks(name, n):
        where[name] = [stack.enter_context(nc.psum_tensor(f"{block}{name}{i}", [P, 512], F32))
                                for i in range(n)]

    def sems(names):
        for name in names.split():
            where[name] = stack.enter_context(nc.semaphore(block + name))
    return tensor, banks, sems


def chained(eng, semaphore, base=0):
    count = [0]

    def link(ins):
        count[0] += 1
        ins.then_inc(semaphore, 1)
        eng.wait_ge(semaphore, base + count[0])
    link.count = count
    return link


def stand(eng, passed):
    eng.sem_inc(passed, 1)


def matmul3(pe, o, w, m, start=True, stop=True):
    pe.matmul(o, w[0], m[1], start=start, stop=False)
    pe.matmul(o, w[1], m[0], start=False, stop=False)
    return pe.matmul(o, w[0], m[0], start=False, stop=stop)


def entries(buf, first, n):
    return buf[:, bass.ds(first, n), :]


def entry(buf, at):
    return entries(buf, at, 1).rearrange("p a s -> p (a s)")


def project(nc, D, K, S):
    B, T, E, TB, KC, G, HD, VD, VW = D.B, D.T, D.E, D.TB, D.KC, D.G, D.HD, D.VD, D.VW
    made = {}
    with ExitStack() as st:
        tensor, banks, sems = allocator(nc, st, made, "project_")
        tensor("w_raw", [P, 4, KC, E])
        tensor("w_h", [P, 3, KC, E], F32R)
        tensor("w_l", [P, 3, KC, E], F32R)
        tensor("xn", [P, TB, E])
        tensor("stats", [P, TB, 6])
        tensor("mv", [P, TB, 2])
        tensor("std", [P, TB])
        tensor("rstd", [P, TB])
        tensor("xT_h", [P, KC, T], F32R)
        tensor("xT_l", [P, KC, T], F32R)
        tensor("part_h", [P, 4, T], F32R)
        tensor("part_l", [P, 4, T], F32R)
        tensor("lam_in", [P, 4, HD])
        tensor("lam_pr", [P, 2, HD])
        tensor("lam_sum", [P, 2])
        tensor("lam_exp", [P, 2])
        banks("ps_t", KC)
        banks("ps_qk", 4)
        banks("ps_v", 2)
        sems("passed x_loaded w_loaded lam_loaded eps_set ident_set ones_set w_split dve_step var_ready "
             "std_ready xn_ready xT_turned xTh_ready xTl_ready qk_done v_done ph_ready pl_ready "
             "v_copied parts_stored lam_dot lam_exped")
        M = named(made)
        LN_STEPS = 2 * TB
        STORED = 8 * 16

        block = st.enter_context(nc.Block())

        @block.sync
        def _(sp):
            with sp.Fori(0, B) as b:
                sp.dma_start(entries(K.x_sb, b * TB, TB),
                             S.x.rearrange("b (t p) e -> p (b t) e", p=P)[:, bass.ds(b * TB, TB), :]
                             ).then_inc(M.x_loaded, 16)
                sp.wait_ge(M.x_loaded, 16 * b + 16)
                stand(sp, M.passed)
            with sp.Fori(0, B) as b:
                sp.wait_ge(M.ph_ready, 4 * b + 4)
                stand(sp, M.passed)
                sp.wait_ge(M.pl_ready, 4 * b + 4 + 4)
                for half, part in enumerate((M.part_h, M.part_l)):
                    for c in range(4):
                        steps = bass.ds(b * G + (c % KC) * (G // KC), G // KC)
                        dst = S.qk[2 * (c // KC) + half, steps].rearrange("g r t -> (g r) t")
                        sp.dma_start(dst.bitcast(F32), part[:, c, :].bitcast(F32)
                                     ).then_inc(M.parts_stored, 16)
            sp.wait_ge(M.parts_stored, STORED * B + 16)

        @block.scalar
        def _(act):
            for n, w in enumerate((S.wq, S.wk, S.wv, S.wo)):
                act.dma_start(M.w_raw[:, n], w.rearrange("(c p) n -> p c n", p=P)).then_inc(M.w_loaded, 16)
            for n, v in enumerate((S.lq1, S.lk1, S.lq2, S.lk2)):
                act.dma_start(M.lam_in[:, n, :], v.partition_broadcast(P)).then_inc(M.lam_loaded, 16)
            act.wait_ge(M.eps_set, 1)

            def spread(b):
                act.wait_ge(M.var_ready, b + 1)
                act.activation(M.std[:, :], M.mv[:, :, 1], ACT.Sqrt, bias=K.eps_col[:, 0:1]
                               ).then_inc(M.std_ready, 1)

            def turned_high(b):
                act.wait_ge(M.xT_turned, b + 2)
                act.wait_ge(M.v_done, b + 1)
                for c in range(KC):
                    act.copy(M.xT_h[:, c, :], M.ps_t[c][:, :]).then_inc(M.xTh_ready, 1)

            def parts_high(b):
                act.wait_ge(M.parts_stored, STORED * b + 16)
                for c in range(4):
                    act.wait_ge(M.qk_done, 4 * b + c + 1)
                    act.activation(M.part_h[:, c, :], M.ps_qk[c][:, :], ACT.Copy,
                                   scale=D.SCALE if c < KC else 1.0).then_inc(M.ph_ready, 1)
                act.wait_ge(M.v_done, b + 2)
                for t in range(TB):
                    v_b = entries(K.v_sb, b * G, G).rearrange("p g (t h w) -> p g t h w", t=TB, w=VW)
                    act.copy(v_b[:, :, t, :, 0:VD],
                             M.ps_v[t // 2][:, (t % 2) * E:(t % 2 + 1) * E].rearrange(
                                 "p (g h d) -> p g h d", g=G, d=VD)).then_inc(M.v_copied, 1)

            spread(0)
            act.wait_ge(M.ones_set, 1)
            with act.Fori(0, B - 1) as b:
                turned_high(b)
                spread(b + 1)
                parts_high(b)
            turned_high(B - 1)
            parts_high(B - 1)
            act.wait_ge(M.lam_dot, 1)
            act.activation(M.lam_exp[:, :], M.lam_sum[:, :], ACT.Exp).then_inc(M.lam_exped, 1)

        @block.gpsimd
        def _(pool):
            pool.sem_inc(M.parts_stored, 16)
            pool.sem_inc(M.v_copied, 4)
            pool.sem_inc(M.v_done, 1)
            pool.sem_inc(M.xT_turned, 1)
            pool.sem_inc(M.xTl_ready, KC)
            pool.sem_inc(M.pl_ready, 4)
            pool.memset(K.eps_col[:, :], EPS).then_inc(M.eps_set, 1)
            pool.memset(K.ident[:, :], 1.0).then_inc(M.ident_set, 1)
            pool.wait_ge(M.ident_set, 1)
            pool.affine_select(out=K.ident[:, :], in_=K.ident[:, :], pattern=[[-1, P]],
                               compare_op=ALU.is_equal, fill=0.0, base=0,
                               channel_multiplier=1).then_inc(M.ident_set, 1)
            pool.wait_ge(M.w_loaded, 64)
            pool.tensor_copy(M.w_h[:, :, :, :], M.w_raw[:, 0:3]).then_inc(M.w_split, 1)
            pool.wait_ge(M.w_split, 1)
            pool.tensor_tensor(M.w_l[:, :, :, :], M.w_raw[:, 0:3], M.w_h[:, :, :, :].bitcast(F32),
                               ALU.subtract).then_inc(M.w_split, 1)
            pool.memset(K.v_sb[:, :, :], 1.0).then_inc(M.ones_set, 1)
            pool.tensor_copy(K.wo_h[:, :, :], M.w_raw[:, 3]).then_inc(M.w_split, 1)
            pool.wait_ge(M.w_split, 3)
            pool.tensor_tensor(K.wo_l[:, :, :], M.w_raw[:, 3], K.wo_h[:, :, :].bitcast(F32),
                               ALU.subtract).then_inc(M.w_split, 1)

        @block.vector
        def _(dve):
            def norm(b):
                dve.wait_ge(M.x_loaded, 16 * b + 16)
                stand(dve, M.passed)
                for t in range(TB):
                    dve.bn_stats(M.stats[:, t, :], entry(K.x_sb, b * TB + t)).then_inc(M.dve_step, 1)
                dve.wait_ge(M.dve_step, LN_STEPS * b + TB)
                stand(dve, M.passed)
                for t in range(TB):
                    dve.bn_aggr(M.mv[:, t, :], M.stats[:, t, :]).then_inc(
                        M.var_ready if t == TB - 1 else M.dve_step, 1)
                dve.wait_ge(M.std_ready, b + 1)
                dve.reciprocal(M.rstd[:, :], M.std[:, :]).then_inc(M.dve_step, 1)
                dve.wait_ge(M.dve_step, LN_STEPS * b + 2 * TB)
                dve.wait_ge(M.xT_turned, b + 1)
                for t in range(TB):
                    dve.tensor_scalar(M.xn[:, t, :], entry(K.x_sb, b * TB + t), M.mv[:, t, 0:1],
                                      M.rstd[:, t:t + 1], ALU.subtract, ALU.mult).then_inc(M.xn_ready, 1)

            def turned_low(b):
                for c in range(KC):
                    dve.wait_ge(M.xTh_ready, KC * b + c + 1)
                    dve.tensor_tensor(M.xT_l[:, c, :], M.ps_t[c][:, :], M.xT_h[:, c, :].bitcast(F32),
                                      ALU.subtract).then_inc(M.xTl_ready, 1)

            def parts_low(b):
                for c in range(4):
                    dve.wait_ge(M.ph_ready, 4 * b + c + 1)
                    dve.scalar_tensor_tensor(M.part_l[:, c, :], M.ps_qk[c][:, :],
                                             D.SCALE if c < KC else 1.0,
                                             M.part_h[:, c, :].bitcast(F32), ALU.mult,
                                             ALU.subtract).then_inc(M.pl_ready, 1)

            norm(0)
            with dve.Fori(0, B - 1) as b:
                turned_low(b)
                norm(b + 1)
                parts_low(b)
            turned_low(B - 1)
            parts_low(B - 1)
            link = chained(dve, M.dve_step, LN_STEPS * B)
            dve.wait_ge(M.lam_loaded, 64)
            pairs = M.lam_in[:, :, :].rearrange("p (a two) d -> p a two d", two=2)
            link(dve.tensor_tensor(M.lam_pr[:, :, :], pairs[:, :, 0, :], pairs[:, :, 1, :], ALU.mult))
            dve.tensor_reduce(M.lam_sum[:, :], M.lam_pr[:, :, :], AX.X, ALU.add).then_inc(M.lam_dot, 1)
            dve.wait_ge(M.lam_exped, 1)
            link(dve.tensor_tensor(K.neg_lam[:, :], M.lam_exp[:, 1:2], M.lam_exp[:, 0:1], ALU.subtract))
            link(dve.tensor_scalar(K.neg_lam[:, :], K.neg_lam[:, :], -LAMBDA_INIT, None, ALU.add))

        @block.tensor
        def _(pe):
            pe.wait_ge(M.ident_set, 2)
            with pe.Fori(0, B) as b:
                pe.wait_ge(M.xn_ready, TB * b + TB)
                pe.wait_ge(M.xTl_ready, KC * b + KC)
                for c in range(KC):
                    for t in range(TB):
                        ins = pe.transpose(M.ps_t[c][:, t * P:(t + 1) * P],
                                           M.xn[:, t, c * P:(c + 1) * P], K.ident[:, :])
                ins.then_inc(M.xT_turned, 1)
                pe.wait_ge(M.w_split, 2)
                pe.wait_ge(M.xTl_ready, KC * b + 2 * KC)
                pe.wait_ge(M.pl_ready, 4 * b + 4)
                for part in range(4):
                    n, m = part // KC, part % KC
                    for c in range(KC):
                        ins = matmul3(pe, M.ps_qk[part][:, :],
                                      [w[:, n, c, m * P:(m + 1) * P] for w in (M.w_h, M.w_l)],
                                      [x[:, c, :] for x in (M.xT_h, M.xT_l)],
                                      start=c == 0, stop=c == KC - 1)
                    ins.then_inc(M.qk_done, 1)
                pe.wait_ge(M.v_copied, 4 * b + 4)
                for t in range(TB):
                    for c in range(KC):
                        ins = matmul3(pe, M.ps_v[t // 2][:, (t % 2) * E:(t % 2 + 1) * E],
                                      [x[:, c, t * P:(t + 1) * P] for x in (M.xT_h, M.xT_l)],
                                      [w[:, 2, c, :] for w in (M.w_h, M.w_l)],
                                      start=c == 0, stop=c == KC - 1)
                ins.then_inc(M.v_done, 1)


def attend(nc, D, K, S):
    T, TB, VD, VW, SH, ROWS, HD, STEPS = D.T, D.TB, D.VD, D.VW, D.SH, D.ROWS, D.HD, D.STEPS
    RING = 4
    ROUNDS = STEPS // RING
    made = {}
    with ExitStack() as st:
        tensor, banks, sems = allocator(nc, st, made, "attend_")
        tensor("k_ring", [P, RING, T], F32R)
        tensor("q_ring", [P, RING, SH, T], F32R)
        tensor("v_ring", [P, RING, TB, 2, VW])
        tensor("m_rows", [2 * SH, RING, T], F32R)
        tensor("probs", [P, 5, 2, 512])
        tensor("pv_copy", [P, T])
        tensor("sums_pv", [P, 2, TB, SH, VW])
        tensor("recip", [P, 2, TB, 2, 2])
        tensor("first", [P, TB, 2, VD])
        tensor("second", [P, TB, 2, VD])
        tensor("neg_max", [P, TB, SH])
        tensor("neg_max2", [P, TB, 2, SH], F32R)
        tensor("ident_b", [P, P], BF16)
        tensor("mask_b", [P, 4, P], BF16)
        tensor("zeros_b", [P, T], BF16)
        made["ps_s"] = st.enter_context(nc.psum_tensor("ps_s", [P, 2, 2, 512], F32))
        banks("ps_m", 2)
        banks("ps_pv", 1)
        banks("ps_turn", 1)
        KQ_DMAS = 3 + 3 * SH
        kq_loaded = [st.enter_context(nc.semaphore(f"kq_loaded{j}")) for j in range(RING)]
        m_loaded = [st.enter_context(nc.semaphore(f"m_loaded{j}")) for j in range(RING)]
        sems("passed buffers_set masks_set pv_zeroed s_filled exp_done max_filled max_read max_step max_halves m_turned "
             "m_copied v_ready cut_done pv_stage pv_copied out_turned acc_stored recip_step recip_ready parts_ready mixed")
        M = named(made)

        def chunk(u):
            if u < 2:
                return [(n, 2 * u + n, 0, 0) for n in range(2)]
            if u < 4:
                return [(n, 2 * (u - 2) + n, kb, col) for n in range(2) for kb, col in ((1, 0), (3, 384))]
            return [(s // 2, s, 2, 256 * (s % 2)) for s in range(SH)]

        CHUNKS = 5
        FILLS = [(3, [s]) for s in range(SH)] + [(2, [s]) for s in range(SH)] + [(1, [0, 1]), (1, [2, 3])] \
            + [(0, list(range(SH)))]
        NF = len(FILLS)

        block = st.enter_context(nc.Block())

        @block.sync
        def _(sp):
            def load(i, j):
                for c, half in enumerate((2, 3, 2)):
                    sp.dma_start(M.k_ring[c * ROWS:(c + 1) * ROWS, j, :].bitcast(F32),
                                 S.qk[half, bass.ds(i, 1)].rearrange("g r t -> (g r) t").bitcast(F32)
                                 ).then_inc(kq_loaded[j], 16)
                for c, half in enumerate((0, 0, 1)):
                    for s in range(SH):
                        row = c * ROWS + s * HD
                        sp.dma_start(M.q_ring[row:row + HD, j, s, :].bitcast(F32),
                                     S.qk[half, bass.ds(i, 1), s * HD:(s + 1) * HD].rearrange(
                                         "g r t -> (g r) t").bitcast(F32)
                                     ).then_inc(kq_loaded[j], 16)

            def load_max(i, j):
                sp.wait_ge(M.m_copied, i + 1)
                for s in range(SH):
                    sp.dma_start(M.q_ring[3 * ROWS:3 * ROWS + 2, j, s, :].bitcast(F32),
                                 M.m_rows[s::SH, j, :].bitcast(F32)).then_inc(m_loaded[j], 16)

            sp.wait_ge(M.buffers_set, 2)
            for j in range(RING):
                load(j, j)
            load_max(0, 0)

            def step(i, j, last=False):
                if not (last and j == RING - 1):
                    load_max(i + 1, (j + 1) % RING)
                if not last:
                    sp.wait_ge(M.s_filled, CHUNKS * i + CHUNKS)
                    load(i + RING, j)

            with sp.Fori(0, ROUNDS - 1) as r:
                for j in range(RING):
                    step(r * RING + j, j)
            for j in range(RING):
                step(STEPS - RING + j, j, last=True)

        @block.gpsimd
        def _(pool):
            pool.memset(M.q_ring[:, :, :, :].bitcast(F32), 0.0).then_inc(M.buffers_set, 1)
            pool.memset(M.k_ring[:, :, :].bitcast(F32), 1.0).then_inc(M.buffers_set, 1)
            pool.memset(M.zeros_b[:, :], 0.0).then_inc(M.masks_set, 1)
            pool.memset(M.mask_b[:, :, :], MASKED).then_inc(M.masks_set, 1)
            pool.memset(M.ident_b[:, :], 1.0).then_inc(M.masks_set, 1)
            pool.wait_ge(M.masks_set, 3)
            pool.affine_select(out=M.mask_b[:, :, :], in_=M.mask_b[:, :, :], pattern=[[0, 4], [1, P]],
                               compare_op=ALU.is_gt, fill=0.0, base=0,
                               channel_multiplier=-1).then_inc(M.masks_set, 1)
            pool.affine_select(out=M.ident_b[:, :], in_=M.ident_b[:, :], pattern=[[-1, P]],
                               compare_op=ALU.is_equal, fill=0.0, base=0,
                               channel_multiplier=1).then_inc(M.masks_set, 1)

            def values(i, j):
                pool.tensor_copy(M.v_ring[:, j].rearrange("p t h w -> p (t h w)"), entry(K.v_sb, i)
                                 ).then_inc(M.v_ready, 1)

            def cut(view):
                pool.affine_select(out=view, in_=view, pattern=[[0, SH], [1, P]], compare_op=ALU.is_ge,
                                   fill=0.0, base=0, channel_multiplier=-1).then_inc(M.cut_done, 1)

            def mix(i, j):
                pool.wait_ge(M.recip_ready, i + 1)
                pv = M.sums_pv[:, j % 2].rearrange("p t (h two) w -> p t h two w", two=2)
                for n, o in enumerate((M.first, M.second)):
                    pool.tensor_tensor(o[:, :, :, :], pv[:, :, :, n, 0:VD],
                                       M.recip[:, j % 2, :, :, n].unsqueeze(3).to_broadcast([P, TB, 2, VD]),
                                       ALU.mult).then_inc(M.parts_ready, 1)
                pool.wait_ge(M.parts_ready, 2 * i + 2)
                pool.tensor_tensor(entry(K.attn, i), M.first[:, :, :, :].rearrange("p t h d -> p (t h d)"),
                                   M.second[:, :, :, :].rearrange("p t h d -> p (t h d)"), ALU.add
                                   ).then_inc(M.mixed, 1)

            def step(i, j, first=False, last=False):
                if not (last and j == RING - 1):
                    values(i + 1, (j + 1) % RING)
                if not first:
                    mix(i - 1, (j - 1) % RING)
                pool.wait_ge(M.exp_done, CHUNKS * i + 2 + 2)
                stand(pool, M.passed)
                cut(M.probs[:, 0:2].rearrange("p u n q -> p (u n) q")[:, :, 0:P])
                pool.wait_ge(M.exp_done, CHUNKS * i + 4 + 2)
                stand(pool, M.passed)
                tiles = M.probs[:, 2:4].rearrange("p u n q -> p (u n) q")
                cut(tiles[:, :, 0:P])
                cut(tiles[:, :, T - P:T])
                pool.wait_ge(M.exp_done, CHUNKS * i + 5 + 2)
                stand(pool, M.passed)
                halves = M.probs[:, 4].rearrange("p n (a q) -> p (n a) q", a=2)
                cut(halves[:, :, 0:P])

            values(0, 0)
            for j in range(RING):
                step(j, j, first=j == 0)
            with pool.Fori(1, ROUNDS - 1) as r:
                for j in range(RING):
                    step(r * RING + j, j)
            for j in range(RING):
                step(STEPS - RING + j, j, last=True)
            mix(STEPS - 1, RING - 1)

        @block.scalar
        def _(act):
            act.sem_inc(M.exp_done, 2)
            act.sem_inc(M.pv_copied, 1)
            act.sem_inc(M.out_turned, 1)
            act.sem_inc(M.pv_stage, 3)

            def exp(i, u, parity):
                act.wait_ge(M.s_filled, CHUNKS * i + u + 1)
                act.wait_ge(M.pv_stage, 3 * i + u // 2 + 1)
                act.activation(M.probs[:, u], M.ps_s[:, parity], ACT.Exp).then_inc(M.exp_done, 1)

            def copy_max(i, j):
                act.wait_ge(M.m_turned, i + 1)
                act.copy(M.m_rows[:, j, :], M.ps_turn[0][0:2 * SH, :]).then_inc(M.m_copied, 1)

            def copy_pv(i):
                act.wait_ge(M.pv_stage, 3 * i + 3 + 3)
                act.wait_ge(M.out_turned, i + 1)
                act.copy(M.pv_copy[:, :], M.ps_pv[0][:, :]).then_inc(M.pv_copied, 1)

            def step(i, j, first=False, last=False):
                exp(i, 0, (CHUNKS * j) % 2)
                if not (last and j == RING - 1):
                    copy_max(i + 1, (j + 1) % RING)
                exp(i, 1, (CHUNKS * j + 1) % 2)
                if not first:
                    copy_pv(i - 1)
                for u in range(2, CHUNKS):
                    exp(i, u, (CHUNKS * j + u) % 2)

            copy_max(0, 0)
            for j in range(RING):
                step(j, j, first=j == 0)
            with act.Fori(1, ROUNDS - 1) as r:
                for j in range(RING):
                    step(r * RING + j, j)
            for j in range(RING):
                step(STEPS - RING + j, j, last=True)
            copy_pv(STEPS - 1)

        @block.vector
        def _(dve):
            dve.sem_inc(M.max_read, 2)
            dve.sem_inc(M.acc_stored, 2)
            dve.sem_inc(M.mixed, 2)

            def reduce(i, j, f):
                tile, heads = FILLS[f]
                dve.wait_ge(M.max_filled, NF * i + f + 1)
                dve.tensor_reduce(M.neg_max[:, tile, heads[0]:heads[-1] + 1],
                                  M.ps_m[(NF * j + f) % 2][:, 0:len(heads) * (tile + 1) * P]
                                  .rearrange("p (s k) -> p s k", s=len(heads)),
                                  AX.X, ALU.max, negate=True).then_inc(M.max_read, 1)

            def halves(i, first=False):
                dve.wait_ge(M.max_read, NF * i + NF + 2)
                if not first:
                    dve.wait_ge(M.m_turned, i)
                dve.tensor_copy(M.neg_max2[:, :, 0, :], M.neg_max[:, :, :]).then_inc(M.max_step, 1)
                dve.wait_ge(M.max_step, i + 1)
                dve.tensor_tensor(M.neg_max2[:, :, 1, :], M.neg_max[:, :, :],
                                  M.neg_max2[:, :, 0, :].bitcast(F32), ALU.subtract
                                  ).then_inc(M.max_halves, 1)

            def store(i, j):
                dve.wait_ge(M.out_turned, i + 2)
                dve.wait_ge(M.mixed, i + 1)
                dve.tensor_copy(
                    M.sums_pv[:, j % 2],
                    M.ps_turn[0][:, :].rearrange("p (t s w) -> p t s w", t=TB, s=SH)[:, :, :, 0:VW]
                ).then_inc(M.acc_stored, 1)
                dve.wait_ge(M.acc_stored, i + 3)
                r = M.recip[:, j % 2]
                dve.reciprocal(r.rearrange("p t h two -> p t (h two)"), M.sums_pv[:, j % 2, :, :, VD]
                               ).then_inc(M.recip_step, 1)
                dve.wait_ge(M.recip_step, i + 1)
                odd = r.rearrange("p t h two -> p (t h) two")[:, :, 1]
                dve.tensor_scalar(odd, odd, K.neg_lam[:, 0:1], None, ALU.mult).then_inc(M.recip_ready, 1)

            def step(i, j, first=False, last=False):
                ahead = not (last and j >= RING - 2)
                for f in range(NF):
                    if ahead:
                        reduce(i + 2, (j + 2) % RING, f)
                    if f == 1 and not first:
                        store(i - 1, (j - 1) % RING)
                if ahead:
                    halves(i + 2)

            for i in range(2):
                for f in range(NF):
                    reduce(i, i, f)
                halves(i, first=i == 0)
            for j in range(RING):
                step(j, j, first=j == 0)
            with dve.Fori(1, ROUNDS - 1) as r:
                for j in range(RING):
                    step(r * RING + j, j)
            for j in range(RING):
                step(STEPS - RING + j, j, last=True)
            store(STEPS - 1, RING - 1)

        @block.tensor
        def _(pe):
            pe.wait_ge(M.masks_set, 5)
            rounds = [0]
            pe.matmul(M.ps_pv[0][:, :], M.ident_b[:, :], M.zeros_b[:, :], start=True, stop=True
                      ).then_inc(M.pv_zeroed, 1)

            def scores(i, j, u):
                parity = (CHUNKS * j + u) % 2
                if u == 0:
                    pe.wait_ge(m_loaded[j], 16 * SH * (rounds[0] + 1))
                pe.wait_ge(M.exp_done, CHUNKS * i + u + 1)
                for n, s, kb, col in chunk(u):
                    q0 = kb * P
                    ins = pe.matmul(M.ps_s[:, parity, n, col:col + T - q0],
                                    M.k_ring[:, j, q0:q0 + P], M.q_ring[:, j, s, q0:T],
                                    start=True, stop=True)
                ins.then_inc(M.s_filled, 1)

            def maxima(i, j, f):
                tile, heads = FILLS[f]
                ps = M.ps_m[(NF * j + f) % 2]
                n_k = (tile + 1) * P
                pe.wait_ge(M.max_read, NF * i + f + 1)
                for n, s in enumerate(heads):
                    pe.matmul(ps[:, n * n_k:(n + 1) * n_k],
                              M.q_ring[0:3 * ROWS, j, s, tile * P:(tile + 1) * P],
                              M.k_ring[0:3 * ROWS, j, 0:n_k], start=n == 0, stop=False)
                diagonal = ps[:, 0:len(heads) * n_k].rearrange("p (s k) -> p s k", s=len(heads))
                pe.matmul(diagonal[:, :, n_k - P:n_k], M.ident_b[:, :], M.mask_b[:, 0:len(heads), :],
                          start=False, stop=True).then_inc(M.max_filled, 1)

            def turn_max(i):
                pe.wait_ge(M.max_halves, i + 1)
                for t in range(TB):
                    ins = pe.transpose(M.ps_turn[0][0:2 * SH, t * P:(t + 1) * P],
                                       M.neg_max2[:, t].bitcast(F32).rearrange("p h s -> p (h s)"),
                                       K.ident[:, :])
                ins.then_inc(M.m_turned, 1)

            def pv(i, j, stage):
                pe.wait_ge(M.cut_done, 4 * i + (1, 3, 4)[stage])
                if stage == 0:
                    pe.wait_ge(M.v_ready, i + 1)
                    pe.wait_ge(M.pv_copied, i + 1)
                for kb in ((0,), (1, 3), (2,))[stage]:
                    for s in range(SH):
                        u = {0: s // 2, 1: 2 + s // 2, 2: 4, 3: 2 + s // 2}[kb]
                        n, _, _, col = [c for c in chunk(u) if c[1] == s and c[2] == kb][0]
                        ins = pe.matmul(M.ps_pv[0][32 * s:32 * s + VW, kb * P:T],
                                        M.v_ring[:, j, kb, s // 2, :],
                                        M.probs[:, u, n, col:col + T - kb * P],
                                        start=kb == 0, stop=kb == 2)
                ins.then_inc(M.pv_stage, 1)

            def turn_out(i):
                pe.wait_ge(M.pv_copied, i + 2)
                for t in range(TB):
                    ins = pe.transpose(M.ps_turn[0][:, t * P:(t + 1) * P],
                                       M.pv_copy[:, t * P:(t + 1) * P], K.ident[:, :])
                ins.then_inc(M.out_turned, 1)

            def step(i, j, first=False, last=False):
                ahead = not (last and j >= RING - 2)
                if ahead:
                    pe.wait_ge(kq_loaded[(j + 2) % RING], 16 * KQ_DMAS * (rounds[0] + (j + 2) // RING + 1))

                def more(*fills):
                    if ahead:
                        for f in fills:
                            maxima(i + 2, (j + 2) % RING, f)
                scores(i, j, 0)
                if not (last and j == RING - 1):
                    pe.wait_ge(M.m_copied, i + 1)
                    pe.wait_ge(M.acc_stored, i + 1)
                    turn_max(i + 1)
                more(0)
                scores(i, j, 1)
                if not first:
                    pv(i - 1, (j - 1) % RING, 2)
                more(1, 2)
                if not first:
                    if not (last and j == RING - 1):
                        pe.wait_ge(M.m_copied, i + 2)
                    pe.wait_ge(M.acc_stored, i + 1)
                    turn_out(i - 1)
                scores(i, j, 2)
                more(3, 4)
                scores(i, j, 3)
                more(5, 6)
                scores(i, j, 4)
                pv(i, j, 0)
                more(7, 8)
                pv(i, j, 1)
                more(9, 10)

            for i in range(2):
                pe.wait_ge(kq_loaded[i], 16 * KQ_DMAS)
                for f in range(NF):
                    maxima(i, i, f)
                if i == 0:
                    turn_max(0)
            for j in range(RING):
                step(j, j, first=j == 0)
            with pe.Fori(1, ROUNDS - 1) as r:
                rounds[0] = r
                for j in range(RING):
                    step(r * RING + j, j)
            rounds[0] = ROUNDS - 1
            for j in range(RING):
                step(STEPS - RING + j, j, last=True)
            pv(STEPS - 1, RING - 1, 2)
            pe.wait_ge(M.acc_stored, STEPS - 1 + 2)
            turn_out(STEPS - 1)


def experts(nc, D, K, S):
    B, T, E, TB, KC, G, VD, NE, NX, NS = D.B, D.T, D.E, D.TB, D.KC, D.G, D.VD, D.NE, D.NX, D.NS
    H = G * 2 * TB
    GS = NE // GROUPS
    made = {}
    with ExitStack() as st:
        tensor, banks, sems = allocator(nc, st, made, "experts_")
        tensor("up_h", [P, NX, KC, P], F32R)
        tensor("up_l", [P, NX, KC, P], F32R)
        tensor("down_h", [P, NX, E], F32R)
        tensor("down_l", [P, NX, E], F32R)
        tensor("stage", [P, 2, 4 * E])
        tensor("square", [P, H, VD])
        tensor("mean_sq", [P, H])
        tensor("head_std", [P, H])
        tensor("head_rstd", [P, H])
        tensor("normed", [P, TB, E])
        tensor("aT_h", [P, KC, T], F32R)
        tensor("aT_l", [P, KC, T], F32R)
        tensor("stats", [P, TB, 6])
        tensor("mv", [P, TB, 2])
        tensor("std", [P, TB])
        tensor("rstd", [P, TB])
        tensor("xT_h", [P, KC, 2 * T], F32R)
        tensor("xT_l", [P, KC, 2 * T], F32R)
        tensor("rw_raw", [NE, E])
        tensor("rw_h", [P, KC, P], F32R)
        tensor("rw_l", [P, KC, P], F32R)
        tensor("logitsT", [NE, T])
        tensor("combT", [NE, T])
        tensor("score", [P, TB, NE])
        tensor("biased", [P, TB, NE])
        tensor("bias", [P, NE])
        tensor("pair_sums", [P, TB * GROUPS, 6])
        tensor("group_score", [P, TB, GROUPS])
        tensor("group_mask", [P, TB, GROUPS])
        tensor("top_val", [P, TB])
        tensor("top_key", [P, TB, NE])
        tensor("first_hot", [P, TB, NE])
        tensor("second_hot", [P, TB, NE])
        tensor("order", [P, NE])
        tensor("comb", [P, TB, NE])
        tensor("relu", [P, 2, T])
        tensor("act", [P, 2, T])
        tensor("act_h", [P, 2, T], F32R)
        tensor("act_l", [P, 2, T], F32R)
        tensor("weight", [P, 4, T])
        tensor("outT", [P, KC, T])
        tensor("y", [P, 2, 2, E])
        banks("ps_h", 2)
        banks("ps_o", KC)
        banks("ps_t", 2)
        banks("ps_x", 2)
        weight_loaded = [st.enter_context(nc.semaphore(f"weight_loaded{j}")) for j in range(4)]
        stage_loaded = [st.enter_context(nc.semaphore(f"stage_loaded{j}")) for j in range(2)]
        sems("passed router_loaded split_done order_set rw_turned rw_high rw_low rw_zeroed "
             "squared mean_ready head_std_ready dve_step heads_normed heads_turned aTh_ready aTl_ready "
             "projected var_ready std_ready rows_normed rows_turned xTh_ready xTl_ready "
             "logits_done logits_copied logits_turned scored comb_ready comb_turned comb_copied comb_stored "
             "up_done relu_done weighted act_done high_done low_done down_done out_copied out_turned y_ready y_stored")
        M = named(made)

        CHUNKS = []
        for n0 in range(0, NX, 4):
            for up in (True, False):
                CHUNKS.append((up, n0))
        READY = {}
        for k, (up, n0) in enumerate(CHUNKS):
            for n in range(n0, n0 + 4):
                READY[up, n] = 2 * k + 2

        def half(b):
            return (b % 2) * T

        def later(what, b, n, last):
            if n < NX:
                what(b, n)
            elif not last:
                what(b + 1, n - NX)

        block = st.enter_context(nc.Block())

        @block.sync
        def _(sp):
            sp.dma_start(M.rw_raw[:, :], S.router_w).then_inc(M.router_loaded, 16)
            sp.dma_start(M.bias[:, :], S.e_bias.partition_broadcast(P)).then_inc(M.router_loaded, 16)
            for k, (up, n0) in enumerate(CHUNKS):
                if k >= 2:
                    sp.wait_ge(M.split_done, 2 * (k - 1))
                slot = M.stage[:, k % 2, :]
                if up:
                    to = slot.rearrange("p (n c i) -> p n c i", n=4, c=KC)
                    for n in range(4):
                        src = (S.shared_up[:, n * P:(n + 1) * P] if n0 < NS else S.w_up[n0 - NS + n])
                        sp.dma_start(to[:, n], src.rearrange("(c p) i -> p c i", p=P)
                                     ).then_inc(stage_loaded[k % 2], 16)
                else:
                    to = slot.rearrange("p (n e) -> p n e", n=4)
                    for n in range(4):
                        src = S.shared_down[n * P:(n + 1) * P, :] if n0 < NS else S.w_down[n0 - NS + n]
                        sp.dma_start(to[:, n], src).then_inc(stage_loaded[k % 2], 16)

            def store_comb(b):
                sp.wait_ge(M.comb_copied, b + 2)
                sp.dma_start(S.comb[:, bass.ds(b * T, T)], M.combT[:, :]).then_inc(M.comb_stored, 16)
                sp.wait_ge(M.comb_stored, 16 * b + 32)
                stand(sp, M.passed)

            def load_weight(b, e):
                sp.wait_ge(M.weighted, NE * b + e + 1)
                sp.dma_start(M.weight[:, e % 4, :],
                             S.comb[e:e + 1, bass.ds(b * T, T)].rearrange("o t -> (o t)").partition_broadcast(P)
                             ).then_inc(weight_loaded[e % 4], 16)

            def store_out(b, pair):
                sp.wait_ge(M.y_ready, 2 * b + pair + 1 + 4)
                sp.dma_start(S.out.rearrange("b (t p) e -> p (b t) e", p=P)[:, bass.ds(b * TB + 2 * pair, 2), :],
                             M.y[:, pair]).then_inc(M.y_stored, 16)

            store_comb(0)

            def batch(b, first=False, last=False):
                for e in range(NE):
                    load_weight(b, e)
                    if e == 4 and not first:
                        store_out(b - 1, 0)
                        store_out(b - 1, 1)
                if not last:
                    store_comb(b + 1)

            batch(0, first=True)
            with sp.Fori(1, B - 1) as b:
                batch(b)
            batch(B - 1, last=True)
            store_out(B - 1, 0)
            store_out(B - 1, 1)
            sp.wait_ge(M.y_stored, 16 * 2 * B + 16)

        @block.gpsimd
        def _(pool):
            pool.sem_inc(M.weighted, 4)
            pool.sem_inc(M.y_stored, 16)
            pool.sem_inc(M.y_ready, 4)
            pool.sem_inc(M.comb_copied, 1)
            pool.sem_inc(M.comb_turned, 1)
            pool.sem_inc(M.comb_stored, 16)
            pool.sem_inc(M.rows_turned, 1)
            pool.sem_inc(M.relu_done, 2)
            pool.sem_inc(M.out_copied, KC)

            def square(b):
                heads = entries(K.attn, b * G, G).rearrange("p g (x d) -> p (g x) d", d=VD)
                pool.tensor_tensor(M.square[:, :, :], heads, heads, ALU.mult).then_inc(M.squared, 1)

            def weigh(b, n):
                e = n - NS
                k = NX * b + n
                pool.wait_ge(M.relu_done, k + 1 + 2)
                pool.wait_ge(weight_loaded[e % 4], 16 * ((NE // 4) * b + e // 4 + 1))
                pool.wait_ge(M.low_done, k + 1)
                pool.tensor_tensor(M.act[:, n % 2, :], M.relu[:, n % 2, :], M.weight[:, e % 4, :],
                                   ALU.mult).then_inc(M.weighted, 1)

            square(0)
            pool.memset(M.rw_h[:, :, :].bitcast(F32), 0.0).then_inc(M.rw_zeroed, 1)
            pool.memset(M.rw_l[:, :, :].bitcast(F32), 0.0).then_inc(M.rw_zeroed, 1)
            for e in range(NE):
                pool.memset(M.order[:, e:e + 1], float(NE - e)).then_inc(M.order_set, 1)
            for k, (up, n0) in enumerate(CHUNKS):
                pool.wait_ge(stage_loaded[k % 2], 64 * (k // 2 + 1))
                high, low = (M.up_h, M.up_l) if up else (M.down_h, M.down_l)
                o = [(w[:, n0:n0 + 4].rearrange("p n c i -> p (n c i)") if up else
                      w[:, n0:n0 + 4].rearrange("p n e -> p (n e)")) for w in (high, low)]
                pool.tensor_copy(o[0], M.stage[:, k % 2, :]).then_inc(M.split_done, 1)
                pool.wait_ge(M.split_done, 2 * k + 1)
                pool.tensor_tensor(o[1], M.stage[:, k % 2, :], o[0].bitcast(F32), ALU.subtract
                                   ).then_inc(M.split_done, 1)

            def batch(b, last=False):
                for n in range(NX):
                    if n >= NS:
                        weigh(b, n)
                    if n == 5 and not last:
                        square(b + 1)

            with pool.Fori(0, B - 1) as b:
                batch(b)
            batch(B - 1, last=True)

        @block.scalar
        def _(act):
            act.sem_inc(M.low_done, 2)
            act.sem_inc(M.down_done, 2)
            act.sem_inc(M.act_done, 2)
            act.sem_inc(M.out_turned, 2)

            def head_spread(b):
                act.wait_ge(M.mean_ready, b + 1)
                act.activation(M.head_std[:, :], M.mean_sq[:, :], ACT.Sqrt, bias=K.eps_col[:, 0:1],
                               scale=1.0 / VD).then_inc(M.head_std_ready, 1)

            def heads_high(b):
                act.wait_ge(M.heads_turned, b + 1)
                for c in range(KC):
                    act.copy(M.aT_h[:, c, :], M.ps_t[c][:, :]).then_inc(M.aTh_ready, 1)

            def spread(b):
                act.wait_ge(M.var_ready, b + 1)
                act.activation(M.std[:, :], M.mv[:, :, 1], ACT.Sqrt, bias=K.eps_col[:, 0:1]
                               ).then_inc(M.std_ready, 1)

            def rows_high(b):
                act.wait_ge(M.rows_turned, b + 2)
                for c in range(KC):
                    act.copy(M.xT_h[:, c, bass.ds(half(b), T)], M.ps_t[c][:, :]).then_inc(M.xTh_ready, 1)

            def copy_logits(b):
                act.wait_ge(M.logits_done, b + 1)
                act.copy(M.logitsT[:, :], M.ps_x[0][0:NE, :]).then_inc(M.logits_copied, 1)

            def score(b):
                act.wait_ge(M.logits_turned, b + 1)
                act.activation(M.score[:, :, :].rearrange("p t e -> p (t e)"),
                               M.ps_x[1][:, 0:TB * NE], ACT.Sigmoid).then_inc(M.scored, 1)

            def copy_comb(b):
                act.wait_ge(M.comb_turned, b + 2)
                act.wait_ge(M.comb_stored, 16 * b + 16)
                act.copy(M.combT[:, :], M.ps_x[0][0:NE, :]).then_inc(M.comb_copied, 1)

            def relu(b, n):
                k = NX * b + n
                act.wait_ge(M.up_done, k + 1)
                act.wait_ge(M.act_done, k + 1)
                act.activation(M.relu[:, n % 2, :], M.ps_h[n % 2][:, :], ACT.Relu).then_inc(M.relu_done, 1)

            def high(b, n):
                k = NX * b + n
                act.wait_ge(M.act_done, k + 1 + 2)
                act.wait_ge(M.down_done, k + 1)
                act.copy(M.act_h[:, n % 2, :], M.act[:, n % 2, :]).then_inc(M.high_done, 1)

            def copy_out(b):
                act.wait_ge(M.down_done, NX * b + NX + 2)
                act.wait_ge(M.out_turned, 2 * b + 2)
                for c in range(KC):
                    act.copy(M.outT[:, c, :], M.ps_o[c][:, :]).then_inc(M.out_copied, 1)

            act.wait_ge(M.rw_turned, 1)
            act.wait_ge(M.rw_zeroed, 2)
            act.copy(M.rw_h[:, :, 0:NE], M.ps_x[0][:, 0:KC * NE].rearrange("p (c e) -> p c e", c=KC)
                     ).then_inc(M.rw_high, 1)
            head_spread(0)
            heads_high(0)
            spread(0)
            rows_high(0)
            copy_logits(0)
            score(0)
            copy_comb(0)
            relu(0, 0)
            relu(0, 1)
            high(0, 0)

            def batch(b, last=False):
                for n in range(NX):
                    later(relu, b, n + 2, last)
                    later(high, b, n + 1, last)
                    if not last:
                        if n == 6:
                            head_spread(b + 1)
                        if n == 8:
                            heads_high(b + 1)
                        if n == 11:
                            spread(b + 1)
                        if n == 12:
                            rows_high(b + 1)
                        if n == 13:
                            copy_logits(b + 1)
                        if n == 14:
                            score(b + 1)
                        if n == 16:
                            copy_comb(b + 1)
                copy_out(b)

            with act.Fori(0, B - 1) as b:
                batch(b)
            batch(B - 1, last=True)

        @block.vector
        def _(dve):
            ROUTER_STEPS = 35
            STEPS = 4 + 2 * TB + ROUTER_STEPS

            def mean_square(b):
                dve.wait_ge(M.squared, b + 1)
                dve.tensor_reduce(M.mean_sq[:, :], M.square[:, :, :], AX.X, ALU.add).then_inc(M.mean_ready, 1)

            def norm_heads(b):
                link = chained(dve, M.dve_step, STEPS * b)
                dve.wait_ge(M.head_std_ready, b + 1)
                link(dve.reciprocal(M.head_rstd[:, :], M.head_std[:, :]))
                link(dve.tensor_scalar(M.head_rstd[:, :], M.head_rstd[:, :], 1.0 - LAMBDA_INIT, None, ALU.mult))
                dve.wait_ge(M.rows_turned, b + 1)
                heads = entries(K.attn, b * G, G).rearrange("p g (t h d) -> p g t h d", t=TB, d=VD)
                scale = M.head_rstd[:, :].rearrange("p (g t h) -> p g t h", t=TB, h=2)
                for t in range(TB):
                    dve.tensor_tensor(M.normed[:, t, :].rearrange("p (g h d) -> p g h d", g=G, d=VD),
                                      heads[:, :, t], scale[:, :, t].unsqueeze(3).to_broadcast([P, G, 2, VD]),
                                      ALU.mult).then_inc(M.heads_normed, 1)

            def heads_low(b):
                for c in range(KC):
                    dve.wait_ge(M.aTh_ready, KC * b + c + 1)
                    dve.tensor_tensor(M.aT_l[:, c, :], M.ps_t[c][:, :], M.aT_h[:, c, :].bitcast(F32),
                                      ALU.subtract).then_inc(M.aTl_ready, 1)

            def add_rows(b):
                base = STEPS * b + 2
                dve.wait_ge(M.projected, b + 1)
                for pair in range(2):
                    rows = entries(K.x_sb, b * TB + 2 * pair, 2).rearrange("p t e -> p (t e)")
                    dve.tensor_tensor(rows, rows, M.ps_x[pair][:, :], ALU.add).then_inc(M.dve_step, 1)
                dve.wait_ge(M.dve_step, base + 2)
                stand(dve, M.passed)
                for t in range(TB):
                    dve.bn_stats(M.stats[:, t, :], entry(K.x_sb, b * TB + t)).then_inc(M.dve_step, 1)
                dve.wait_ge(M.dve_step, base + 2 + TB)
                stand(dve, M.passed)
                for t in range(TB):
                    dve.bn_aggr(M.mv[:, t, :], M.stats[:, t, :]).then_inc(
                        M.var_ready if t == TB - 1 else M.dve_step, 1)

            def norm_rows(b):
                dve.wait_ge(M.std_ready, b + 1)
                dve.reciprocal(M.rstd[:, :], M.std[:, :]).then_inc(M.dve_step, 1)
                dve.wait_ge(M.dve_step, STEPS * b + 4 + 2 * TB)
                dve.wait_ge(M.heads_turned, b + 1)
                for t in range(TB):
                    dve.tensor_scalar(M.normed[:, t, :], entry(K.x_sb, b * TB + t), M.mv[:, t, 0:1],
                                      M.rstd[:, t:t + 1], ALU.subtract, ALU.mult).then_inc(M.rows_normed, 1)

            def rows_low(b):
                for c in range(KC):
                    dve.wait_ge(M.xTh_ready, KC * b + c + 1)
                    at = bass.ds(half(b), T)
                    dve.tensor_tensor(M.xT_l[:, c, at], M.ps_t[c][:, :], M.xT_h[:, c, at].bitcast(F32),
                                      ALU.subtract).then_inc(M.xTl_ready, 1)

            def over(x, n):
                return x[:, :].unsqueeze(2).to_broadcast([P, TB, n])

            def top(link, vals, n, hot):
                key = M.top_key[:, :, 0:n]
                link(dve.tensor_reduce(M.top_val[:, :], vals, AX.X, ALU.max))
                link(dve.tensor_tensor(key, vals, over(M.top_val, n), ALU.is_equal))
                link(dve.tensor_tensor(key, key, M.order[:, 0:n].unsqueeze(1).to_broadcast([P, TB, n]), ALU.mult))
                link(dve.tensor_reduce(M.top_val[:, :], key, AX.X, ALU.max))
                link(dve.tensor_tensor(hot, key, over(M.top_val, n), ALU.is_equal))

            def top2(link, vals, n, hots):
                first, second = (h[:, :, 0:n] for h in hots)
                top(link, vals, n, first)
                link(dve.scalar_tensor_tensor(vals, first, FAR, vals, ALU.mult, ALU.add))
                top(link, vals, n, second)
                link(dve.tensor_tensor(first, first, second, ALU.add))

            def route(b, part):
                done = [0, 6, 19][part]
                link = chained(dve, M.dve_step, STEPS * b + 4 + 2 * TB + done)
                hots = (M.first_hot, M.second_hot)
                if part == 0:
                    dve.wait_ge(M.scored, b + 1)
                    link(dve.tensor_tensor(M.biased[:, :, :], M.score[:, :, :],
                                           M.bias[:, :].unsqueeze(1).to_broadcast([P, TB, NE]), ALU.add))
                    s = M.biased[:, :, :].rearrange("p t (g k) -> p (t g) k", g=GROUPS)
                    for at, d in ((0, 1), (3, 2), (5, 3)):
                        link(dve.tensor_tensor(M.pair_sums[:, :, at:at + GS - d], s[:, :, 0:GS - d],
                                               s[:, :, d:GS], ALU.add))
                    link(dve.tensor_reduce(M.group_score[:, :, :].rearrange("p t g -> p (t g)"),
                                           M.pair_sums[:, :, :], AX.X, ALU.max))
                    assert link.count[0] == 5
                    link(dve.tensor_copy(M.group_mask[:, :, :], M.group_score[:, :, :]))
                elif part == 1:
                    top2(link, M.group_mask[:, :, :], GROUPS, hots)
                    link(dve.tensor_tensor(
                        M.biased[:, :, :].rearrange("p t (g k) -> p t g k", g=GROUPS),
                        M.biased[:, :, :].rearrange("p t (g k) -> p t g k", g=GROUPS),
                        M.first_hot[:, :, 0:GROUPS].unsqueeze(3).to_broadcast([P, TB, GROUPS, GS]), ALU.mult))
                    assert link.count[0] == 13
                else:
                    top2(link, M.biased[:, :, :], NE, hots)
                    chosen = M.first_hot[:, :, :]
                    link(dve.tensor_tensor(chosen, chosen, M.score[:, :, :], ALU.mult))
                    link(dve.tensor_reduce(M.top_val[:, :], chosen, AX.X, ALU.add))
                    link(dve.tensor_scalar(M.top_val[:, :], M.top_val[:, :], 1e-20, None, ALU.add))
                    dve.reciprocal(M.top_val[:, :], M.top_val[:, :]).then_inc(M.dve_step, 1)
                    dve.wait_ge(M.dve_step, STEPS * b + 4 + 2 * TB + done + 16)
                    dve.wait_ge(M.comb_turned, b + 1)
                    dve.tensor_tensor(M.comb[:, :, :], chosen, over(M.top_val, NE), ALU.mult
                                      ).then_inc(M.comb_ready, 1)

            def activate(b, n):
                k = NX * b + n
                if n < NS:
                    dve.wait_ge(M.relu_done, k + 1 + 2)
                    dve.wait_ge(M.low_done, k + 1)
                    left = M.relu[:, n % 2, :]
                else:
                    dve.wait_ge(M.weighted, NE * b + n - NS + 1 + 4)
                    left = M.act[:, n % 2, :]
                dve.tensor_tensor(M.act[:, n % 2, :], left, M.relu[:, n % 2, :], ALU.mult
                                  ).then_inc(M.act_done, 1)

            def low(b, n):
                k = NX * b + n
                dve.wait_ge(M.high_done, k + 1 + 2)
                dve.wait_ge(M.down_done, k + 1)
                dve.tensor_tensor(M.act_l[:, n % 2, :], M.act[:, n % 2, :], M.act_h[:, n % 2, :].bitcast(F32),
                                  ALU.subtract).then_inc(M.low_done, 1)

            def add_out(b, pair):
                dve.wait_ge(M.out_turned, 2 * b + pair + 1 + 2)
                dve.wait_ge(M.y_stored, 32 * b + 16)
                rows = entries(K.x_sb, b * TB + 2 * pair, 2)
                dve.tensor_tensor(M.y[:, pair].rearrange("p t e -> p (t e)"),
                                  rows.rearrange("p t e -> p (t e)"), M.ps_t[pair][:, :], ALU.add
                                  ).then_inc(M.y_ready, 1)

            dve.sem_inc(M.high_done, 2)
            dve.wait_ge(M.rw_high, 1)
            dve.tensor_tensor(M.rw_l[:, :, 0:NE], M.ps_x[0][:, 0:KC * NE].rearrange("p (c e) -> p c e", c=KC),
                              M.rw_h[:, :, 0:NE].bitcast(F32), ALU.subtract).then_inc(M.rw_low, 1)
            mean_square(0)
            norm_heads(0)
            heads_low(0)
            add_rows(0)
            norm_rows(0)
            rows_low(0)
            dve.wait_ge(M.order_set, NE)
            dve.wait_ge(M.router_loaded, 32)
            for part in range(3):
                route(0, part)
            activate(0, 0)
            activate(0, 1)
            low(0, 0)

            def batch(b, first=False, last=False):
                for n in range(NX):
                    later(low, b, n + 1, last)
                    later(activate, b, n + 2, last)
                    if n == 1 and not first:
                        add_out(b - 1, 0)
                        add_out(b - 1, 1)
                    if not last:
                        if n == 6:
                            mean_square(b + 1)
                        if n == 7:
                            norm_heads(b + 1)
                        if n == 8:
                            heads_low(b + 1)
                        if n == 10:
                            add_rows(b + 1)
                        if n == 11:
                            norm_rows(b + 1)
                        if n == 12:
                            rows_low(b + 1)
                        if n in (14, 15, 16):
                            route(b + 1, n - 14)

            batch(0, first=True)
            with dve.Fori(1, B - 1) as b:
                batch(b)
            batch(B - 1, last=True)
            add_out(B - 1, 0)
            add_out(B - 1, 1)

        @block.tensor
        def _(pe):
            def turn_heads(b):
                pe.wait_ge(M.heads_normed, TB * b + TB)
                pe.wait_ge(M.y_ready, 2 * b + 2)
                turn(M.heads_turned)

            def turn_rows(b):
                pe.wait_ge(M.rows_normed, TB * b + TB)
                turn(M.rows_turned)

            def turn(semaphore):
                for c in range(KC):
                    for t in range(TB):
                        ins = pe.transpose(M.ps_t[c][:, t * P:(t + 1) * P],
                                           M.normed[:, t, c * P:(c + 1) * P], K.ident[:, :])
                ins.then_inc(semaphore, 1)

            def project_heads(b):
                pe.wait_ge(M.aTl_ready, KC * b + KC)
                pe.wait_ge(M.comb_copied, b + 1)
                for t in range(TB):
                    for c in range(KC):
                        ins = matmul3(pe, M.ps_x[t // 2][:, (t % 2) * E:(t % 2 + 1) * E],
                                      [x[:, c, t * P:(t + 1) * P] for x in (M.aT_h, M.aT_l)],
                                      [w[:, c, :] for w in (K.wo_h, K.wo_l)],
                                      start=c == 0, stop=c == KC - 1)
                ins.then_inc(M.projected, 1)

            def logits(b):
                pe.wait_ge(M.xTl_ready, KC * b + KC)
                pe.wait_ge(M.var_ready, b + 1)
                for c in range(KC):
                    ins = matmul3(pe, M.ps_x[0][:, :], [w[:, c, :] for w in (M.rw_h, M.rw_l)],
                                  [x[:, c, bass.ds(half(b), T)] for x in (M.xT_h, M.xT_l)],
                                  start=c == 0, stop=c == KC - 1)
                ins.then_inc(M.logits_done, 1)

            def turn_logits(b):
                pe.wait_ge(M.logits_copied, b + 1)
                stand(pe, M.passed)
                for t in range(TB):
                    ins = pe.transpose(M.ps_x[1][:, t * NE:(t + 1) * NE],
                                       M.logitsT[:, t * P:(t + 1) * P], K.ident[0:NE, 0:NE])
                ins.then_inc(M.logits_turned, 1)

            def turn_comb(b):
                pe.wait_ge(M.comb_ready, b + 1)
                for t in range(TB):
                    ins = pe.transpose(M.ps_x[0][0:NE, t * P:(t + 1) * P], M.comb[:, t, :], K.ident[:, :])
                ins.then_inc(M.comb_turned, 1)

            def up(b, n):
                if n % 4 == 0:
                    pe.wait_ge(M.split_done, READY[True, n])
                pe.wait_ge(M.relu_done, NX * b + n + 1)
                for c in range(KC):
                    ins = matmul3(pe, M.ps_h[n % 2][:, :], [w[:, n, c, :] for w in (M.up_h, M.up_l)],
                                  [x[:, c, bass.ds(half(b), T)] for x in (M.xT_h, M.xT_l)],
                                  start=c == 0, stop=c == KC - 1)
                ins.then_inc(M.up_done, 1)

            def down(b, n):
                if n % 4 == 0:
                    pe.wait_ge(M.split_done, READY[False, n])
                if n == 0:
                    pe.wait_ge(M.out_copied, KC * b + KC)
                pe.wait_ge(M.low_done, NX * b + n + 1 + 2)
                for c in range(KC):
                    ins = matmul3(pe, M.ps_o[c][:, :],
                                  [w[:, n, c * P:(c + 1) * P] for w in (M.down_h, M.down_l)],
                                  [a[:, n % 2, :] for a in (M.act_h, M.act_l)],
                                  start=n == 0, stop=n == NX - 1)
                ins.then_inc(M.down_done, 1)

            def turn_out(b, pair):
                pe.wait_ge(M.out_copied, KC * b + 2 * KC)
                for t in range(2):
                    for c in range(KC):
                        ins = pe.transpose(M.ps_t[pair][:, t * E + c * P:t * E + (c + 1) * P],
                                           M.outT[:, c, (2 * pair + t) * P:(2 * pair + t + 1) * P],
                                           K.ident[:, :])
                ins.then_inc(M.out_turned, 1)

            pe.wait_ge(M.router_loaded, 32)
            for c in range(KC):
                ins = pe.transpose(M.ps_x[0][:, c * NE:(c + 1) * NE], M.rw_raw[:, c * P:(c + 1) * P],
                                   K.ident[0:NE, 0:NE])
            ins.then_inc(M.rw_turned, 1)
            turn_heads(0)
            pe.wait_ge(M.rw_low, 1)
            project_heads(0)
            turn_rows(0)
            logits(0)
            turn_logits(0)
            up(0, 0)
            up(0, 1)
            turn_comb(0)

            def batch(b, first=False, last=False):
                for n in range(NX):
                    later(up, b, n + 2, last)
                    if not first and n < 2:
                        turn_out(b - 1, n)
                    if not last:
                        if n == 7:
                            turn_heads(b + 1)
                        if n == 9:
                            project_heads(b + 1)
                        if n == 12:
                            turn_rows(b + 1)
                        if n == 13:
                            logits(b + 1)
                        if n == 14:
                            turn_logits(b + 1)
                        if n == 17:
                            turn_comb(b + 1)
                    down(b, n)

            batch(0, first=True)
            with pe.Fori(1, B - 1) as b:
                batch(b)
            batch(B - 1, last=True)
            turn_out(B - 1, 0)
            turn_out(B - 1, 1)


def layer_kernel(nc, x, wq, wk, wv, wo, lq1, lk1, lq2, lk2, router_w, e_bias, w_up, w_down,
                 shared_up, shared_down, out):
    D, S = Shapes(), Tensors()
    kept = {}
    D.B, D.T, D.E = x.shape
    D.HD = lq1.shape[0]
    D.VD = 2 * D.HD
    D.VW = D.VD + 1
    D.KC = D.E // P
    D.TB = D.T // P
    D.SH = 4
    D.ROWS = D.SH * D.HD
    D.G = D.E // D.ROWS
    D.STEPS = D.B * D.G
    D.NE = router_w.shape[0]
    D.NS = shared_up.shape[1] // P
    D.NX = D.NS + D.NE
    D.SCALE = D.HD ** -0.5
    assert D.KC == 2 and D.TB == 4 and D.ROWS == 32 and w_up.shape[2] == P and D.STEPS % 4 == 0

    S.x, S.wq, S.wk, S.wv, S.wo, S.lq1, S.lk1, S.lq2, S.lk2 = x, wq, wk, wv, wo, lq1, lk1, lq2, lk2
    S.router_w, S.e_bias, S.w_up, S.w_down = router_w, e_bias, w_up, w_down
    S.shared_up, S.shared_down, S.out = shared_up, shared_down, out
    S.qk = nc.dram_tensor("qk_halves", [4, D.STEPS, D.ROWS, D.T], F32R, kind="Internal").ap()
    S.comb = nc.dram_tensor("comb_rows", [D.NE, D.B * D.T], F32, kind="Internal").ap()

    with ExitStack() as ctx:
        tensor, _, _ = allocator(nc, ctx, kept)
        tensor("x_sb", [P, D.B * D.TB, D.E])
        tensor("attn", [P, D.STEPS, D.TB * 2 * D.VD])
        tensor("ident", [P, P])
        tensor("wo_h", [P, D.KC, D.E], F32R)
        tensor("wo_l", [P, D.KC, D.E], F32R)
        tensor("eps_col", [P, 1])
        tensor("neg_lam", [P, 1])
        with ExitStack() as attention:
            tensor, _, _ = allocator(nc, attention, kept)
            tensor("v_sb", [P, D.STEPS, D.TB * 2 * D.VW])
            K = named(kept)
            project(nc, D, K, S)
            attend(nc, D, K, S)
        experts(nc, D, K, S)


_INS = ['L0_attn_x', 'L0_attn_Wq', 'L0_attn_Wk', 'L0_attn_Wv', 'L0_attn_Wo', 'L0_attn_lq1', 'L0_attn_lk1',
        'L0_attn_lq2', 'L0_attn_lk2', 'L0_ffn_router_weight', 'L0_ffn_e_bias', 'L0_ffn_w_up',
        'L0_ffn_w_down', 'L0_ffn_shared_up', 'L0_ffn_shared_down']


def kernel(**inputs):
    import numpy as _np
    import concourse.bacc as _bacc
    from concourse import mybir as _mybir
    from concourse.bass_utils import run_bass_kernel_spmd as _run

    nc = _bacc.Bacc("TRN2", target_bir_lowering=False, num_devices=1)
    arrays, args = {}, []
    for name in _INS:
        a = _np.ascontiguousarray(inputs[name])
        arrays[f"in_{name}_dram"] = a
        args.append(nc.dram_tensor(f"in_{name}_dram", a.shape, _mybir.dt.from_np(a.dtype), kind="ExternalInput").ap())
    shape = inputs['L0_attn_x'].shape
    out = nc.dram_tensor("out_0_dram", shape, _mybir.dt.float32, kind="ExternalOutput").ap()
    layer_kernel(nc, *args, out)
    r = _run(nc, [arrays], core_ids=[0])
    return r.results[0]["out_0_dram"]
```

```python
import math
from contextlib import ExitStack
from collections import namedtuple

import concourse.bass as bass
from concourse import mybir

F32 = mybir.dt.float32
F32R = mybir.dt.float32r
BF16 = mybir.dt.bfloat16
ALU = mybir.AluOpType
ACT = mybir.ActivationFunctionType
AX = mybir.AxisListType

P = 128
LAMBDA_INIT = 0.8 - 0.6 * math.exp(-0.3 * 12)
EPS = 1e-5
GROUPS = 4
MASKED = -2.0e38
FAR = -1.0e30


class Shapes:
    pass


class Tensors:
    pass


def named(found):
    return namedtuple("Named", sorted(found))(**found)


def allocator(nc, stack, where, block=""):
    def tensor(name, shape, dt=F32):
        where[name] = stack.enter_context(nc.sbuf_tensor(block + name, list(shape), dt))

    def banks(name, n):
        where[name] = [stack.enter_context(nc.psum_tensor(f"{block}{name}{i}", [P, 512], F32))
                                for i in range(n)]

    def sems(names):
        for name in names.split():
            where[name] = stack.enter_context(nc.semaphore(block + name))
    return tensor, banks, sems


def chained(eng, semaphore, base=0):
    count = [0]

    def link(ins):
        count[0] += 1
        ins.then_inc(semaphore, 1)
        eng.wait_ge(semaphore, base + count[0])
    link.count = count
    return link


def stand(eng, passed):
    eng.sem_inc(passed, 1)


def matmul3(pe, o, w, m, start=True, stop=True):
    pe.matmul(o, w[0], m[1], start=start, stop=False)
    pe.matmul(o, w[1], m[0], start=False, stop=False)
    return pe.matmul(o, w[0], m[0], start=False, stop=stop)


def entries(buf, first, n):
    return buf[:, bass.ds(first, n), :]


def entry(buf, at):
    return entries(buf, at, 1).rearrange("p a s -> p (a s)")


def store_parts(sp, D, K, S, b):
    for m in range(D.KC):
        n = D.G // D.KC
        steps = slice(b * D.G + m * n, b * D.G + (m + 1) * n)
        for dst, at, low in ((S.q, 4 * b + m, 2), (S.k, 4 * b + D.KC + m, 1)):
            sp.dma_start(dst[steps, :, :, low].rearrange("g s r t -> (g s r) t").bitcast(F32),
                         K.part_l[:, at, :].bitcast(F32)).then_inc(K.parts_stored, 16)
            places = slice(0, 2) if low == 2 else slice(0, 3, 2)
            sp.dma_start(dst[steps, :, :, places].rearrange("g s r c t -> (g s r) c t").bitcast(F32),
                         K.part_h[:, at, :].bitcast(F32).unsqueeze(1).to_broadcast([P, 2, D.T])
                         ).then_inc(K.parts_stored, 16)
    sp.dma_start(S.v[b * D.G:(b + 1) * D.G].rearrange("g p w -> p g w"),
                 K.v_stage[:, b].rearrange("p g t h w -> p g (t h w)")).then_inc(K.parts_stored, 16)


PARTS_STORED = (4 * 2 + 1) * 16
STORED_EARLY = 2


def load_kq(sp, D, K, S, i, j):
    rows = 3 * D.HD
    sp.dma_start(K.k_ring[0:3 * D.ROWS, j, :].bitcast(F32),
                 S.k[bass.ds(i, 1)].rearrange("g s r c t -> (g s r c) t").bitcast(F32)
                 ).then_inc(K.kq_loaded[j], 16)
    for s in range(D.SH):
        sp.dma_start(K.q_ring[s * rows:(s + 1) * rows, j, s, :].bitcast(F32),
                     S.q[bass.ds(i, 1), s].rearrange("g r c t -> (g r c) t").bitcast(F32)
                     ).then_inc(K.kq_loaded[j], 16)


def load_v(sp, K, S, i, j):
    sp.dma_start(K.v_ring[:, j].rearrange("p t h w -> p (t h w)"),
                 S.v[bass.ds(i, 1)].rearrange("g p w -> (g p) w")).then_inc(K.v_loaded[j], 16)


STEP_LOADS = 1 + 4


def project(nc, D, K, S):
    B, T, E, TB, KC, G, HD, VD, VW = D.B, D.T, D.E, D.TB, D.KC, D.G, D.HD, D.VD, D.VW
    made = {}
    with ExitStack() as st:
        tensor, banks, sems = allocator(nc, st, made, "project_")
        tensor("w_raw", [P, 4, KC, E])
        tensor("w_h", [P, 3, KC, E], F32R)
        tensor("w_l", [P, 3, KC, E], F32R)
        tensor("x", [P, B * TB, E])
        tensor("xn", [P, TB, E])
        tensor("stats", [P, TB, 6])
        tensor("mv", [P, TB, 2])
        tensor("std", [P, TB])
        tensor("rstd", [P, TB])
        made["xT_h"], made["xT_l"] = K.ffn_h[:, 0:2 * KC, :], K.ffn_l[:, 0:2 * KC, :]
        tensor("table", [P, 1])
        tensor("lam_in", [P, 4, HD])
        tensor("lam_pr", [P, 2, HD])
        tensor("lam_sum", [P, 2])
        tensor("lam_exp", [P, 2])
        banks("ps_t", KC)
        banks("ps_qk", 4)
        banks("ps_v", 2)
        w_loaded = [st.enter_context(nc.semaphore(f"w_loaded{n}")) for n in range(4)]
        x_loaded = [st.enter_context(nc.semaphore(f"x_loaded{n}")) for n in range(TB + B - 1)]
        sems("passed lam_loaded eps_set ident_set ones_set masks_set rings_set w_high w_low table_in dve_step var_ready "
             "std_ready xn_ready xT_turned xTh_ready xTl_ready qk_done v_done ph_ready pl_ready "
             "v_copied lam_dot lam_exped")
        M = named(made)
        LN_STEPS = 2 * TB

        block = st.enter_context(nc.Block())

        @block.sync
        def _(sp):
            for b in range(B):
                for t in range(TB) if b == 0 else (None,):
                    tiles = slice(t, t + 1) if b == 0 else slice(b * TB, (b + 1) * TB)
                    sp.dma_start(M.x[:, tiles], S.x.rearrange("b (t p) e -> p (b t) e", p=P)[:, tiles]
                                 ).then_inc(x_loaded[t if b == 0 else TB - 1 + b], 16)

            def store(b):
                sp.wait_ge(M.ph_ready, 4 * b + 4)
                sp.wait_ge(M.pl_ready, 4 * b + 4 + 4)
                sp.wait_ge(M.v_copied, TB * b + TB + 4)
                store_parts(sp, D, K, S, b)

            store(0)
            sp.wait_ge(M.rings_set, 2)
            sp.wait_ge(K.parts_stored, PARTS_STORED)
            for j in range(D.RING):
                load_kq(sp, D, K, S, j, j)
                if j < D.RING - 1:
                    load_v(sp, K, S, j, j)
            for b in range(1, STORED_EARLY):
                store(b)
        @block.scalar
        def _(act):
            weights = [w.rearrange("(c p) n -> p c n", p=P) for w in (S.wq, S.wk, S.wv, S.wo)]
            for n in range(3):
                act.dma_start(M.w_raw[:, n], weights[n]).then_inc(w_loaded[n], 16)
            act.wait_ge(M.eps_set, 1)

            def high(n):
                act.wait_ge(w_loaded[n], 16)
                act.copy(M.w_h[:, n] if n < 3 else K.wo_h[:, :, :], M.w_raw[:, n]).then_inc(M.w_high, 1)

            def spread(b):
                act.wait_ge(M.var_ready, b + 1)
                act.activation(M.std[:, :], M.mv[:, :, 1], ACT.Sqrt, bias=K.eps_col[:, 0:1]
                               ).then_inc(M.std_ready, 1)

            def turned_high(b):
                act.wait_ge(M.xT_turned, b + 2)
                act.wait_ge(M.v_done, b + 1)
                for c in range(KC):
                    act.copy(entry(M.xT_h, KC * (b % 2) + c), M.ps_t[c][:, :]).then_inc(M.xTh_ready, 1)

            def parts_high(b):
                for c in range(4):
                    act.wait_ge(M.qk_done, 4 * b + c + 1)
                    act.activation(entry(K.part_h, 4 * b + c), M.ps_qk[c][:, :], ACT.Copy,
                                   scale=D.SCALE if c < KC else 1.0).then_inc(M.ph_ready, 1)

            def values(b):
                act.wait_ge(M.v_done, b + 3)
                for t in range(TB):
                    act.copy(K.v_stage[:, bass.ds(b, 1), :, t, :, 0:VD].rearrange("p o g h d -> p (o g) h d"),
                             M.ps_v[t // 2][:, (t % 2) * E:(t % 2 + 1) * E].rearrange(
                                 "p (g h d) -> p g h d", g=G, d=VD)).then_inc(M.v_copied, 1)

            act.activation(M.table[:, :], K.eps_col[:, :], ACT.Sqrt).then_inc(M.table_in, 1)
            for n in range(3):
                high(n)
            spread(0)
            act.dma_start(M.w_raw[:, 3], weights[3]).then_inc(w_loaded[3], 16)
            for n, v in enumerate((S.lq1, S.lk1, S.lq2, S.lk2)):
                act.dma_start(M.lam_in[:, n, :], v.partition_broadcast(P)).then_inc(M.lam_loaded, 16)
            act.wait_ge(M.ones_set, 1)
            turned_high(0)
            high(3)
            with act.Fori(0, B - 1) as b:
                spread(b + 1)
                parts_high(b)
                turned_high(b + 1)
                values(b)
            parts_high(B - 1)
            values(B - 1)
            act.wait_ge(M.lam_dot, 1)
            act.activation(M.lam_exp[:, :], M.lam_sum[:, :], ACT.Exp).then_inc(M.lam_exped, 1)

        @block.gpsimd
        def _(pool):
            pool.sem_inc(M.v_copied, 4)
            pool.sem_inc(M.v_done, 2)
            pool.sem_inc(M.xT_turned, 1)
            pool.sem_inc(M.xTl_ready, KC)
            pool.sem_inc(M.pl_ready, 4)
            pool.memset(K.eps_col[:, :], EPS).then_inc(M.eps_set, 1)
            pool.memset(K.ident[:, :], 1.0).then_inc(M.ident_set, 1)
            pool.wait_ge(M.ident_set, 1)
            pool.affine_select(out=K.ident[:, :], in_=K.ident[:, :], pattern=[[-1, P]],
                               compare_op=ALU.is_equal, fill=0.0, base=0,
                               channel_multiplier=1).then_inc(M.ident_set, 1)
            def low(n):
                high_half = M.w_h[:, n] if n < 3 else K.wo_h[:, :, :]
                low_half = M.w_l[:, n] if n < 3 else K.wo_l[:, :, :]
                pool.wait_ge(M.w_high, n + 1)
                pool.tensor_tensor(low_half, M.w_raw[:, n], high_half.bitcast(F32),
                                   ALU.subtract).then_inc(M.w_low, 1)

            pool.memset(K.v_stage[:, :, :, :, :, :], 1.0).then_inc(M.ones_set, 1)
            for n in range(3):
                low(n)
            pool.memset(K.zeros_b[:, :], 0.0).then_inc(M.masks_set, 1)
            pool.memset(K.mask_b[:, :, :], MASKED).then_inc(M.masks_set, 1)
            pool.memset(K.ident_b[:, :], 1.0).then_inc(M.masks_set, 1)
            pool.wait_ge(M.masks_set, 3)
            pool.affine_select(out=K.mask_b[:, :, :], in_=K.mask_b[:, :, :], pattern=[[0, 4], [1, P]],
                               compare_op=ALU.is_gt, fill=0.0, base=0,
                               channel_multiplier=-1).then_inc(M.masks_set, 1)
            pool.affine_select(out=K.ident_b[:, :], in_=K.ident_b[:, :], pattern=[[-1, P]],
                               compare_op=ALU.is_equal, fill=0.0, base=0,
                               channel_multiplier=1).then_inc(M.masks_set, 1)
            pool.memset(K.k_ring[:, :, :].bitcast(F32), 1.0).then_inc(M.rings_set, 1)
            pool.memset(K.q_ring[:, :, :, :].bitcast(F32), 0.0).then_inc(M.rings_set, 1)
            low(3)

        @block.vector
        def _(dve):
            def x_tile(b, t):
                return entry(M.x, b * TB + t)

            def norm(b):
                for t in range(TB):
                    if isinstance(b, int) and b == 0:
                        dve.wait_ge(x_loaded[t], 16)
                    dve.bn_stats(M.stats[:, t, :], x_tile(b, t)).then_inc(M.dve_step, 1)
                dve.wait_ge(M.dve_step, LN_STEPS * b + TB)
                stand(dve, M.passed)
                for t in range(TB):
                    dve.bn_aggr(M.mv[:, t, :], M.stats[:, t, :]).then_inc(
                        M.var_ready if t == TB - 1 else M.dve_step, 1)
                dve.wait_ge(M.std_ready, b + 1)
                dve.reciprocal(M.rstd[:, :], M.std[:, :]).then_inc(M.dve_step, 1)
                dve.wait_ge(M.dve_step, LN_STEPS * b + 2 * TB)
                dve.wait_ge(M.xT_turned, b + 1)
                for t in range(TB):
                    dve.tensor_scalar(M.xn[:, t, :], x_tile(b, t), M.mv[:, t, 0:1],
                                      M.rstd[:, t:t + 1], ALU.subtract, ALU.mult).then_inc(M.xn_ready, 1)

            def turned_low(b):
                for c in range(KC):
                    dve.wait_ge(M.xTh_ready, KC * b + c + 1)
                    at = KC * (b % 2) + c
                    dve.tensor_tensor(entry(M.xT_l, at), M.ps_t[c][:, :], entry(M.xT_h, at).bitcast(F32),
                                      ALU.subtract).then_inc(M.xTl_ready, 1)

            def parts_low(b):
                for c in range(4):
                    dve.wait_ge(M.ph_ready, 4 * b + c + 1)
                    dve.scalar_tensor_tensor(entry(K.part_l, 4 * b + c), M.ps_qk[c][:, :],
                                             D.SCALE if c < KC else 1.0,
                                             entry(K.part_h, 4 * b + c).bitcast(F32), ALU.mult,
                                             ALU.subtract).then_inc(M.pl_ready, 1)

            norm(0)
            for b in range(1, B):
                dve.wait_ge(x_loaded[TB - 1 + b], 16)
            turned_low(0)
            with dve.Fori(0, B - 1) as b:
                norm(b + 1)
                parts_low(b)
                turned_low(b + 1)
            parts_low(B - 1)
            link = chained(dve, M.dve_step, LN_STEPS * B)
            dve.wait_ge(M.lam_loaded, 64)
            pairs = M.lam_in[:, :, :].rearrange("p (a two) d -> p a two d", two=2)
            link(dve.tensor_tensor(M.lam_pr[:, :, :], pairs[:, :, 0, :], pairs[:, :, 1, :], ALU.mult))
            dve.tensor_reduce(M.lam_sum[:, :], M.lam_pr[:, :, :], AX.X, ALU.add).then_inc(M.lam_dot, 1)
            dve.wait_ge(M.lam_exped, 1)
            link(dve.tensor_tensor(K.neg_lam[:, :], M.lam_exp[:, 1:2], M.lam_exp[:, 0:1], ALU.subtract))
            link(dve.tensor_scalar(K.neg_lam[:, :], K.neg_lam[:, :], -LAMBDA_INIT, None, ALU.add))

        @block.tensor
        def _(pe):
            pe.wait_ge(M.ident_set, 2)

            def turn(b):
                pe.wait_ge(M.xTl_ready, KC * b + KC)
                for t in range(TB):
                    pe.wait_ge(M.xn_ready, TB * b + t + 1)
                    for c in range(KC):
                        ins = pe.transpose(M.ps_t[c][:, t * P:(t + 1) * P],
                                           M.xn[:, t, c * P:(c + 1) * P], K.ident[:, :])
                ins.then_inc(M.xT_turned, 1)

            def queries_keys(b, j):
                pe.wait_ge(M.xTl_ready, KC * b + 2 * KC)
                pe.wait_ge(M.pl_ready, 4 * b + 4)
                for part in range(4):
                    n, m = part // KC, part % KC
                    if m == 0:
                        pe.wait_ge(M.w_low, n + 1)
                    for c in range(KC):
                        ins = matmul3(pe, M.ps_qk[part][:, :],
                                      [w[:, n, c, m * P:(m + 1) * P] for w in (M.w_h, M.w_l)],
                                      [x[:, KC * j + c, :] for x in (M.xT_h, M.xT_l)],
                                      start=c == 0, stop=c == KC - 1)
                    ins.then_inc(M.qk_done, 1)

            def values(b, j):
                pe.wait_ge(M.w_low, 3)
                pe.wait_ge(M.v_copied, 4 * b + 4)
                for t in range(TB):
                    for c in range(KC):
                        ins = matmul3(pe, M.ps_v[t // 2][:, (t % 2) * E:(t % 2 + 1) * E],
                                      [x[:, KC * j + c, t * P:(t + 1) * P] for x in (M.xT_h, M.xT_l)],
                                      [w[:, 2, c, :] for w in (M.w_h, M.w_l)],
                                      start=c == 0, stop=c == KC - 1)
                ins.then_inc(M.v_done, 1)

            def pair(b, last=False):
                for j in range(2):
                    queries_keys(b + j, j)
                    if not (last and j == 1):
                        turn(b + j + 1)
                    values(b + j, j)

            turn(0)
            with pe.Fori(0, B // 2 - 1) as r:
                pair(2 * r)
            pair(B - 2, last=True)


def attend(nc, D, K, S):
    T, TB, VD, VW, SH, ROWS, HD, STEPS = D.T, D.TB, D.VD, D.VW, D.SH, D.ROWS, D.HD, D.STEPS
    RING, E, KC, NS, NX = D.RING, D.E, D.KC, D.NS, D.NX
    ROUNDS = STEPS // RING
    made = {}
    with ExitStack() as st:
        tensor, banks, sems = allocator(nc, st, made, "attend_")
        tensor("weights", [P, 2, 2 * E])
        tensor("m_rows", [2 * SH, RING, T], F32R)
        tensor("probs", [P, 5, 2, 512])
        tensor("pv_copy", [P, T])
        tensor("sums_pv", [P, 2, TB, SH, VW])
        tensor("recip", [P, 2, TB, 2, 2])
        tensor("first", [P, TB, 2, VD])
        tensor("second", [P, TB, 2, VD])
        tensor("neg_max", [P, TB, SH])
        tensor("neg_max2", [P, TB, 2, SH], F32R)
        made["ps_s"] = st.enter_context(nc.psum_tensor("ps_s", [P, 2, 2, 512], F32))
        banks("ps_m", 2)
        banks("ps_pv", 1)
        banks("ps_turn", 1)
        weights_loaded = [st.enter_context(nc.semaphore(f"weights_loaded{j}")) for j in range(2)]
        m_loaded = [st.enter_context(nc.semaphore(f"m_loaded{j}")) for j in range(RING)]
        sems("passed pv_zeroed s_filled exp_done max_filled max_read max_step max_halves m_turned "
             "m_copied weights_high weights_low cut_done pv_stage pv_copied out_turned acc_stored recip_step recip_ready parts_ready mixed")
        M = named(made)

        def chunk(u):
            if u < 2:
                return [(n, 2 * u + n, 0, 0) for n in range(2)]
            if u < 4:
                return [(n, 2 * (u - 2) + n, kb, col) for n in range(2) for kb, col in ((1, 0), (3, 384))]
            return [(s // 2, s, 2, 256 * (s % 2)) for s in range(SH)]

        CHUNKS = 5
        WEIGHT_ROUNDS = NX // RING
        FILLS = [(3, [s]) for s in range(SH)] + [(2, [s]) for s in range(SH)] + [(1, [0, 1]), (1, [2, 3])] \
            + [(0, list(range(SH)))]
        NF = len(FILLS)

        block = st.enter_context(nc.Block())

        @block.sync
        def _(sp):
            def load_weights(n, j):
                sp.wait_ge(M.weights_low, n + 1)
                up, down = M.weights[:, j % 2, 0:E], M.weights[:, j % 2, E:2 * E]
                if isinstance(n, int):
                    sources = S.shared_up[:, n * P:(n + 1) * P], S.shared_down[n * P:(n + 1) * P, :]
                else:
                    e = bass.ds(n - NS, 1)
                    sources = (S.w_up[e].rearrange("o a i -> (o a) i"), S.w_down[e].rearrange("o i e -> (o i) e"))
                sp.dma_start(up.rearrange("p (c i) -> p c i", c=KC), sources[0].rearrange("(c p) i -> p c i", p=P)
                             ).then_inc(weights_loaded[j % 2], 16)
                sp.dma_start(down, sources[1]).then_inc(weights_loaded[j % 2], 16)

            def load_max(i, j):
                sp.wait_ge(M.m_copied, i + 1)
                for s in range(SH):
                    sp.dma_start(K.q_ring[3 * ROWS:3 * ROWS + 2, j, s, :].bitcast(F32),
                                 M.m_rows[s::SH, j, :].bitcast(F32)).then_inc(m_loaded[j], 16)

            load_max(0, 0)

            def step(i, j, last=False, weights=True):
                if not (last and j > 0):
                    sp.wait_ge(M.pv_stage, 3 * i + 3)
                    load_v(sp, K, S, i + RING - 1, (j - 1) % RING)
                if not (last and j == RING - 1):
                    load_max(i + 1, (j + 1) % RING)
                if weights:
                    load_weights(i, j)
                if not last:
                    sp.wait_ge(M.s_filled, CHUNKS * i + CHUNKS)
                    load_kq(sp, D, K, S, i + RING, j)

            for j in range(RING):
                step(j, j)
                if j + 1 < D.B - STORED_EARLY + 1:
                    store_parts(sp, D, K, S, STORED_EARLY + j)
            sp.wait_ge(K.parts_stored, PARTS_STORED * D.B)
            with sp.Fori(1, WEIGHT_ROUNDS) as r:
                for j in range(RING):
                    step(r * RING + j, j)
            with sp.Fori(WEIGHT_ROUNDS, ROUNDS - 1) as r:
                for j in range(RING):
                    step(r * RING + j, j, weights=False)
            for j in range(RING):
                step(STEPS - RING + j, j, last=True, weights=False)

        @block.gpsimd
        def _(pool):
            pool.sem_inc(M.weights_low, 2)
            def split_low(n, j):
                at = entry(K.ffn_h, n), entry(K.ffn_l, n)
                pool.wait_ge(M.weights_high, n + 1)
                pool.tensor_tensor(at[1], M.weights[:, j % 2, :], at[0].bitcast(F32), ALU.subtract
                                   ).then_inc(M.weights_low, 1)

            def cut(view):
                pool.affine_select(out=view, in_=view, pattern=[[0, SH], [1, P]], compare_op=ALU.is_ge,
                                   fill=0.0, base=0, channel_multiplier=-1).then_inc(M.cut_done, 1)

            def mix(i, j):
                pool.wait_ge(M.recip_ready, i + 1)
                pool.wait_ge(M.mixed, i + 2)
                pv = M.sums_pv[:, j % 2].rearrange("p t (h two) w -> p t h two w", two=2)
                for n, o in enumerate((M.first, M.second)):
                    pool.tensor_tensor(o[:, :, :, :], pv[:, :, :, n, 0:VD],
                                       M.recip[:, j % 2, :, :, n].unsqueeze(3).to_broadcast([P, TB, 2, VD]),
                                       ALU.mult).then_inc(M.parts_ready, 1)
                pool.wait_ge(M.parts_ready, 2 * i + 2)
                pool.tensor_tensor(entry(K.attn, i), M.first[:, :, :, :].rearrange("p t h d -> p (t h d)"),
                                   M.second[:, :, :, :].rearrange("p t h d -> p (t h d)"), ALU.add
                                   ).then_inc(M.mixed, 1)

            def step(i, j, first=False, weights=True):
                pool.wait_ge(M.exp_done, CHUNKS * i + 2 + 2)
                stand(pool, M.passed)
                cut(M.probs[:, 0:2].rearrange("p u n q -> p (u n) q")[:, :, 0:P])
                pool.wait_ge(M.exp_done, CHUNKS * i + 4 + 2)
                stand(pool, M.passed)
                tiles = M.probs[:, 2:4].rearrange("p u n q -> p (u n) q")
                cut(tiles[:, :, 0:P])
                cut(tiles[:, :, T - P:T])
                pool.wait_ge(M.exp_done, CHUNKS * i + 5 + 2)
                stand(pool, M.passed)
                halves = M.probs[:, 4].rearrange("p n (a q) -> p (n a) q", a=2)
                cut(halves[:, :, 0:P])
                if not first:
                    mix(i - 1, (j - 1) % RING)
                if weights:
                    split_low(i, j)

            for j in range(RING):
                step(j, j, first=j == 0)
            with pool.Fori(1, WEIGHT_ROUNDS) as r:
                for j in range(RING):
                    step(r * RING + j, j)
            with pool.Fori(WEIGHT_ROUNDS, ROUNDS) as r:
                for j in range(RING):
                    step(r * RING + j, j, weights=False)
            mix(STEPS - 1, RING - 1)

        @block.scalar
        def _(act):
            act.sem_inc(M.exp_done, 2)
            act.sem_inc(M.pv_copied, 1)
            act.sem_inc(M.out_turned, 1)
            act.sem_inc(M.pv_stage, 3)

            def exp(i, u, parity):
                act.wait_ge(M.s_filled, CHUNKS * i + u + 1)
                act.wait_ge(M.pv_stage, 3 * i + u // 2 + 1)
                act.activation(M.probs[:, u], M.ps_s[:, parity], ACT.Exp).then_inc(M.exp_done, 1)

            def copy_max(i, j):
                act.wait_ge(M.m_turned, i + 1)
                act.copy(M.m_rows[:, j, :], M.ps_turn[0][0:2 * SH, :]).then_inc(M.m_copied, 1)

            def copy_pv(i):
                act.wait_ge(M.pv_stage, 3 * i + 3 + 3)
                act.wait_ge(M.out_turned, i + 1)
                act.copy(M.pv_copy[:, :], M.ps_pv[0][:, :]).then_inc(M.pv_copied, 1)

            def split_high(n, j):
                turn = n // 2 if isinstance(n, int) else r_turns[0] * (RING // 2) + j // 2
                act.wait_ge(weights_loaded[j % 2], 32 * (turn + 1))
                act.copy(entry(K.ffn_h, n), M.weights[:, j % 2, :]).then_inc(M.weights_high, 1)

            def step(i, j, first=False, last=False, weights=True):
                exp(i, 0, (CHUNKS * j) % 2)
                if not first:
                    copy_pv(i - 1)
                if not (last and j == RING - 1):
                    copy_max(i + 1, (j + 1) % RING)
                exp(i, 1, (CHUNKS * j + 1) % 2)
                for u in range(2, CHUNKS):
                    exp(i, u, (CHUNKS * j + u) % 2)
                if weights:
                    split_high(i, j)

            r_turns = [0]
            copy_max(0, 0)
            for j in range(RING):
                step(j, j, first=j == 0)
            with act.Fori(1, WEIGHT_ROUNDS) as r:
                r_turns[0] = r
                for j in range(RING):
                    step(r * RING + j, j)
            with act.Fori(WEIGHT_ROUNDS, ROUNDS - 1) as r:
                for j in range(RING):
                    step(r * RING + j, j, weights=False)
            for j in range(RING):
                step(STEPS - RING + j, j, last=True, weights=False)
            copy_pv(STEPS - 1)

        @block.vector
        def _(dve):
            dve.sem_inc(M.max_read, 2)
            dve.sem_inc(M.acc_stored, 2)
            dve.sem_inc(M.mixed, 2)

            def reduce(i, j, f, first=False):
                tile, heads = FILLS[f]
                if f == 0 and not first:
                    dve.wait_ge(M.max_halves, i)
                dve.wait_ge(M.max_filled, NF * i + f + 1)
                dve.tensor_reduce(M.neg_max[:, tile, heads[0]:heads[-1] + 1],
                                  M.ps_m[(NF * j + f) % 2][:, 0:len(heads) * (tile + 1) * P]
                                  .rearrange("p (s k) -> p s k", s=len(heads)),
                                  AX.X, ALU.max, negate=True).then_inc(M.max_read, 1)

            def halves(i, first=False):
                dve.wait_ge(M.max_read, NF * i + NF + 2)
                if not first:
                    dve.wait_ge(M.m_turned, i)
                dve.tensor_copy(M.neg_max2[:, :, 0, :], M.neg_max[:, :, :]).then_inc(M.max_step, 1)
                dve.wait_ge(M.max_step, i + 1)
                dve.tensor_tensor(M.neg_max2[:, :, 1, :], M.neg_max[:, :, :],
                                  M.neg_max2[:, :, 0, :].bitcast(F32), ALU.subtract
                                  ).then_inc(M.max_halves, 1)

            def store(i, j):
                dve.wait_ge(M.out_turned, i + 2)
                dve.wait_ge(M.mixed, i + 1)
                dve.tensor_copy(
                    M.sums_pv[:, j % 2],
                    M.ps_turn[0][:, :].rearrange("p (t s w) -> p t s w", t=TB, s=SH)[:, :, :, 0:VW]
                ).then_inc(M.acc_stored, 1)
                dve.wait_ge(M.acc_stored, i + 3)
                r = M.recip[:, j % 2]
                dve.reciprocal(r.rearrange("p t h two -> p t (h two)"), M.sums_pv[:, j % 2, :, :, VD]
                               ).then_inc(M.recip_step, 1)
                dve.wait_ge(M.recip_step, i + 1)
                odd = r.rearrange("p t h two -> p (t h) two")[:, :, 1]
                dve.tensor_scalar(odd, odd, K.neg_lam[:, 0:1], None, ALU.mult).then_inc(M.recip_ready, 1)

            def step(i, j, first=False, last=False):
                ahead = not (last and j >= RING - 2)
                for f in range(NF):
                    if ahead:
                        reduce(i + 2, (j + 2) % RING, f)
                    if f == 3 and not first:
                        store(i - 1, (j - 1) % RING)
                if ahead:
                    halves(i + 2)

            for i in range(2):
                for f in range(NF):
                    reduce(i, i, f, first=i == 0)
                halves(i, first=i == 0)
            for j in range(RING):
                step(j, j, first=j == 0)
            with dve.Fori(1, ROUNDS - 1) as r:
                for j in range(RING):
                    step(r * RING + j, j)
            for j in range(RING):
                step(STEPS - RING + j, j, last=True)
            store(STEPS - 1, RING - 1)

        @block.tensor
        def _(pe):
            rounds = [0]
            pe.matmul(M.ps_pv[0][:, :], K.ident_b[:, :], K.zeros_b[:, :], start=True, stop=True
                      ).then_inc(M.pv_zeroed, 1)

            def scores(i, j, u):
                parity = (CHUNKS * j + u) % 2
                if u == 0:
                    pe.wait_ge(m_loaded[j], 16 * SH * (rounds[0] + 1))
                pe.wait_ge(M.exp_done, CHUNKS * i + u + 1)
                for n, s, kb, col in chunk(u):
                    q0 = kb * P
                    ins = pe.matmul(M.ps_s[:, parity, n, col:col + T - q0],
                                    K.k_ring[:, j, q0:q0 + P], K.q_ring[:, j, s, q0:T],
                                    start=True, stop=True)
                ins.then_inc(M.s_filled, 1)

            def maxima(i, j, f):
                tile, heads = FILLS[f]
                ps = M.ps_m[(NF * j + f) % 2]
                n_k = (tile + 1) * P
                pe.wait_ge(M.max_read, NF * i + f + 1)
                for n, s in enumerate(heads):
                    pe.matmul(ps[:, n * n_k:(n + 1) * n_k],
                              K.q_ring[0:3 * ROWS, j, s, tile * P:(tile + 1) * P],
                              K.k_ring[0:3 * ROWS, j, 0:n_k], start=n == 0, stop=False)
                diagonal = ps[:, 0:len(heads) * n_k].rearrange("p (s k) -> p s k", s=len(heads))
                pe.matmul(diagonal[:, :, n_k - P:n_k], K.ident_b[:, :], K.mask_b[:, 0:len(heads), :],
                          start=False, stop=True).then_inc(M.max_filled, 1)

            def turn_max(i):
                pe.wait_ge(M.max_halves, i + 1)
                for t in range(TB):
                    ins = pe.transpose(M.ps_turn[0][0:2 * SH, t * P:(t + 1) * P],
                                       M.neg_max2[:, t].bitcast(F32).rearrange("p h s -> p (h s)"),
                                       K.ident[:, :])
                ins.then_inc(M.m_turned, 1)

            def pv(i, j, stage, tiles=None):
                pe.wait_ge(M.cut_done, 4 * i + (1, 3, 4)[stage])
                if stage == 0:
                    pe.wait_ge(K.v_loaded[j], 16 * (rounds[0] + 1))
                    pe.wait_ge(M.pv_copied, i + 1)
                for kb in tiles or ((0,), (1, 3), (2,))[stage]:
                    for s in range(SH):
                        u = {0: s // 2, 1: 2 + s // 2, 2: 4, 3: 2 + s // 2}[kb]
                        n, _, _, col = [c for c in chunk(u) if c[1] == s and c[2] == kb][0]
                        ins = pe.matmul(M.ps_pv[0][32 * s:32 * s + VW, kb * P:T],
                                        K.v_ring[:, j, kb, s // 2, :],
                                        M.probs[:, u, n, col:col + T - kb * P],
                                        start=kb == 0, stop=kb == 2)
                if kb != 1:
                    ins.then_inc(M.pv_stage, 1)

            def turn_out(i):
                pe.wait_ge(M.pv_copied, i + 2)
                for t in range(TB):
                    ins = pe.transpose(M.ps_turn[0][:, t * P:(t + 1) * P],
                                       M.pv_copy[:, t * P:(t + 1) * P], K.ident[:, :])
                ins.then_inc(M.out_turned, 1)

            def step(i, j, first=False, last=False):
                ahead = not (last and j >= RING - 2)
                if ahead:
                    pe.wait_ge(K.kq_loaded[(j + 2) % RING], 16 * STEP_LOADS * (rounds[0] + (j + 2) // RING + 1))

                def more(*fills):
                    if ahead:
                        for f in fills:
                            maxima(i + 2, (j + 2) % RING, f)
                scores(i, j, 0)
                more(0)
                if not first:
                    pv(i - 1, (j - 1) % RING, 2)
                more(1)
                if not (last and j == RING - 1):
                    pe.wait_ge(M.m_copied, i + 1)
                    pe.wait_ge(M.acc_stored, i + 1)
                    turn_max(i + 1)
                scores(i, j, 1)
                more(2)
                scores(i, j, 2)
                if not first:
                    if not (last and j == RING - 1):
                        pe.wait_ge(M.m_copied, i + 2)
                    pe.wait_ge(M.acc_stored, i + 1)
                    turn_out(i - 1)
                more(3)
                scores(i, j, 3)
                more(4)
                pv(i, j, 0)
                more(5)
                scores(i, j, 4)
                more(6)
                more(7)
                pv(i, j, 1, (1,))
                more(8)
                pv(i, j, 1, (3,))
                more(9, 10)

            for i in range(2):
                pe.wait_ge(K.kq_loaded[i], 16 * STEP_LOADS)
                for f in range(NF):
                    maxima(i, i, f)
                if i == 0:
                    turn_max(0)
            for j in range(RING):
                step(j, j, first=j == 0)
            with pe.Fori(1, ROUNDS - 1) as r:
                rounds[0] = r
                for j in range(RING):
                    step(r * RING + j, j)
            rounds[0] = ROUNDS - 1
            for j in range(RING):
                step(STEPS - RING + j, j, last=True)
            pv(STEPS - 1, RING - 1, 2)
            pe.wait_ge(M.acc_stored, STEPS - 1 + 2)
            turn_out(STEPS - 1)


def experts(nc, D, K, S):
    B, T, E, TB, KC, G, VD, NE, NX, NS = D.B, D.T, D.E, D.TB, D.KC, D.G, D.VD, D.NE, D.NX, D.NS
    H = G * 2 * TB
    GS = NE // GROUPS
    made = {}
    with ExitStack() as st:
        tensor, banks, sems = allocator(nc, st, made, "experts_")
        tensor("x_sb", [P, B * TB, E])
        tensor("square", [P, H, VD])
        tensor("mean_sq", [P, H])
        tensor("head_std", [P, H])
        tensor("head_rstd", [P, H])
        tensor("normed", [P, TB, E])
        tensor("aT_h", [P, KC, T], F32R)
        tensor("aT_l", [P, KC, T], F32R)
        tensor("stats", [P, TB, 6])
        tensor("mv", [P, TB, 2])
        tensor("std", [P, TB])
        tensor("rstd", [P, TB])
        tensor("xT_h", [P, KC, 2 * T], F32R)
        tensor("xT_l", [P, KC, 2 * T], F32R)
        tensor("rw_raw", [NE, E])
        tensor("rw_h", [P, KC, P], F32R)
        tensor("rw_l", [P, KC, P], F32R)
        tensor("logitsT", [NE, T])
        tensor("combT", [NE, T])
        tensor("score", [P, TB, NE])
        tensor("biased", [P, TB, NE])
        tensor("bias", [P, NE])
        tensor("pair_sums", [P, TB * GROUPS, 6])
        tensor("group_score", [P, TB, GROUPS])
        tensor("group_mask", [P, TB, GROUPS])
        tensor("top_val", [P, TB])
        tensor("top_key", [P, TB, NE])
        tensor("first_hot", [P, TB, NE])
        tensor("second_hot", [P, TB, NE])
        tensor("order", [P, NE])
        tensor("comb", [P, TB, NE])
        tensor("relu", [P, 2, T])
        tensor("act", [P, 2, T])
        tensor("act_h", [P, 2, T], F32R)
        tensor("act_l", [P, 2, T], F32R)
        tensor("weight", [P, 4, T])
        tensor("outT", [P, KC, T])
        tensor("y", [P, 2, 2, E])
        banks("ps_h", 2)
        banks("ps_o", KC)
        banks("ps_t", 2)
        banks("ps_x", 2)
        weight_loaded = [st.enter_context(nc.semaphore(f"weight_loaded{j}")) for j in range(4)]
        sems("passed x_loaded router_loaded order_set rw_turned rw_high rw_low rw_zeroed "
             "squared mean_ready head_std_ready dve_step heads_normed heads_turned aTh_ready aTl_ready "
             "projected var_ready std_ready rows_normed rows_turned xTh_ready xTl_ready "
             "logits_done logits_copied logits_turned scored comb_ready comb_turned comb_copied comb_stored "
             "up_done relu_done weighted act_done high_done low_done down_done out_copied out_turned y_ready y_stored")
        M = named(made)

        def half(b):
            return (b % 2) * T

        def later(what, b, n, last):
            if n < NX:
                what(b, n)
            elif not last:
                what(b + 1, n - NX)

        block = st.enter_context(nc.Block())

        @block.sync
        def _(sp):
            sp.dma_start(M.rw_raw[:, :], S.router_w).then_inc(M.router_loaded, 16)
            sp.dma_start(M.bias[:, :], S.e_bias.partition_broadcast(P)).then_inc(M.router_loaded, 16)
            for b in range(B):
                if b:
                    sp.wait_ge(M.x_loaded, 16 * b)
                sp.dma_start(M.x_sb[:, b * TB:(b + 1) * TB, :], S.x[b].rearrange("(t p) e -> p t e", p=P)
                             ).then_inc(M.x_loaded, 16)

            def store_comb(b):
                sp.wait_ge(M.comb_copied, b + 2)
                sp.dma_start(S.comb[:, bass.ds(b * T, T)], M.combT[:, :]).then_inc(M.comb_stored, 16)
                sp.wait_ge(M.comb_stored, 16 * b + 32)
                stand(sp, M.passed)

            def load_weight(b, e):
                sp.wait_ge(M.weighted, NE * b + e + 1)
                sp.dma_start(M.weight[:, e % 4, :],
                             S.comb[e:e + 1, bass.ds(b * T, T)].rearrange("o t -> (o t)").partition_broadcast(P)
                             ).then_inc(weight_loaded[e % 4], 16)

            def store_out(b, pair):
                sp.wait_ge(M.y_ready, 2 * b + pair + 1 + 4)
                sp.dma_start(S.out.rearrange("b (t p) e -> p (b t) e", p=P)[:, bass.ds(b * TB + 2 * pair, 2), :],
                             M.y[:, pair]).then_inc(M.y_stored, 16)

            store_comb(0)

            def batch(b, first=False, last=False):
                for e in range(NE):
                    load_weight(b, e)
                    if e == 4 and not first:
                        store_out(b - 1, 0)
                        store_out(b - 1, 1)
                if not last:
                    store_comb(b + 1)

            batch(0, first=True)
            with sp.Fori(1, B - 1) as b:
                batch(b)
            batch(B - 1, last=True)
            store_out(B - 1, 0)
            store_out(B - 1, 1)
            sp.wait_ge(M.y_stored, 16 * 2 * B + 16)

        @block.gpsimd
        def _(pool):
            pool.sem_inc(M.weighted, 4)
            pool.sem_inc(M.y_stored, 16)
            pool.sem_inc(M.y_ready, 4)
            pool.sem_inc(M.comb_copied, 1)
            pool.sem_inc(M.comb_turned, 1)
            pool.sem_inc(M.comb_stored, 16)
            pool.sem_inc(M.rows_turned, 1)
            pool.sem_inc(M.relu_done, 2)
            pool.sem_inc(M.out_copied, KC)

            def square(b):
                heads = entries(K.attn, b * G, G).rearrange("p g (x d) -> p (g x) d", d=VD)
                pool.tensor_tensor(M.square[:, :, :], heads, heads, ALU.mult).then_inc(M.squared, 1)

            def weigh(b, n):
                e = n - NS
                k = NX * b + n
                pool.wait_ge(M.relu_done, k + 1 + 2)
                pool.wait_ge(weight_loaded[e % 4], 16 * ((NE // 4) * b + e // 4 + 1))
                pool.wait_ge(M.low_done, k + 1)
                pool.tensor_tensor(M.act[:, n % 2, :], M.relu[:, n % 2, :], M.weight[:, e % 4, :],
                                   ALU.mult).then_inc(M.weighted, 1)

            square(0)
            pool.memset(M.rw_h[:, :, :].bitcast(F32), 0.0).then_inc(M.rw_zeroed, 1)
            pool.memset(M.rw_l[:, :, :].bitcast(F32), 0.0).then_inc(M.rw_zeroed, 1)
            for e in range(NE):
                pool.memset(M.order[:, e:e + 1], float(NE - e)).then_inc(M.order_set, 1)
            def batch(b, last=False):
                for n in range(NX):
                    if n == 0 and not last:
                        pool.wait_ge(M.mean_ready, b + 1)
                        square(b + 1)
                    if n >= NS:
                        weigh(b, n)

            with pool.Fori(0, B - 1) as b:
                batch(b)
            batch(B - 1, last=True)

        @block.scalar
        def _(act):
            act.sem_inc(M.low_done, 2)
            act.sem_inc(M.down_done, 2)
            act.sem_inc(M.act_done, 2)
            act.sem_inc(M.out_turned, 2)

            def head_spread(b):
                act.wait_ge(M.mean_ready, b + 1)
                act.activation(M.head_std[:, :], M.mean_sq[:, :], ACT.Sqrt, bias=K.eps_col[:, 0:1],
                               scale=1.0 / VD).then_inc(M.head_std_ready, 1)

            def heads_high(b):
                act.wait_ge(M.heads_turned, b + 1)
                for c in range(KC):
                    act.copy(M.aT_h[:, c, :], M.ps_t[c][:, :]).then_inc(M.aTh_ready, 1)

            def spread(b):
                act.wait_ge(M.var_ready, b + 1)
                act.activation(M.std[:, :], M.mv[:, :, 1], ACT.Sqrt, bias=K.eps_col[:, 0:1]
                               ).then_inc(M.std_ready, 1)

            def rows_high(b):
                act.wait_ge(M.rows_turned, b + 2)
                for c in range(KC):
                    act.copy(M.xT_h[:, c, bass.ds(half(b), T)], M.ps_t[c][:, :]).then_inc(M.xTh_ready, 1)

            def copy_logits(b):
                act.wait_ge(M.logits_done, b + 1)
                act.copy(M.logitsT[:, :], M.ps_x[0][0:NE, :]).then_inc(M.logits_copied, 1)

            def score(b):
                act.wait_ge(M.logits_turned, b + 1)
                act.activation(M.score[:, :, :].rearrange("p t e -> p (t e)"),
                               M.ps_x[1][:, 0:TB * NE], ACT.Sigmoid).then_inc(M.scored, 1)

            def copy_comb(b):
                act.wait_ge(M.comb_turned, b + 2)
                act.wait_ge(M.comb_stored, 16 * b + 16)
                act.copy(M.combT[:, :], M.ps_x[0][0:NE, :]).then_inc(M.comb_copied, 1)

            def relu(b, n):
                k = NX * b + n
                act.wait_ge(M.up_done, k + 1)
                act.wait_ge(M.act_done, k + 1)
                act.activation(M.relu[:, n % 2, :], M.ps_h[n % 2][:, :], ACT.Relu).then_inc(M.relu_done, 1)

            def high(b, n):
                k = NX * b + n
                act.wait_ge(M.act_done, k + 1 + 2)
                act.wait_ge(M.down_done, k + 1)
                act.copy(M.act_h[:, n % 2, :], M.act[:, n % 2, :]).then_inc(M.high_done, 1)

            def copy_out(b):
                act.wait_ge(M.down_done, NX * b + NX + 2)
                act.wait_ge(M.out_turned, 2 * b + 2)
                for c in range(KC):
                    act.copy(M.outT[:, c, :], M.ps_o[c][:, :]).then_inc(M.out_copied, 1)

            act.wait_ge(M.rw_turned, 1)
            act.wait_ge(M.rw_zeroed, 2)
            act.copy(M.rw_h[:, :, 0:NE], M.ps_x[0][:, 0:KC * NE].rearrange("p (c e) -> p c e", c=KC)
                     ).then_inc(M.rw_high, 1)
            head_spread(0)
            heads_high(0)
            spread(0)
            rows_high(0)
            copy_logits(0)
            score(0)
            relu(0, 0)
            relu(0, 1)
            high(0, 0)

            def batch(b, first=False, last=False):
                for n in range(NX):
                    later(relu, b, n + 2, last)
                    later(high, b, n + 1, last)
                    if first and n == 2:
                        copy_comb(0)
                    if not last:
                        if n == 0:
                            head_spread(b + 1)
                        if n == 3:
                            heads_high(b + 1)
                        if n == 5:
                            spread(b + 1)
                        if n == 7:
                            rows_high(b + 1)
                        if n == 9:
                            copy_logits(b + 1)
                        if n == 10:
                            score(b + 1)
                        if n == 17:
                            copy_comb(b + 1)
                copy_out(b)

            batch(0, first=True)
            with act.Fori(1, B - 1) as b:
                batch(b)
            batch(B - 1, last=True)

        @block.vector
        def _(dve):
            ROUTER_STEPS = 35
            STEPS = 4 + 2 * TB + ROUTER_STEPS

            def mean_square(b):
                dve.wait_ge(M.squared, b + 1)
                dve.tensor_reduce(M.mean_sq[:, :], M.square[:, :, :], AX.X, ALU.add).then_inc(M.mean_ready, 1)

            def norm_heads(b):
                link = chained(dve, M.dve_step, STEPS * b)
                dve.wait_ge(M.head_std_ready, b + 1)
                link(dve.reciprocal(M.head_rstd[:, :], M.head_std[:, :]))
                link(dve.tensor_scalar(M.head_rstd[:, :], M.head_rstd[:, :], 1.0 - LAMBDA_INIT, None, ALU.mult))
                dve.wait_ge(M.rows_turned, b + 1)
                heads = entries(K.attn, b * G, G).rearrange("p g (t h d) -> p g t h d", t=TB, d=VD)
                scale = M.head_rstd[:, :].rearrange("p (g t h) -> p g t h", t=TB, h=2)
                for t in range(TB):
                    dve.tensor_tensor(M.normed[:, t, :].rearrange("p (g h d) -> p g h d", g=G, d=VD),
                                      heads[:, :, t], scale[:, :, t].unsqueeze(3).to_broadcast([P, G, 2, VD]),
                                      ALU.mult).then_inc(M.heads_normed, 1)

            def heads_low(b):
                for c in range(KC):
                    dve.wait_ge(M.aTh_ready, KC * b + c + 1)
                    dve.tensor_tensor(M.aT_l[:, c, :], M.ps_t[c][:, :], M.aT_h[:, c, :].bitcast(F32),
                                      ALU.subtract).then_inc(M.aTl_ready, 1)

            def add_rows(b):
                base = STEPS * b + 2
                dve.wait_ge(M.x_loaded, 16 * b + 16)
                dve.wait_ge(M.projected, b + 1)
                for pair in range(2):
                    rows = entries(M.x_sb, b * TB + 2 * pair, 2).rearrange("p t e -> p (t e)")
                    dve.tensor_tensor(rows, rows, M.ps_x[pair][:, :], ALU.add).then_inc(M.dve_step, 1)
                dve.wait_ge(M.dve_step, base + 2)
                stand(dve, M.passed)
                for t in range(TB):
                    dve.bn_stats(M.stats[:, t, :], entry(M.x_sb, b * TB + t)).then_inc(M.dve_step, 1)
                dve.wait_ge(M.dve_step, base + 2 + TB)
                stand(dve, M.passed)
                for t in range(TB):
                    dve.bn_aggr(M.mv[:, t, :], M.stats[:, t, :]).then_inc(
                        M.var_ready if t == TB - 1 else M.dve_step, 1)

            def norm_rows(b):
                dve.wait_ge(M.std_ready, b + 1)
                dve.reciprocal(M.rstd[:, :], M.std[:, :]).then_inc(M.dve_step, 1)
                dve.wait_ge(M.dve_step, STEPS * b + 4 + 2 * TB)
                dve.wait_ge(M.heads_turned, b + 1)
                for t in range(TB):
                    dve.tensor_scalar(M.normed[:, t, :], entry(M.x_sb, b * TB + t), M.mv[:, t, 0:1],
                                      M.rstd[:, t:t + 1], ALU.subtract, ALU.mult).then_inc(M.rows_normed, 1)

            def rows_low(b):
                for c in range(KC):
                    dve.wait_ge(M.xTh_ready, KC * b + c + 1)
                    at = bass.ds(half(b), T)
                    dve.tensor_tensor(M.xT_l[:, c, at], M.ps_t[c][:, :], M.xT_h[:, c, at].bitcast(F32),
                                      ALU.subtract).then_inc(M.xTl_ready, 1)

            def over(x, n):
                return x[:, :].unsqueeze(2).to_broadcast([P, TB, n])

            def top(link, vals, n, hot):
                key = M.top_key[:, :, 0:n]
                link(dve.tensor_reduce(M.top_val[:, :], vals, AX.X, ALU.max))
                link(dve.tensor_tensor(key, vals, over(M.top_val, n), ALU.is_equal))
                link(dve.tensor_tensor(key, key, M.order[:, 0:n].unsqueeze(1).to_broadcast([P, TB, n]), ALU.mult))
                link(dve.tensor_reduce(M.top_val[:, :], key, AX.X, ALU.max))
                link(dve.tensor_tensor(hot, key, over(M.top_val, n), ALU.is_equal))

            def top_one(link, vals, n, hot):
                top(link, vals, n, hot)
                link(dve.scalar_tensor_tensor(vals, hot, FAR, vals, ALU.mult, ALU.add))

            def top_other(link, vals, n, hot, both):
                top(link, vals, n, hot)
                link(dve.tensor_tensor(both, both, hot, ALU.add))

            def route(b, part):
                done = [0, 6, 12, 19, 25, 31][part]
                link = chained(dve, M.dve_step, STEPS * b + 4 + 2 * TB + done)
                groups = [hot[:, :, 0:GROUPS] for hot in (M.first_hot, M.second_hot)]
                chosen, other = M.first_hot[:, :, :], M.second_hot[:, :, :]
                if part == 0:
                    dve.wait_ge(M.scored, b + 1)
                    link(dve.tensor_tensor(M.biased[:, :, :], M.score[:, :, :],
                                           M.bias[:, :].unsqueeze(1).to_broadcast([P, TB, NE]), ALU.add))
                    s = M.biased[:, :, :].rearrange("p t (g k) -> p (t g) k", g=GROUPS)
                    for at, d in ((0, 1), (3, 2), (5, 3)):
                        link(dve.tensor_tensor(M.pair_sums[:, :, at:at + GS - d], s[:, :, 0:GS - d],
                                               s[:, :, d:GS], ALU.add))
                    link(dve.tensor_reduce(M.group_score[:, :, :].rearrange("p t g -> p (t g)"),
                                           M.pair_sums[:, :, :], AX.X, ALU.max))
                    link(dve.tensor_copy(M.group_mask[:, :, :], M.group_score[:, :, :]))
                elif part == 1:
                    top_one(link, M.group_mask[:, :, :], GROUPS, groups[0])
                elif part == 2:
                    top_other(link, M.group_mask[:, :, :], GROUPS, groups[1], groups[0])
                    link(dve.tensor_tensor(
                        M.biased[:, :, :].rearrange("p t (g k) -> p t g k", g=GROUPS),
                        M.biased[:, :, :].rearrange("p t (g k) -> p t g k", g=GROUPS),
                        groups[0].unsqueeze(3).to_broadcast([P, TB, GROUPS, GS]), ALU.mult))
                elif part == 3:
                    top_one(link, M.biased[:, :, :], NE, chosen)
                elif part == 4:
                    top_other(link, M.biased[:, :, :], NE, other, chosen)
                else:
                    link(dve.tensor_tensor(chosen, chosen, M.score[:, :, :], ALU.mult))
                    link(dve.tensor_reduce(M.top_val[:, :], chosen, AX.X, ALU.add))
                    link(dve.tensor_scalar(M.top_val[:, :], M.top_val[:, :], 1e-20, None, ALU.add))
                    link(dve.reciprocal(M.top_val[:, :], M.top_val[:, :]))
                    dve.wait_ge(M.comb_turned, b + 1)
                    dve.tensor_tensor(M.comb[:, :, :], chosen, over(M.top_val, NE), ALU.mult
                                      ).then_inc(M.comb_ready, 1)

            def activate(b, n):
                k = NX * b + n
                if n < NS:
                    dve.wait_ge(M.relu_done, k + 1 + 2)
                    dve.wait_ge(M.low_done, k + 1)
                    left = M.relu[:, n % 2, :]
                else:
                    dve.wait_ge(M.weighted, NE * b + n - NS + 1 + 4)
                    left = M.act[:, n % 2, :]
                dve.tensor_tensor(M.act[:, n % 2, :], left, M.relu[:, n % 2, :], ALU.mult
                                  ).then_inc(M.act_done, 1)

            def low(b, n):
                k = NX * b + n
                dve.wait_ge(M.high_done, k + 1 + 2)
                dve.wait_ge(M.down_done, k + 1)
                dve.tensor_tensor(M.act_l[:, n % 2, :], M.act[:, n % 2, :], M.act_h[:, n % 2, :].bitcast(F32),
                                  ALU.subtract).then_inc(M.low_done, 1)

            def add_out(b, pair):
                dve.wait_ge(M.out_turned, 2 * b + pair + 1 + 2)
                dve.wait_ge(M.y_stored, 32 * b + 16)
                rows = entries(M.x_sb, b * TB + 2 * pair, 2)
                dve.tensor_tensor(M.y[:, pair].rearrange("p t e -> p (t e)"),
                                  rows.rearrange("p t e -> p (t e)"), M.ps_t[pair][:, :], ALU.add
                                  ).then_inc(M.y_ready, 1)

            dve.sem_inc(M.high_done, 2)
            dve.wait_ge(M.rw_high, 1)
            dve.tensor_tensor(M.rw_l[:, :, 0:NE], M.ps_x[0][:, 0:KC * NE].rearrange("p (c e) -> p c e", c=KC),
                              M.rw_h[:, :, 0:NE].bitcast(F32), ALU.subtract).then_inc(M.rw_low, 1)
            mean_square(0)
            norm_heads(0)
            heads_low(0)
            add_rows(0)
            norm_rows(0)
            rows_low(0)
            dve.wait_ge(M.order_set, NE)
            dve.wait_ge(M.router_loaded, 32)
            activate(0, 0)
            activate(0, 1)
            low(0, 0)

            def batch(b, first=False, last=False):
                for n in range(NX):
                    later(low, b, n + 1, last)
                    later(activate, b, n + 2, last)
                    if n == 1 and not first:
                        add_out(b - 1, 0)
                        add_out(b - 1, 1)
                    if first and n < 2:
                        for part in range(3 * n, 3 * n + 3):
                            route(0, part)
                    if not last:
                        if n == 0:
                            mean_square(b + 1)
                        if n == 2:
                            norm_heads(b + 1)
                        if n == 3:
                            heads_low(b + 1)
                        if n == 5:
                            add_rows(b + 1)
                        if n == 6:
                            norm_rows(b + 1)
                        if n == 7:
                            rows_low(b + 1)
                        if 11 <= n < 17:
                            route(b + 1, n - 11)

            batch(0, first=True)
            with dve.Fori(1, B - 1) as b:
                batch(b)
            batch(B - 1, last=True)
            add_out(B - 1, 0)
            add_out(B - 1, 1)

        @block.tensor
        def _(pe):
            def turn_heads(b):
                pe.wait_ge(M.heads_normed, TB * b + TB)
                pe.wait_ge(M.y_ready, 2 * b + 2)
                turn(M.heads_turned)

            def turn_rows(b):
                pe.wait_ge(M.rows_normed, TB * b + TB)
                turn(M.rows_turned)

            def turn(semaphore):
                for c in range(KC):
                    for t in range(TB):
                        ins = pe.transpose(M.ps_t[c][:, t * P:(t + 1) * P],
                                           M.normed[:, t, c * P:(c + 1) * P], K.ident[:, :])
                ins.then_inc(semaphore, 1)

            def project_heads(b):
                pe.wait_ge(M.aTl_ready, KC * b + KC)
                pe.wait_ge(M.comb_copied, b + 1)
                for t in range(TB):
                    for c in range(KC):
                        ins = matmul3(pe, M.ps_x[t // 2][:, (t % 2) * E:(t % 2 + 1) * E],
                                      [x[:, c, t * P:(t + 1) * P] for x in (M.aT_h, M.aT_l)],
                                      [w[:, c, :] for w in (K.wo_h, K.wo_l)],
                                      start=c == 0, stop=c == KC - 1)
                ins.then_inc(M.projected, 1)

            def logits(b):
                pe.wait_ge(M.xTl_ready, KC * b + KC)
                pe.wait_ge(M.var_ready, b + 1)
                for c in range(KC):
                    ins = matmul3(pe, M.ps_x[0][:, :], [w[:, c, :] for w in (M.rw_h, M.rw_l)],
                                  [x[:, c, bass.ds(half(b), T)] for x in (M.xT_h, M.xT_l)],
                                  start=c == 0, stop=c == KC - 1)
                ins.then_inc(M.logits_done, 1)

            def turn_logits(b):
                pe.wait_ge(M.logits_copied, b + 1)
                stand(pe, M.passed)
                for t in range(TB):
                    ins = pe.transpose(M.ps_x[1][:, t * NE:(t + 1) * NE],
                                       M.logitsT[:, t * P:(t + 1) * P], K.ident[0:NE, 0:NE])
                ins.then_inc(M.logits_turned, 1)

            def turn_comb(b):
                pe.wait_ge(M.comb_ready, b + 1)
                for t in range(TB):
                    ins = pe.transpose(M.ps_x[0][0:NE, t * P:(t + 1) * P], M.comb[:, t, :], K.ident[:, :])
                ins.then_inc(M.comb_turned, 1)

            def up(b, n):
                pe.wait_ge(M.relu_done, NX * b + n + 1)
                for c in range(KC):
                    ins = matmul3(pe, M.ps_h[n % 2][:, :], [w[:, n, c * P:(c + 1) * P] for w in (K.ffn_h, K.ffn_l)],
                                  [x[:, c, bass.ds(half(b), T)] for x in (M.xT_h, M.xT_l)],
                                  start=c == 0, stop=c == KC - 1)
                ins.then_inc(M.up_done, 1)

            def down(b, n):
                if n == 0:
                    pe.wait_ge(M.out_copied, KC * b + KC)
                pe.wait_ge(M.low_done, NX * b + n + 1 + 2)
                for c in range(KC):
                    ins = matmul3(pe, M.ps_o[c][:, :],
                                  [w[:, n, E + c * P:E + (c + 1) * P] for w in (K.ffn_h, K.ffn_l)],
                                  [a[:, n % 2, :] for a in (M.act_h, M.act_l)],
                                  start=n == 0, stop=n == NX - 1)
                ins.then_inc(M.down_done, 1)

            def turn_out(b, pair):
                pe.wait_ge(M.out_copied, KC * b + 2 * KC)
                for t in range(2):
                    for c in range(KC):
                        ins = pe.transpose(M.ps_t[pair][:, t * E + c * P:t * E + (c + 1) * P],
                                           M.outT[:, c, (2 * pair + t) * P:(2 * pair + t + 1) * P],
                                           K.ident[:, :])
                ins.then_inc(M.out_turned, 1)

            pe.wait_ge(M.router_loaded, 32)
            for c in range(KC):
                ins = pe.transpose(M.ps_x[0][:, c * NE:(c + 1) * NE], M.rw_raw[:, c * P:(c + 1) * P],
                                   K.ident[0:NE, 0:NE])
            ins.then_inc(M.rw_turned, 1)
            turn_heads(0)
            pe.wait_ge(M.rw_low, 1)
            project_heads(0)
            turn_rows(0)
            logits(0)
            turn_logits(0)
            up(0, 0)
            up(0, 1)

            def batch(b, first=False, last=False):
                for n in range(NX):
                    later(up, b, n + 2, last)
                    if not first and n < 2:
                        turn_out(b - 1, n)
                    if first and n == 2:
                        turn_comb(0)
                    if not last:
                        if n == 3:
                            turn_heads(b + 1)
                        if n == 5:
                            project_heads(b + 1)
                        if n == 7:
                            turn_rows(b + 1)
                        if n == 9:
                            logits(b + 1)
                        if n == 10:
                            turn_logits(b + 1)
                        if n == 18:
                            turn_comb(b + 1)
                    down(b, n)

            batch(0, first=True)
            with pe.Fori(1, B - 1) as b:
                batch(b)
            batch(B - 1, last=True)
            turn_out(B - 1, 0)
            turn_out(B - 1, 1)


def layer_kernel(nc, x, wq, wk, wv, wo, lq1, lk1, lq2, lk2, router_w, e_bias, w_up, w_down,
                 shared_up, shared_down, out):
    D, S = Shapes(), Tensors()
    kept = {}
    D.B, D.T, D.E = x.shape
    D.HD = lq1.shape[0]
    D.VD = 2 * D.HD
    D.VW = D.VD + 1
    D.KC = D.E // P
    D.TB = D.T // P
    D.SH = 4
    D.ROWS = D.SH * D.HD
    D.G = D.E // D.ROWS
    D.STEPS = D.B * D.G
    D.NE = router_w.shape[0]
    D.NS = shared_up.shape[1] // P
    D.NX = D.NS + D.NE
    D.SCALE = D.HD ** -0.5
    assert D.KC == 2 and D.TB == 4 and D.ROWS == 32 and w_up.shape[2] == P and D.STEPS % 4 == 0 and D.NS == 4 and D.B == 4

    S.x, S.wq, S.wk, S.wv, S.wo, S.lq1, S.lk1, S.lq2, S.lk2 = x, wq, wk, wv, wo, lq1, lk1, lq2, lk2
    S.router_w, S.e_bias, S.w_up, S.w_down = router_w, e_bias, w_up, w_down
    S.shared_up, S.shared_down, S.out = shared_up, shared_down, out
    D.RING = 4
    S.q = nc.dram_tensor("q_halves", [D.STEPS, D.SH, D.HD, 3, D.T], F32R, kind="Internal").ap()
    S.k = nc.dram_tensor("k_halves", [D.STEPS, D.SH, D.HD, 3, D.T], F32R, kind="Internal").ap()
    S.v = nc.dram_tensor("values", [D.STEPS, P, D.TB * 2 * D.VW], F32, kind="Internal").ap()
    S.comb = nc.dram_tensor("comb_rows", [D.NE, D.B * D.T], F32, kind="Internal").ap()

    with ExitStack() as ctx:
        tensor, _, _ = allocator(nc, ctx, kept)
        tensor("attn", [P, D.STEPS, D.TB * 2 * D.VD])
        tensor("ident", [P, P])
        tensor("wo_h", [P, D.KC, D.E], F32R)
        tensor("wo_l", [P, D.KC, D.E], F32R)
        tensor("ffn_h", [P, D.NX, 2 * D.E], F32R)
        tensor("ffn_l", [P, D.NX, 2 * D.E], F32R)
        tensor("eps_col", [P, 1])
        tensor("neg_lam", [P, 1])
        with ExitStack() as attention:
            tensor, _, _ = allocator(nc, attention, kept)
            tensor("k_ring", [P, D.RING, D.T], F32R)
            tensor("q_ring", [P, D.RING, D.SH, D.T], F32R)
            tensor("v_ring", [P, D.RING, D.TB, 2, D.VW])
            tensor("ident_b", [P, P], BF16)
            tensor("mask_b", [P, D.SH, P], BF16)
            tensor("zeros_b", [P, D.T], BF16)
            kept["part_h"], kept["part_l"] = (kept[w][:, 2 * D.KC:, :] for w in ("ffn_h", "ffn_l"))
            tensor("v_stage", [P, D.B, D.G, D.TB, 2, D.VW])
            kept["parts_stored"] = attention.enter_context(nc.semaphore("parts_stored"))
            for name in ("kq_loaded", "v_loaded"):
                kept[name] = [attention.enter_context(nc.semaphore(f"{name}{j}")) for j in range(D.RING)]
            K = named(kept)
            project(nc, D, K, S)
            attend(nc, D, K, S)
        experts(nc, D, K, S)


_INS = ['L0_attn_x', 'L0_attn_Wq', 'L0_attn_Wk', 'L0_attn_Wv', 'L0_attn_Wo', 'L0_attn_lq1', 'L0_attn_lk1',
        'L0_attn_lq2', 'L0_attn_lk2', 'L0_ffn_router_weight', 'L0_ffn_e_bias', 'L0_ffn_w_up',
        'L0_ffn_w_down', 'L0_ffn_shared_up', 'L0_ffn_shared_down']


def kernel(**inputs):
    import numpy as _np
    import concourse.bacc as _bacc
    from concourse import mybir as _mybir
    from concourse.bass_utils import run_bass_kernel_spmd as _run

    nc = _bacc.Bacc("TRN2", target_bir_lowering=False, num_devices=1)
    arrays, args = {}, []
    for name in _INS:
        a = _np.ascontiguousarray(inputs[name])
        arrays[f"in_{name}_dram"] = a
        args.append(nc.dram_tensor(f"in_{name}_dram", a.shape, _mybir.dt.from_np(a.dtype), kind="ExternalInput").ap())
    shape = inputs['L0_attn_x'].shape
    out = nc.dram_tensor("out_0_dram", shape, _mybir.dt.float32, kind="ExternalOutput").ap()
    layer_kernel(nc, *args, out)
    r = _run(nc, [arrays], core_ids=[0])
    return r.results[0]["out_0_dram"]
```

```python
import math
from contextlib import ExitStack
from collections import namedtuple

import concourse.bass as bass
from concourse import mybir

F32 = mybir.dt.float32
F32R = mybir.dt.float32r
BF16 = mybir.dt.bfloat16
ALU = mybir.AluOpType
ACT = mybir.ActivationFunctionType
AX = mybir.AxisListType

P = 128
LAMBDA_INIT = 0.8 - 0.6 * math.exp(-0.3 * 12)
EPS = 1e-5
GROUPS = 4
MASKED = -2.0e38
FAR = -1.0e30


class Shapes:
    pass


class Tensors:
    pass


def named(found):
    return namedtuple("Named", sorted(found))(**found)


def allocator(nc, stack, where, block=""):
    def tensor(name, shape, dt=F32):
        where[name] = stack.enter_context(nc.sbuf_tensor(block + name, list(shape), dt))

    def banks(name, n):
        where[name] = [stack.enter_context(nc.psum_tensor(f"{block}{name}{i}", [P, 512], F32))
                                for i in range(n)]

    def sems(names):
        for name in names.split():
            where[name] = stack.enter_context(nc.semaphore(block + name))
    return tensor, banks, sems


def chained(eng, semaphore, base=0):
    count = [0]

    def link(ins):
        count[0] += 1
        ins.then_inc(semaphore, 1)
        eng.wait_ge(semaphore, base + count[0])
    link.count = count
    return link


def stand(eng, passed):
    eng.sem_inc(passed, 1)


def matmul3(pe, o, w, m, start=True, stop=True):
    pe.matmul(o, w[0], m[1], start=start, stop=False)
    pe.matmul(o, w[1], m[0], start=False, stop=False)
    return pe.matmul(o, w[0], m[0], start=False, stop=stop)


def entries(buf, first, n):
    return buf[:, bass.ds(first, n), :]


def entry(buf, at):
    return entries(buf, at, 1).rearrange("p a s -> p (a s)")


def store_parts(sp, D, K, S, b):
    for m in range(D.KC):
        n = D.G // D.KC
        steps = slice(b * D.G + m * n, b * D.G + (m + 1) * n)
        for dst, at, low in ((S.q, 4 * b + m, 2), (S.k, 4 * b + D.KC + m, 1)):
            sp.dma_start(dst[steps, :, :, low].rearrange("g s r t -> (g s r) t").bitcast(F32),
                         K.part_l[:, at, :].bitcast(F32)).then_inc(K.parts_stored, 16)
            places = slice(0, 2) if low == 2 else slice(0, 3, 2)
            sp.dma_start(dst[steps, :, :, places].rearrange("g s r c t -> (g s r) c t").bitcast(F32),
                         K.part_h[:, at, :].bitcast(F32).unsqueeze(1).to_broadcast([P, 2, D.T])
                         ).then_inc(K.parts_stored, 16)
    sp.dma_start(S.v[b * D.G:(b + 1) * D.G].rearrange("g p w -> p g w"),
                 K.v_stage[:, b].rearrange("p g t h w -> p g (t h w)")).then_inc(K.parts_stored, 16)


PARTS_STORED = (4 * 2 + 1) * 16
STORED_EARLY = 2


def load_kq(sp, D, K, S, i, j):
    rows = 3 * D.HD
    sp.dma_start(K.k_ring[0:3 * D.ROWS, j, :].bitcast(F32),
                 S.k[bass.ds(i, 1)].rearrange("g s r c t -> (g s r c) t").bitcast(F32)
                 ).then_inc(K.kq_loaded[j], 16)
    for s in range(D.SH):
        sp.dma_start(K.q_ring[s * rows:(s + 1) * rows, j, s, :].bitcast(F32),
                     S.q[bass.ds(i, 1), s].rearrange("g r c t -> (g r c) t").bitcast(F32)
                     ).then_inc(K.kq_loaded[j], 16)


def load_v(sp, K, S, i, j):
    sp.dma_start(K.v_ring[:, j].rearrange("p t h w -> p (t h w)"),
                 S.v[bass.ds(i, 1)].rearrange("g p w -> (g p) w")).then_inc(K.v_loaded[j], 16)


STEP_LOADS = 1 + 4


def project(nc, D, K, S):
    B, T, E, TB, KC, G, HD, VD, VW = D.B, D.T, D.E, D.TB, D.KC, D.G, D.HD, D.VD, D.VW
    made = {}
    with ExitStack() as st:
        tensor, banks, sems = allocator(nc, st, made, "project_")
        tensor("w_raw", [P, 4, KC, E])
        tensor("w_h", [P, 3, KC, E], F32R)
        tensor("w_l", [P, 3, KC, E], F32R)
        tensor("x", [P, B * TB, E])
        tensor("xn", [P, TB, E])
        tensor("stats", [P, TB, 6])
        tensor("mv", [P, TB, 2])
        tensor("std", [P, TB])
        tensor("rstd", [P, TB])
        made["xT_h"], made["xT_l"] = K.ffn_h[:, 0:2 * KC, :], K.ffn_l[:, 0:2 * KC, :]
        tensor("table", [P, 1])
        tensor("lam_in", [P, 4, HD])
        tensor("lam_pr", [P, 2, HD])
        banks("ps_t", KC)
        banks("ps_qk", 4)
        banks("ps_v", 2)
        w_loaded = [st.enter_context(nc.semaphore(f"w_loaded{n}")) for n in range(4)]
        x_loaded = [st.enter_context(nc.semaphore(f"x_loaded{n}")) for n in range(TB + B - 1)]
        sems("passed lam_loaded eps_set ident_set ones_set masks_set rings_set w_high w_low table_in dve_step var_ready "
             "std_ready xn_ready xT_turned xTh_ready xTl_ready qk_done v_done ph_ready pl_ready "
             "v_copied")
        M = named(made)
        LN_STEPS = 2 * TB

        block = st.enter_context(nc.Block())

        @block.sync
        def _(sp):
            for b in range(B):
                for t in range(TB) if b == 0 else (None,):
                    tiles = slice(t, t + 1) if b == 0 else slice(b * TB, (b + 1) * TB)
                    sp.dma_start(M.x[:, tiles], S.x.rearrange("b (t p) e -> p (b t) e", p=P)[:, tiles]
                                 ).then_inc(x_loaded[t if b == 0 else TB - 1 + b], 16)

            def store(b):
                sp.wait_ge(M.ph_ready, 4 * b + 4)
                sp.wait_ge(M.pl_ready, 4 * b + 4 + 4)
                sp.wait_ge(M.v_copied, TB * b + TB + 4)
                store_parts(sp, D, K, S, b)

            store(0)
            sp.wait_ge(M.rings_set, 2)
            sp.wait_ge(K.parts_stored, PARTS_STORED)
            for j in range(D.RING):
                load_kq(sp, D, K, S, j, j)
                if j < D.RING - 1:
                    load_v(sp, K, S, j, j)
            for b in range(1, STORED_EARLY):
                store(b)
        @block.scalar
        def _(act):
            weights = [w.rearrange("(c p) n -> p c n", p=P) for w in (S.wq, S.wk, S.wv, S.wo)]
            for n in range(3):
                act.dma_start(M.w_raw[:, n], weights[n]).then_inc(w_loaded[n], 16)
            act.wait_ge(M.eps_set, 1)

            def high(n):
                act.wait_ge(w_loaded[n], 16)
                act.copy(M.w_h[:, n] if n < 3 else K.wo_h[:, :, :], M.w_raw[:, n]).then_inc(M.w_high, 1)

            def spread(b):
                act.wait_ge(M.var_ready, b + 1)
                act.activation(M.std[:, :], M.mv[:, :, 1], ACT.Sqrt, bias=K.eps_col[:, 0:1]
                               ).then_inc(M.std_ready, 1)

            def turned_high(b):
                act.wait_ge(M.xT_turned, b + 2)
                act.wait_ge(M.v_done, b + 1)
                for c in range(KC):
                    act.copy(entry(M.xT_h, KC * (b % 2) + c), M.ps_t[c][:, :]).then_inc(M.xTh_ready, 1)

            def parts_high(b):
                for c in range(4):
                    act.wait_ge(M.qk_done, 4 * b + c + 1)
                    act.activation(entry(K.part_h, 4 * b + c), M.ps_qk[c][:, :], ACT.Copy,
                                   scale=D.SCALE if c < KC else 1.0).then_inc(M.ph_ready, 1)

            def values(b):
                act.wait_ge(M.v_done, b + 3)
                for t in range(TB):
                    act.copy(K.v_stage[:, bass.ds(b, 1), :, t, :, 0:VD].rearrange("p o g h d -> p (o g) h d"),
                             M.ps_v[t // 2][:, (t % 2) * E:(t % 2 + 1) * E].rearrange(
                                 "p (g h d) -> p g h d", g=G, d=VD)).then_inc(M.v_copied, 1)

            act.activation(M.table[:, :], K.eps_col[:, :], ACT.Sqrt).then_inc(M.table_in, 1)
            for n in range(3):
                high(n)
            spread(0)
            act.dma_start(M.w_raw[:, 3], weights[3]).then_inc(w_loaded[3], 16)
            for n, v in enumerate((S.lq1, S.lk1, S.lq2, S.lk2)):
                act.dma_start(M.lam_in[:, n, :], v.partition_broadcast(P)).then_inc(M.lam_loaded, 16)
            act.wait_ge(M.ones_set, 1)
            turned_high(0)
            high(3)
            with act.Fori(0, B - 1) as b:
                spread(b + 1)
                parts_high(b)
                turned_high(b + 1)
                values(b)
            parts_high(B - 1)
            values(B - 1)

        @block.gpsimd
        def _(pool):
            pool.sem_inc(M.v_copied, 4)
            pool.sem_inc(M.v_done, 2)
            pool.sem_inc(M.xT_turned, 1)
            pool.sem_inc(M.xTl_ready, KC)
            pool.sem_inc(M.pl_ready, 4)
            pool.memset(K.eps_col[:, :], EPS).then_inc(M.eps_set, 1)
            pool.memset(K.ident[:, :], 1.0).then_inc(M.ident_set, 1)
            pool.wait_ge(M.ident_set, 1)
            pool.affine_select(out=K.ident[:, :], in_=K.ident[:, :], pattern=[[-1, P]],
                               compare_op=ALU.is_equal, fill=0.0, base=0,
                               channel_multiplier=1).then_inc(M.ident_set, 1)
            def low(n):
                high_half = M.w_h[:, n] if n < 3 else K.wo_h[:, :, :]
                low_half = M.w_l[:, n] if n < 3 else K.wo_l[:, :, :]
                pool.wait_ge(M.w_high, n + 1)
                pool.tensor_tensor(low_half, M.w_raw[:, n], high_half.bitcast(F32),
                                   ALU.subtract).then_inc(M.w_low, 1)

            pool.memset(K.v_stage[:, :, :, :, :, :], 1.0).then_inc(M.ones_set, 1)
            for n in range(3):
                low(n)
            pool.memset(K.zeros_b[:, :], 0.0).then_inc(M.masks_set, 1)
            pool.memset(K.mask_b[:, :, :], MASKED).then_inc(M.masks_set, 1)
            pool.memset(K.ident_b[:, :], 1.0).then_inc(M.masks_set, 1)
            pool.wait_ge(M.masks_set, 3)
            pool.affine_select(out=K.mask_b[:, :, :], in_=K.mask_b[:, :, :], pattern=[[0, 4], [1, P]],
                               compare_op=ALU.is_gt, fill=0.0, base=0,
                               channel_multiplier=-1).then_inc(M.masks_set, 1)
            pool.affine_select(out=K.ident_b[:, :], in_=K.ident_b[:, :], pattern=[[-1, P]],
                               compare_op=ALU.is_equal, fill=0.0, base=0,
                               channel_multiplier=1).then_inc(M.masks_set, 1)
            pool.memset(K.k_ring[:, :, :].bitcast(F32), 1.0).then_inc(M.rings_set, 1)
            pool.memset(K.q_ring[:, :, :, :].bitcast(F32), 0.0).then_inc(M.rings_set, 1)
            low(3)

        @block.vector
        def _(dve):
            def x_tile(b, t):
                return entry(M.x, b * TB + t)

            def norm(b):
                for t in range(TB):
                    if isinstance(b, int) and b == 0:
                        dve.wait_ge(x_loaded[t], 16)
                    dve.bn_stats(M.stats[:, t, :], x_tile(b, t)).then_inc(M.dve_step, 1)
                dve.wait_ge(M.dve_step, LN_STEPS * b + TB)
                stand(dve, M.passed)
                for t in range(TB):
                    dve.bn_aggr(M.mv[:, t, :], M.stats[:, t, :]).then_inc(
                        M.var_ready if t == TB - 1 else M.dve_step, 1)
                dve.wait_ge(M.std_ready, b + 1)
                dve.reciprocal(M.rstd[:, :], M.std[:, :]).then_inc(M.dve_step, 1)
                dve.wait_ge(M.dve_step, LN_STEPS * b + 2 * TB)
                dve.wait_ge(M.xT_turned, b + 1)
                for t in range(TB):
                    dve.tensor_scalar(M.xn[:, t, :], x_tile(b, t), M.mv[:, t, 0:1],
                                      M.rstd[:, t:t + 1], ALU.subtract, ALU.mult).then_inc(M.xn_ready, 1)

            def turned_low(b):
                for c in range(KC):
                    dve.wait_ge(M.xTh_ready, KC * b + c + 1)
                    at = KC * (b % 2) + c
                    dve.tensor_tensor(entry(M.xT_l, at), M.ps_t[c][:, :], entry(M.xT_h, at).bitcast(F32),
                                      ALU.subtract).then_inc(M.xTl_ready, 1)

            def parts_low(b):
                for c in range(4):
                    dve.wait_ge(M.ph_ready, 4 * b + c + 1)
                    dve.scalar_tensor_tensor(entry(K.part_l, 4 * b + c), M.ps_qk[c][:, :],
                                             D.SCALE if c < KC else 1.0,
                                             entry(K.part_h, 4 * b + c).bitcast(F32), ALU.mult,
                                             ALU.subtract).then_inc(M.pl_ready, 1)

            norm(0)
            for b in range(1, B):
                dve.wait_ge(x_loaded[TB - 1 + b], 16)
            turned_low(0)
            with dve.Fori(0, B - 1) as b:
                norm(b + 1)
                parts_low(b)
                turned_low(b + 1)
            parts_low(B - 1)
            link = chained(dve, M.dve_step, LN_STEPS * B)
            dve.wait_ge(M.lam_loaded, 64)
            pairs = M.lam_in[:, :, :].rearrange("p (a two) d -> p a two d", two=2)
            link(dve.tensor_tensor(M.lam_pr[:, :, :], pairs[:, :, 0, :], pairs[:, :, 1, :], ALU.mult))
            dve.tensor_reduce(K.lam_sum[:, :], M.lam_pr[:, :, :], AX.X, ALU.add).then_inc(K.lam_dot, 1)

        @block.tensor
        def _(pe):
            pe.wait_ge(M.ident_set, 2)

            def turn(b):
                pe.wait_ge(M.xTl_ready, KC * b + KC)
                for t in range(TB):
                    pe.wait_ge(M.xn_ready, TB * b + t + 1)
                    for c in range(KC):
                        ins = pe.transpose(M.ps_t[c][:, t * P:(t + 1) * P],
                                           M.xn[:, t, c * P:(c + 1) * P], K.ident[:, :])
                ins.then_inc(M.xT_turned, 1)

            def queries_keys(b, j):
                pe.wait_ge(M.xTl_ready, KC * b + 2 * KC)
                pe.wait_ge(M.pl_ready, 4 * b + 4)
                for part in range(4):
                    n, m = part // KC, part % KC
                    if m == 0:
                        pe.wait_ge(M.w_low, n + 1)
                    for c in range(KC):
                        ins = matmul3(pe, M.ps_qk[part][:, :],
                                      [w[:, n, c, m * P:(m + 1) * P] for w in (M.w_h, M.w_l)],
                                      [x[:, KC * j + c, :] for x in (M.xT_h, M.xT_l)],
                                      start=c == 0, stop=c == KC - 1)
                    ins.then_inc(M.qk_done, 1)

            def values(b, j):
                pe.wait_ge(M.w_low, 3)
                pe.wait_ge(M.v_copied, 4 * b + 4)
                for t in range(TB):
                    for c in range(KC):
                        ins = matmul3(pe, M.ps_v[t // 2][:, (t % 2) * E:(t % 2 + 1) * E],
                                      [x[:, KC * j + c, t * P:(t + 1) * P] for x in (M.xT_h, M.xT_l)],
                                      [w[:, 2, c, :] for w in (M.w_h, M.w_l)],
                                      start=c == 0, stop=c == KC - 1)
                ins.then_inc(M.v_done, 1)

            def pair(b, last=False):
                for j in range(2):
                    queries_keys(b + j, j)
                    if not (last and j == 1):
                        turn(b + j + 1)
                    values(b + j, j)

            turn(0)
            with pe.Fori(0, B // 2 - 1) as r:
                pair(2 * r)
            pair(B - 2, last=True)


def mix_tensors(D, tensor):
    H = D.G * 2 * D.TB
    tensor("square", [P, H, D.VD])
    tensor("mean_sq", [P, H])
    tensor("head_std", [P, H])
    tensor("head_rstd", [P, H])
    tensor("normed", [P, D.TB, D.E])
    tensor("stats", [P, D.TB, 6])
    tensor("mv", [P, D.TB, 2])
    tensor("std", [P, D.TB])
    tensor("rstd", [P, D.TB])


def heads_T(K, low, c):
    return K.q_ring[:, 0, 2 * low + c, :]


def rows_T(K, b, low, c):
    return K.q_ring[:, bass.ds(1 + b % 2, 1), 2 * low + c, :].rearrange("p o t -> p (o t)")


def tiles_of(D, halves):
    return [t for h in halves for t in range(h * D.TB // 2, (h + 1) * D.TB // 2)]


def square(pool, D, K, M, b, halves=(0, 1)):
    n = D.G // 2
    for h in halves:
        heads = entries(K.attn, b * D.G + h * n, n).rearrange("p g (x d) -> p (g x) d", d=D.VD)
        x = M.square.shape[1] // 2
        pool.tensor_tensor(M.square[:, h * x:(h + 1) * x, :], heads, heads, ALU.mult).then_inc(K.squared, 1)


def head_spread(act, D, K, M, b):
    act.wait_ge(K.mean_ready, b + 1)
    act.activation(M.head_std[:, :], M.mean_sq[:, :], ACT.Sqrt, bias=K.eps_col[:, 0:1],
                   scale=1.0 / D.VD).then_inc(K.head_std_ready, 1)


def heads_high(act, D, K, M, b):
    act.wait_ge(K.heads_turned, b + 1)
    for c in range(D.KC):
        act.copy(heads_T(K, 0, c), M.ps_t[c][:, :]).then_inc(K.aTh_ready, 1)


def spread(act, D, K, M, b):
    act.wait_ge(K.var_ready, b + 1)
    act.activation(M.std[:, :], M.mv[:, :, 1], ACT.Sqrt, bias=K.eps_col[:, 0:1]
                   ).then_inc(K.std_ready, 1)


def rows_high(act, D, K, M, b):
    act.wait_ge(K.rows_turned, b + 2)
    for c in range(D.KC):
        act.copy(rows_T(K, b, 0, c), M.ps_t[c][:, :]).then_inc(K.xTh_ready, 1)


def mean_square(dve, D, K, M, b):
    dve.wait_ge(K.squared, 2 * b + 2)
    dve.tensor_reduce(M.mean_sq[:, :], M.square[:, :, :], AX.X, ALU.add).then_inc(K.mean_ready, 1)


def head_scale(dve, D, K, M, b):
    link = chained(dve, K.dve_step, D.MIX_STEPS * b)
    dve.wait_ge(K.head_std_ready, b + 1)
    link(dve.reciprocal(M.head_rstd[:, :], M.head_std[:, :]))
    link(dve.tensor_scalar(M.head_rstd[:, :], M.head_rstd[:, :], 1.0 - LAMBDA_INIT, None, ALU.mult))


def norm_heads(dve, D, K, M, b, halves=(0, 1)):
    if 0 in halves:
        dve.wait_ge(K.rows_turned, b + 1)
    heads = entries(K.attn, b * D.G, D.G).rearrange("p g (t h d) -> p g t h d", t=D.TB, d=D.VD)
    scale = M.head_rstd[:, :].rearrange("p (g t h) -> p g t h", t=D.TB, h=2)
    for t in tiles_of(D, halves):
        dve.tensor_tensor(M.normed[:, t, :].rearrange("p (g h d) -> p g h d", g=D.G, d=D.VD),
                          heads[:, :, t], scale[:, :, t].unsqueeze(3).to_broadcast([P, D.G, 2, D.VD]),
                          ALU.mult).then_inc(K.heads_normed, 1)


def heads_low(dve, D, K, M, b, halves=(0, 1)):
    for c in halves:
        dve.wait_ge(K.aTh_ready, D.KC * b + c + 1)
        dve.tensor_tensor(heads_T(K, 1, c), M.ps_t[c][:, :], heads_T(K, 0, c).bitcast(F32),
                          ALU.subtract).then_inc(K.aTl_ready, 1)


def add_rows(dve, D, K, M, b, halves=(0, 1)):
    dve.wait_ge(K.x_loaded, 16 * b + 16)
    dve.wait_ge(K.projected, b + 1)
    for pair in halves:
        rows = entries(K.x_sb, b * D.TB + 2 * pair, 2).rearrange("p t e -> p (t e)")
        dve.tensor_tensor(rows, rows, M.ps_x[pair][:, :], ALU.add).then_inc(K.dve_step, 1)


def row_stats(dve, D, K, M, b, halves=(0, 1)):
    base = D.MIX_STEPS * b + 2
    if 0 in halves:
        dve.wait_ge(K.dve_step, base + 2)
        stand(dve, M.passed)
    for t in tiles_of(D, halves):
        dve.bn_stats(M.stats[:, t, :], entry(K.x_sb, b * D.TB + t)).then_inc(K.dve_step, 1)
    if 1 not in halves:
        return
    dve.wait_ge(K.dve_step, base + 2 + D.TB)
    stand(dve, M.passed)
    for t in range(D.TB):
        dve.bn_aggr(M.mv[:, t, :], M.stats[:, t, :]).then_inc(
            K.var_ready if t == D.TB - 1 else K.dve_step, 1)


def norm_rows(dve, D, K, M, b, halves=(0, 1)):
    if 0 in halves:
        dve.wait_ge(K.std_ready, b + 1)
        dve.reciprocal(M.rstd[:, :], M.std[:, :]).then_inc(K.dve_step, 1)
        dve.wait_ge(K.dve_step, D.MIX_STEPS * b + 4 + 2 * D.TB)
        dve.wait_ge(K.heads_turned, b + 1)
    for t in tiles_of(D, halves):
        dve.tensor_scalar(M.normed[:, t, :], entry(K.x_sb, b * D.TB + t), M.mv[:, t, 0:1],
                          M.rstd[:, t:t + 1], ALU.subtract, ALU.mult).then_inc(K.rows_normed, 1)


def rows_low(dve, D, K, M, b, halves=(0, 1)):
    for c in halves:
        dve.wait_ge(K.xTh_ready, D.KC * b + c + 1)
        dve.tensor_tensor(rows_T(K, b, 1, c), M.ps_t[c][:, :], rows_T(K, b, 0, c).bitcast(F32),
                          ALU.subtract).then_inc(K.xTl_ready, 1)


def turn_heads(pe, D, K, M, b):
    pe.wait_ge(K.heads_normed, D.TB * b + D.TB)
    pe.wait_ge(K.y_ready, 2 * b + 2)
    turn(pe, D, K, M, K.heads_turned)


def turn_rows(pe, D, K, M, b):
    pe.wait_ge(K.rows_normed, D.TB * b + D.TB)
    turn(pe, D, K, M, K.rows_turned)


def turn(pe, D, K, M, semaphore):
    for c in range(D.KC):
        for t in range(D.TB):
            ins = pe.transpose(M.ps_t[c][:, t * P:(t + 1) * P],
                               M.normed[:, t, c * P:(c + 1) * P], K.ident[:, :])
    ins.then_inc(semaphore, 1)


def project_heads(pe, D, K, M, b):
    pe.wait_ge(K.aTl_ready, D.KC * b + D.KC)
    pe.wait_ge(K.comb_copied, b + 1)
    for t in range(D.TB):
        for c in range(D.KC):
            ins = matmul3(pe, M.ps_x[t // 2][:, (t % 2) * D.E:(t % 2 + 1) * D.E],
                          [heads_T(K, low, c)[:, t * P:(t + 1) * P] for low in range(2)],
                          [w[:, c, :] for w in (K.wo_h, K.wo_l)],
                          start=c == 0, stop=c == D.KC - 1)
    ins.then_inc(K.projected, 1)


def attend(nc, D, K, S):
    T, TB, VD, VW, SH, ROWS, HD, STEPS = D.T, D.TB, D.VD, D.VW, D.SH, D.ROWS, D.HD, D.STEPS
    RING, E, KC, NS, NX = D.RING, D.E, D.KC, D.NS, D.NX
    ROUNDS = STEPS // RING
    made = {}
    with ExitStack() as st:
        tensor, banks, sems = allocator(nc, st, made, "attend_")
        tensor("weights", [P, 2, 2 * E])
        tensor("m_rows", [2 * SH, 2, T], F32R)
        tensor("probs", [P, 5, 2, 512])
        tensor("pv_copy", [P, T])
        tensor("sums_pv", [P, 2, TB, SH, VW])
        tensor("recip", [P, 2, TB, 2, 2])
        tensor("first", [P, TB, 2, VD])
        tensor("second", [P, TB, 2, VD])
        tensor("lam_exp", [P, 2])
        tensor("neg_max", [P, TB, SH])
        tensor("neg_max2", [P, TB, 2, SH], F32R)
        made["ps_s"] = st.enter_context(nc.psum_tensor("ps_s", [P, 2, 2, 512], F32))
        banks("ps_m", 2)
        made["ps_t"] = made["ps_x"] = made["ps_m"]
        banks("ps_pv", 1)
        banks("ps_turn", 1)
        mix_tensors(D, tensor)
        weights_loaded = [st.enter_context(nc.semaphore(f"weights_loaded{j}")) for j in range(2)]
        m_loaded = [st.enter_context(nc.semaphore(f"m_loaded{j}")) for j in range(RING)]
        sems("passed lam_exped lam_step pv_zeroed s_filled exp_done max_filled max_read max_step max_halves m_turned "
             "m_copied weights_high weights_low cut_done pv_stage pv_copied out_turned acc_stored recip_step recip_ready parts_ready mixed")
        M = named(made)

        def chunk(u):
            if u < 2:
                return [(n, 2 * u + n, 0, 0) for n in range(2)]
            if u < 4:
                return [(n, 2 * (u - 2) + n, kb, col) for n in range(2) for kb, col in ((1, 0), (3, 384))]
            return [(s // 2, s, 2, 256 * (s % 2)) for s in range(SH)]

        CHUNKS = 5
        WEIGHT_ROUNDS = NX // RING
        FILLS = [(3, [s]) for s in range(SH)] + [(2, [s]) for s in range(SH)] + [(1, [0, 1]), (1, [2, 3])] \
            + [(0, list(range(SH)))]
        NF = len(FILLS)

        block = st.enter_context(nc.Block())

        @block.sync
        def _(sp):
            def load_weights(n, j):
                sp.wait_ge(M.weights_low, n + 1)
                up, down = M.weights[:, j % 2, 0:E], M.weights[:, j % 2, E:2 * E]
                if isinstance(n, int):
                    sources = S.shared_up[:, n * P:(n + 1) * P], S.shared_down[n * P:(n + 1) * P, :]
                else:
                    e = bass.ds(n - NS, 1)
                    sources = (S.w_up[e].rearrange("o a i -> (o a) i"), S.w_down[e].rearrange("o i e -> (o i) e"))
                sp.dma_start(up.rearrange("p (c i) -> p c i", c=KC), sources[0].rearrange("(c p) i -> p c i", p=P)
                             ).then_inc(weights_loaded[j % 2], 16)
                sp.dma_start(down, sources[1]).then_inc(weights_loaded[j % 2], 16)

            def load_max(i, j):
                sp.wait_ge(M.m_copied, i + 1)
                for s in range(SH):
                    sp.dma_start(K.q_ring[3 * ROWS:3 * ROWS + 2, j, s, :].bitcast(F32),
                                 M.m_rows[s::SH, j % 2, :].bitcast(F32)).then_inc(m_loaded[j], 16)

            load_max(0, 0)
            sp.dma_start(K.rw_raw[:, :], S.router_w).then_inc(K.router_loaded, 16)
            sp.dma_start(K.bias[:, :], S.e_bias.partition_broadcast(P)).then_inc(K.router_loaded, 16)

            def step(i, j, last=False, weights=True):
                if not (last and j > 0):
                    sp.wait_ge(M.pv_stage, 3 * i + 3)
                    load_v(sp, K, S, i + RING - 1, (j - 1) % RING)
                if not (last and j == RING - 1):
                    load_max(i + 1, (j + 1) % RING)
                if weights:
                    load_weights(i, j)
                if not last:
                    sp.wait_ge(M.s_filled, CHUNKS * i + CHUNKS)
                    load_kq(sp, D, K, S, i + RING, j)

            for j in range(RING):
                step(j, j)
                if j + 1 < D.B - STORED_EARLY + 1:
                    store_parts(sp, D, K, S, STORED_EARLY + j)
            sp.wait_ge(K.parts_stored, PARTS_STORED * D.B)
            with sp.Fori(1, WEIGHT_ROUNDS) as r:
                for j in range(RING):
                    step(r * RING + j, j)
            with sp.Fori(WEIGHT_ROUNDS, ROUNDS - 1) as r:
                for j in range(RING):
                    step(r * RING + j, j, weights=False)
            for j in range(RING):
                step(STEPS - RING + j, j, last=True, weights=False)
                if j:
                    sp.wait_ge(K.x_loaded, 16 * j)
                sp.dma_start(K.x_sb[:, j * TB:(j + 1) * TB, :], S.x[j].rearrange("(t p) e -> p t e", p=P)
                             ).then_inc(K.x_loaded, 16)

        @block.gpsimd
        def _(pool):
            pool.sem_inc(M.weights_low, 2)
            pool.sem_inc(K.y_ready, 4)
            pool.sem_inc(K.comb_copied, 1)
            pool.sem_inc(K.rows_turned, 1)
            def split_low(n, j):
                at = entry(K.ffn_h, n), entry(K.ffn_l, n)
                pool.wait_ge(M.weights_high, n + 1)
                pool.tensor_tensor(at[1], M.weights[:, j % 2, :], at[0].bitcast(F32), ALU.subtract
                                   ).then_inc(M.weights_low, 1)

            def cut(view):
                pool.affine_select(out=view, in_=view, pattern=[[0, SH], [1, P]], compare_op=ALU.is_ge,
                                   fill=0.0, base=0, channel_multiplier=-1).then_inc(M.cut_done, 1)

            def mix(i, j):
                pool.wait_ge(M.recip_ready, i + 1)
                pool.wait_ge(M.mixed, i + 2)
                pv = M.sums_pv[:, j % 2].rearrange("p t (h two) w -> p t h two w", two=2)
                for n, o in enumerate((M.first, M.second)):
                    pool.tensor_tensor(o[:, :, :, :], pv[:, :, :, n, 0:VD],
                                       M.recip[:, j % 2, :, :, n].unsqueeze(3).to_broadcast([P, TB, 2, VD]),
                                       ALU.mult).then_inc(M.parts_ready, 1)
                pool.wait_ge(M.parts_ready, 2 * i + 2)
                pool.tensor_tensor(entry(K.attn, i), M.first[:, :, :, :].rearrange("p t h d -> p (t h d)"),
                                   M.second[:, :, :, :].rearrange("p t h d -> p (t h d)"), ALU.add
                                   ).then_inc(M.mixed, 1)

            def step(i, j, first=False, weights=True):
                pool.wait_ge(M.exp_done, CHUNKS * i + 2 + 2)
                stand(pool, M.passed)
                cut(M.probs[:, 0:2].rearrange("p u n q -> p (u n) q")[:, :, 0:P])
                pool.wait_ge(M.exp_done, CHUNKS * i + 4 + 2)
                stand(pool, M.passed)
                tiles = M.probs[:, 2:4].rearrange("p u n q -> p (u n) q")
                cut(tiles[:, :, 0:P])
                cut(tiles[:, :, T - P:T])
                pool.wait_ge(M.exp_done, CHUNKS * i + 5 + 2)
                stand(pool, M.passed)
                halves = M.probs[:, 4].rearrange("p n (a q) -> p (n a) q", a=2)
                cut(halves[:, :, 0:P])
                if not first:
                    mix(i - 1, (j - 1) % RING)
                if weights:
                    split_low(i, j)

            for j in range(RING):
                step(j, j, first=j == 0)
            with pool.Fori(1, WEIGHT_ROUNDS) as r:
                for j in range(RING):
                    step(r * RING + j, j)
            with pool.Fori(WEIGHT_ROUNDS, ROUNDS - 1) as r:
                for j in range(RING):
                    step(r * RING + j, j, weights=False)
            for j in range(RING):
                step(STEPS - RING + j, j, weights=False)
                if j == 0:
                    square(pool, D, K, M, 0)
            mix(STEPS - 1, RING - 1)

        @block.scalar
        def _(act):
            act.sem_inc(M.exp_done, 2)
            act.sem_inc(M.pv_copied, 1)
            act.sem_inc(M.out_turned, 1)
            act.sem_inc(M.pv_stage, 3)

            def exp(i, u, parity):
                act.wait_ge(M.s_filled, CHUNKS * i + u + 1)
                act.wait_ge(M.pv_stage, 3 * i + u // 2 + 1)
                act.activation(M.probs[:, u], M.ps_s[:, parity], ACT.Exp).then_inc(M.exp_done, 1)

            def copy_max(i, j):
                act.wait_ge(M.m_turned, i + 1)
                act.copy(M.m_rows[:, j % 2, :], M.ps_turn[0][0:2 * SH, :]).then_inc(M.m_copied, 1)

            def copy_pv(i):
                act.wait_ge(M.pv_stage, 3 * i + 3 + 3)
                act.wait_ge(M.out_turned, i + 1)
                act.copy(M.pv_copy[:, :], M.ps_pv[0][:, :]).then_inc(M.pv_copied, 1)

            def split_high(n, j):
                turn = n // 2 if isinstance(n, int) else r_turns[0] * (RING // 2) + j // 2
                act.wait_ge(weights_loaded[j % 2], 32 * (turn + 1))
                act.copy(entry(K.ffn_h, n), M.weights[:, j % 2, :]).then_inc(M.weights_high, 1)

            def step(i, j, first=False, last=False, weights=True):
                exp(i, 0, (CHUNKS * j) % 2)
                if not first:
                    copy_pv(i - 1)
                if not (last and j == RING - 1):
                    copy_max(i + 1, (j + 1) % RING)
                exp(i, 1, (CHUNKS * j + 1) % 2)
                for u in range(2, CHUNKS):
                    exp(i, u, (CHUNKS * j + u) % 2)
                    if last and j == 1 and u == 3:
                        head_spread(act, D, K, M, 0)
                    if last and j == 2 and u == 3:
                        heads_high(act, D, K, M, 0)
                if weights:
                    split_high(i, j)
                if last and j == 3:
                    spread(act, D, K, M, 0)

            act.wait_ge(K.lam_dot, 1)
            act.activation(M.lam_exp[:, :], K.lam_sum[:, :], ACT.Exp).then_inc(M.lam_exped, 1)
            r_turns = [0]
            copy_max(0, 0)
            for j in range(RING):
                step(j, j, first=j == 0)
            with act.Fori(1, WEIGHT_ROUNDS) as r:
                r_turns[0] = r
                for j in range(RING):
                    step(r * RING + j, j)
            with act.Fori(WEIGHT_ROUNDS, ROUNDS - 1) as r:
                for j in range(RING):
                    step(r * RING + j, j, weights=False)
            for j in range(RING):
                step(STEPS - RING + j, j, last=True, weights=False)
            copy_pv(STEPS - 1)
            rows_high(act, D, K, M, 0)

        @block.vector
        def _(dve):
            dve.sem_inc(M.max_read, 2)
            dve.sem_inc(M.acc_stored, 2)
            dve.sem_inc(M.mixed, 2)

            def reduce(i, j, f, first=False):
                tile, heads = FILLS[f]
                if f == 0 and not first:
                    dve.wait_ge(M.max_halves, i)
                dve.wait_ge(M.max_filled, NF * i + f + 1)
                dve.tensor_reduce(M.neg_max[:, tile, heads[0]:heads[-1] + 1],
                                  M.ps_m[(NF * j + f) % 2][:, 0:len(heads) * (tile + 1) * P]
                                  .rearrange("p (s k) -> p s k", s=len(heads)),
                                  AX.X, ALU.max, negate=True).then_inc(M.max_read, 1)

            def halves(i, first=False):
                dve.wait_ge(M.max_read, NF * i + NF + 2)
                if not first:
                    dve.wait_ge(M.m_turned, i)
                dve.tensor_copy(M.neg_max2[:, :, 0, :], M.neg_max[:, :, :]).then_inc(M.max_step, 1)
                dve.wait_ge(M.max_step, i + 1)
                dve.tensor_tensor(M.neg_max2[:, :, 1, :], M.neg_max[:, :, :],
                                  M.neg_max2[:, :, 0, :].bitcast(F32), ALU.subtract
                                  ).then_inc(M.max_halves, 1)

            def store(i, j):
                dve.wait_ge(M.out_turned, i + 2)
                dve.wait_ge(M.mixed, i + 1)
                dve.tensor_copy(
                    M.sums_pv[:, j % 2],
                    M.ps_turn[0][:, :].rearrange("p (t s w) -> p t s w", t=TB, s=SH)[:, :, :, 0:VW]
                ).then_inc(M.acc_stored, 1)
                dve.wait_ge(M.acc_stored, i + 3)
                r = M.recip[:, j % 2]
                dve.reciprocal(r.rearrange("p t h two -> p t (h two)"), M.sums_pv[:, j % 2, :, :, VD]
                               ).then_inc(M.recip_step, 1)
                dve.wait_ge(M.recip_step, i + 1)
                odd = r.rearrange("p t h two -> p (t h) two")[:, :, 1]
                dve.tensor_scalar(odd, odd, K.neg_lam[:, 0:1], None, ALU.mult).then_inc(M.recip_ready, 1)

            def step(i, j, first=False, last=False):
                ahead = not (last and j >= RING - 2)
                if last and j == 1:
                    mean_square(dve, D, K, M, 0)
                if last and j == 2:
                    head_scale(dve, D, K, M, 0)
                    norm_heads(dve, D, K, M, 0)
                for f in range(NF):
                    if ahead:
                        reduce(i + 2, (j + 2) % RING, f)
                    if f == 3 and not first:
                        store(i - 1, (j - 1) % RING)
                if ahead:
                    halves(i + 2)
                if last and j == 2:
                    heads_low(dve, D, K, M, 0)
                if last and j == 3:
                    add_rows(dve, D, K, M, 0)
                    row_stats(dve, D, K, M, 0)
                    norm_rows(dve, D, K, M, 0)

            for i in range(2):
                for f in range(NF):
                    reduce(i, i, f, first=i == 0)
                halves(i, first=i == 0)
            link = chained(dve, M.lam_step)
            dve.wait_ge(M.lam_exped, 1)
            link(dve.tensor_tensor(K.neg_lam[:, :], M.lam_exp[:, 1:2], M.lam_exp[:, 0:1], ALU.subtract))
            link(dve.tensor_scalar(K.neg_lam[:, :], K.neg_lam[:, :], -LAMBDA_INIT, None, ALU.add))
            for j in range(RING):
                step(j, j, first=j == 0)
            with dve.Fori(1, ROUNDS - 1) as r:
                for j in range(RING):
                    step(r * RING + j, j)
            for j in range(RING):
                step(STEPS - RING + j, j, last=True)
            store(STEPS - 1, RING - 1)
            rows_low(dve, D, K, M, 0)

        @block.tensor
        def _(pe):
            rounds = [0]
            pe.matmul(M.ps_pv[0][:, :], K.ident_b[:, :], K.zeros_b[:, :], start=True, stop=True
                      ).then_inc(M.pv_zeroed, 1)

            def scores(i, j, u):
                parity = (CHUNKS * j + u) % 2
                if u == 0:
                    pe.wait_ge(m_loaded[j], 16 * SH * (rounds[0] + 1))
                pe.wait_ge(M.exp_done, CHUNKS * i + u + 1)
                for n, s, kb, col in chunk(u):
                    q0 = kb * P
                    ins = pe.matmul(M.ps_s[:, parity, n, col:col + T - q0],
                                    K.k_ring[:, j, q0:q0 + P], K.q_ring[:, j, s, q0:T],
                                    start=True, stop=True)
                ins.then_inc(M.s_filled, 1)

            def maxima(i, j, f):
                tile, heads = FILLS[f]
                ps = M.ps_m[(NF * j + f) % 2]
                n_k = (tile + 1) * P
                pe.wait_ge(M.max_read, NF * i + f + 1)
                for n, s in enumerate(heads):
                    pe.matmul(ps[:, n * n_k:(n + 1) * n_k],
                              K.q_ring[0:3 * ROWS, j, s, tile * P:(tile + 1) * P],
                              K.k_ring[0:3 * ROWS, j, 0:n_k], start=n == 0, stop=False)
                diagonal = ps[:, 0:len(heads) * n_k].rearrange("p (s k) -> p s k", s=len(heads))
                pe.matmul(diagonal[:, :, n_k - P:n_k], K.ident_b[:, :], K.mask_b[:, 0:len(heads), :],
                          start=False, stop=True).then_inc(M.max_filled, 1)

            def turn_max(i):
                pe.wait_ge(M.max_halves, i + 1)
                for t in range(TB):
                    ins = pe.transpose(M.ps_turn[0][0:2 * SH, t * P:(t + 1) * P],
                                       M.neg_max2[:, t].bitcast(F32).rearrange("p h s -> p (h s)"),
                                       K.ident[:, :])
                ins.then_inc(M.m_turned, 1)

            def pv(i, j, stage, tiles=None):
                pe.wait_ge(M.cut_done, 4 * i + (1, 3, 4)[stage])
                if stage == 0:
                    pe.wait_ge(K.v_loaded[j], 16 * (rounds[0] + 1))
                    pe.wait_ge(M.pv_copied, i + 1)
                for kb in tiles or ((0,), (1, 3), (2,))[stage]:
                    for s in range(SH):
                        u = {0: s // 2, 1: 2 + s // 2, 2: 4, 3: 2 + s // 2}[kb]
                        n, _, _, col = [c for c in chunk(u) if c[1] == s and c[2] == kb][0]
                        ins = pe.matmul(M.ps_pv[0][32 * s:32 * s + VW, kb * P:T],
                                        K.v_ring[:, j, kb, s // 2, :],
                                        M.probs[:, u, n, col:col + T - kb * P],
                                        start=kb == 0, stop=kb == 2)
                if kb != 1:
                    ins.then_inc(M.pv_stage, 1)

            def turn_out(i):
                pe.wait_ge(M.pv_copied, i + 2)
                for t in range(TB):
                    ins = pe.transpose(M.ps_turn[0][:, t * P:(t + 1) * P],
                                       M.pv_copy[:, t * P:(t + 1) * P], K.ident[:, :])
                ins.then_inc(M.out_turned, 1)

            def step(i, j, first=False, last=False):
                ahead = not (last and j >= RING - 2)
                if ahead:
                    pe.wait_ge(K.kq_loaded[(j + 2) % RING], 16 * STEP_LOADS * (rounds[0] + (j + 2) // RING + 1))

                def more(*fills):
                    if ahead:
                        for f in fills:
                            maxima(i + 2, (j + 2) % RING, f)
                scores(i, j, 0)
                more(0)
                if not first:
                    pv(i - 1, (j - 1) % RING, 2)
                more(1)
                if not (last and j == RING - 1):
                    pe.wait_ge(M.m_copied, i + 1)
                    pe.wait_ge(M.acc_stored, i + 1)
                    turn_max(i + 1)
                scores(i, j, 1)
                more(2)
                scores(i, j, 2)
                if not first:
                    if not (last and j == RING - 1):
                        pe.wait_ge(M.m_copied, i + 2)
                    pe.wait_ge(M.acc_stored, i + 1)
                    turn_out(i - 1)
                more(3)
                if last and j == 2:
                    pe.wait_ge(M.max_read, NF * STEPS + 2)
                    turn_heads(pe, D, K, M, 0)
                scores(i, j, 3)
                more(4)
                pv(i, j, 0)
                more(5)
                scores(i, j, 4)
                more(6)
                more(7)
                pv(i, j, 1, (1,))
                more(8)
                pv(i, j, 1, (3,))
                more(9, 10)
                if last and j == 2:
                    project_heads(pe, D, K, M, 0)

            for i in range(2):
                pe.wait_ge(K.kq_loaded[i], 16 * STEP_LOADS)
                for f in range(NF):
                    maxima(i, i, f)
                    if i == 1 and f == 1:
                        turn_max(0)
            for j in range(RING):
                step(j, j, first=j == 0)
            with pe.Fori(1, ROUNDS - 1) as r:
                rounds[0] = r
                for j in range(RING):
                    step(r * RING + j, j)
            rounds[0] = ROUNDS - 1
            for j in range(RING):
                step(STEPS - RING + j, j, last=True)
            pv(STEPS - 1, RING - 1, 2)
            turn_rows(pe, D, K, M, 0)
            pe.wait_ge(M.acc_stored, STEPS - 1 + 2)
            turn_out(STEPS - 1)


def experts(nc, D, K, S):
    B, T, E, TB, KC, G, VD, NE, NX, NS = D.B, D.T, D.E, D.TB, D.KC, D.G, D.VD, D.NE, D.NX, D.NS
    GS = NE // GROUPS
    made = {}
    with ExitStack() as st:
        tensor, banks, sems = allocator(nc, st, made, "experts_")
        mix_tensors(D, tensor)
        tensor("rw_h", [P, KC, P], F32R)
        tensor("rw_l", [P, KC, P], F32R)
        tensor("logitsT", [NE, T])
        tensor("combT", [NE, T])
        tensor("score", [P, TB, NE])
        tensor("biased", [P, TB, NE])
        tensor("pair_sums", [P, TB * GROUPS, 6])
        tensor("group_score", [P, TB, GROUPS])
        tensor("group_mask", [P, TB, GROUPS])
        tensor("top_val", [P, TB])
        tensor("top_key", [P, TB, NE])
        tensor("first_hot", [P, TB, NE])
        tensor("second_hot", [P, TB, NE])
        tensor("order", [P, NE])
        tensor("comb", [P, TB, NE])
        tensor("relu", [P, 2, T])
        tensor("act", [P, 2, T])
        made["act_h"], made["act_l"] = K.k_ring[:, 0:2, :], K.k_ring[:, 2:4, :]
        tensor("weight", [P, 4, T])
        tensor("outT", [P, KC, T])
        tensor("y", [P, 2, 2, E])
        banks("ps_h", 2)
        banks("ps_o", KC)
        banks("ps_t", 2)
        banks("ps_x", 2)
        weight_loaded = [st.enter_context(nc.semaphore(f"weight_loaded{j}")) for j in range(4)]
        sems("passed order_set rw_turned rw_high rw_low rw_zeroed "
             "logits_done logits_copied logits_turned scored comb_ready comb_turned comb_stored "
             "up_done relu_done weighted act_done high_done low_done down_done out_copied out_turned y_stored")
        M = named(made)

        def later(what, b, n, last):
            if n < NX:
                what(b, n)
            elif not last:
                what(b + 1, n - NX)

        def activate(eng, b, n):
            k = NX * b + n
            if n < NS:
                eng.wait_ge(M.relu_done, k + 1 + 2)
                eng.wait_ge(M.low_done, k + 1)
                left = M.relu[:, n % 2, :]
            else:
                eng.wait_ge(M.weighted, NE * b + n - NS + 1 + 4)
                left = M.act[:, n % 2, :]
            eng.tensor_tensor(M.act[:, n % 2, :], left, M.relu[:, n % 2, :], ALU.mult
                              ).then_inc(M.act_done, 1)

        def low(eng, b, n):
            k = NX * b + n
            eng.wait_ge(M.high_done, k + 1 + 2)
            eng.wait_ge(M.down_done, k + 1)
            eng.tensor_tensor(M.act_l[:, n % 2, :], M.act[:, n % 2, :], M.act_h[:, n % 2, :].bitcast(F32),
                              ALU.subtract).then_inc(M.low_done, 1)

        block = st.enter_context(nc.Block())

        @block.sync
        def _(sp):
            def store_comb(b):
                sp.wait_ge(K.comb_copied, b + 2)
                sp.dma_start(S.comb[:, bass.ds(b * T, T)], M.combT[:, :]).then_inc(M.comb_stored, 16)
                sp.wait_ge(M.comb_stored, 16 * b + 32)
                stand(sp, M.passed)

            def load_weight(b, e):
                sp.wait_ge(M.weighted, NE * b + e + 1)
                sp.dma_start(M.weight[:, e % 4, :],
                             S.comb[e:e + 1, bass.ds(b * T, T)].rearrange("o t -> (o t)").partition_broadcast(P)
                             ).then_inc(weight_loaded[e % 4], 16)

            def store_out(b, pair):
                sp.wait_ge(K.y_ready, 2 * b + pair + 1 + 4)
                sp.dma_start(S.out.rearrange("b (t p) e -> p (b t) e", p=P)[:, bass.ds(b * TB + 2 * pair, 2), :],
                             M.y[:, pair]).then_inc(M.y_stored, 16)

            store_comb(0)

            def batch(b, first=False, last=False):
                for e in range(NE):
                    load_weight(b, e)
                    if e == 4 and not first:
                        store_out(b - 1, 0)
                        store_out(b - 1, 1)
                if not last:
                    store_comb(b + 1)

            batch(0, first=True)
            with sp.Fori(1, B - 1) as b:
                batch(b)
            batch(B - 1, last=True)
            store_out(B - 1, 0)
            store_out(B - 1, 1)
            sp.wait_ge(M.y_stored, 16 * 2 * B + 16)

        @block.gpsimd
        def _(pool):
            pool.sem_inc(M.weighted, 4)
            pool.sem_inc(M.y_stored, 16)
            pool.sem_inc(M.comb_turned, 1)
            pool.sem_inc(M.comb_stored, 16)
            pool.sem_inc(M.relu_done, 2)
            pool.sem_inc(M.out_copied, KC)

            def weigh(b, n):
                e = n - NS
                k = NX * b + n
                pool.wait_ge(M.relu_done, k + 1 + 2)
                pool.wait_ge(weight_loaded[e % 4], 16 * ((NE // 4) * b + e // 4 + 1))
                pool.wait_ge(M.low_done, k + 1)
                pool.tensor_tensor(M.act[:, n % 2, :], M.relu[:, n % 2, :], M.weight[:, e % 4, :],
                                   ALU.mult).then_inc(M.weighted, 1)

            pool.memset(M.rw_h[:, :, :].bitcast(F32), 0.0).then_inc(M.rw_zeroed, 1)
            pool.memset(M.rw_l[:, :, :].bitcast(F32), 0.0).then_inc(M.rw_zeroed, 1)
            for e in range(NE):
                pool.memset(M.order[:, e:e + 1], float(NE - e)).then_inc(M.order_set, 1)
            def next_square(b, half):
                pool.wait_ge(K.mean_ready, b + 1)
                square(pool, D, K, M, b + 1, halves=(half,))

            def shared(b):
                activate(pool, b, 0)
                for n in range(NS):
                    if n + 1 < NS:
                        activate(pool, b, n + 1)
                    low(pool, b, n)
                    if n < 2:
                        next_square(b, n)

            def batch(b, first=False, last=False):
                if first:
                    shared(b)
                else:
                    for n in range(NS):
                        if n < 2 and not last:
                            next_square(b, n)
                        if n == 0:
                            pool.wait_ge(M.act_done, NX * b + 2)
                        activate(pool, b, n)
                for n in range(NS, NX):
                    weigh(b, n)

            batch(0, first=True)
            with pool.Fori(1, B - 1) as b:
                batch(b)
            batch(B - 1, last=True)

        @block.scalar
        def _(act):
            act.sem_inc(M.low_done, 2)
            act.sem_inc(M.down_done, 2)
            act.sem_inc(M.act_done, 2)
            act.sem_inc(M.out_turned, 2)

            def copy_logits(b):
                act.wait_ge(M.logits_done, b + 1)
                act.copy(M.logitsT[:, :], M.ps_x[0][0:NE, :]).then_inc(M.logits_copied, 1)

            def score(b):
                act.wait_ge(M.logits_turned, b + 1)
                act.activation(M.score[:, :, :].rearrange("p t e -> p (t e)"),
                               M.ps_x[1][:, 0:TB * NE], ACT.Sigmoid).then_inc(M.scored, 1)

            def copy_comb(b):
                act.wait_ge(M.comb_turned, b + 2)
                act.wait_ge(M.comb_stored, 16 * b + 16)
                act.copy(M.combT[:, :], M.ps_x[0][0:NE, :]).then_inc(K.comb_copied, 1)

            def relu(b, n):
                k = NX * b + n
                act.wait_ge(M.up_done, k + 1)
                act.wait_ge(M.act_done, k + 1)
                act.activation(M.relu[:, n % 2, :], M.ps_h[n % 2][:, :], ACT.Relu).then_inc(M.relu_done, 1)

            def high(b, n):
                k = NX * b + n
                act.wait_ge(M.act_done, k + 1 + 2)
                act.wait_ge(M.down_done, k + 1)
                act.copy(M.act_h[:, n % 2, :], M.act[:, n % 2, :]).then_inc(M.high_done, 1)

            def copy_out(b):
                act.wait_ge(M.down_done, NX * b + NX + 2)
                act.wait_ge(M.out_turned, 2 * b + 2)
                for c in range(KC):
                    act.copy(M.outT[:, c, :], M.ps_o[c][:, :]).then_inc(M.out_copied, 1)

            relu(0, 0)
            act.wait_ge(M.rw_turned, 1)
            act.wait_ge(M.rw_zeroed, 2)
            act.copy(M.rw_h[:, :, 0:NE], M.ps_x[0][:, 0:KC * NE].rearrange("p (c e) -> p c e", c=KC)
                     ).then_inc(M.rw_high, 1)
            relu(0, 1)
            high(0, 0)
            copy_logits(0)
            score(0)

            def batch(b, first=False, last=False):
                for n in range(NX):
                    later(relu, b, n + 2, last)
                    later(high, b, n + 1, last)
                    if first and n == 2:
                        copy_comb(0)
                        head_spread(act, D, K, M, 1)
                    if not last:
                        if n == 1 and not first:
                            head_spread(act, D, K, M, b + 1)
                        if n == 5:
                            heads_high(act, D, K, M, b + 1)
                        if n == 8:
                            spread(act, D, K, M, b + 1)
                        if n == 10:
                            rows_high(act, D, K, M, b + 1)
                        if n == 11:
                            copy_logits(b + 1)
                        if n == 12:
                            score(b + 1)
                        if n == 19:
                            copy_comb(b + 1)
                copy_out(b)

            batch(0, first=True)
            with act.Fori(1, B - 1) as b:
                batch(b)
            batch(B - 1, last=True)

        @block.vector
        def _(dve):
            STEPS = D.MIX_STEPS

            def over(x, n):
                return x[:, :].unsqueeze(2).to_broadcast([P, TB, n])

            def top_keys(link, vals, n):
                key = M.top_key[:, :, 0:n]
                link(dve.tensor_reduce(M.top_val[:, :], vals, AX.X, ALU.max))
                link(dve.tensor_tensor(key, vals, over(M.top_val, n), ALU.is_equal))
                link(dve.tensor_tensor(key, key, M.order[:, 0:n].unsqueeze(1).to_broadcast([P, TB, n]), ALU.mult))

            def top_hot(link, n, hot):
                key = M.top_key[:, :, 0:n]
                link(dve.tensor_reduce(M.top_val[:, :], key, AX.X, ALU.max))
                link(dve.tensor_tensor(hot, key, over(M.top_val, n), ALU.is_equal))

            def top_one(link, vals, n, hot):
                top_hot(link, n, hot)
                link(dve.scalar_tensor_tensor(vals, hot, FAR, vals, ALU.mult, ALU.add))

            def top_other(link, n, hot, both):
                top_hot(link, n, hot)
                link(dve.tensor_tensor(both, both, hot, ALU.add))

            def route(b, part):
                done = [0, 3, 6, 9, 12, 15, 19, 22, 25, 28, 31, 34][part]
                link = chained(dve, K.dve_step, STEPS * b + 4 + 2 * TB + done)
                groups = [hot[:, :, 0:GROUPS] for hot in (M.first_hot, M.second_hot)]
                chosen, other = M.first_hot[:, :, :], M.second_hot[:, :, :]
                s = M.biased[:, :, :].rearrange("p t (g k) -> p (t g) k", g=GROUPS)

                def pair_sum(at, d):
                    link(dve.tensor_tensor(M.pair_sums[:, :, at:at + GS - d], s[:, :, 0:GS - d],
                                           s[:, :, d:GS], ALU.add))
                if part == 0:
                    dve.wait_ge(M.scored, b + 1)
                    link(dve.tensor_tensor(M.biased[:, :, :], M.score[:, :, :],
                                           K.bias[:, :].unsqueeze(1).to_broadcast([P, TB, NE]), ALU.add))
                    pair_sum(0, 1)
                    pair_sum(3, 2)
                elif part == 1:
                    pair_sum(5, 3)
                    link(dve.tensor_reduce(M.group_score[:, :, :].rearrange("p t g -> p (t g)"),
                                           M.pair_sums[:, :, :], AX.X, ALU.max))
                    link(dve.tensor_copy(M.group_mask[:, :, :], M.group_score[:, :, :]))
                elif part in (2, 4):
                    top_keys(link, M.group_mask[:, :, :], GROUPS)
                elif part == 3:
                    top_one(link, M.group_mask[:, :, :], GROUPS, groups[0])
                elif part == 5:
                    top_other(link, GROUPS, groups[1], groups[0])
                    link(dve.tensor_tensor(
                        M.biased[:, :, :].rearrange("p t (g k) -> p t g k", g=GROUPS),
                        M.biased[:, :, :].rearrange("p t (g k) -> p t g k", g=GROUPS),
                        groups[0].unsqueeze(3).to_broadcast([P, TB, GROUPS, GS]), ALU.mult))
                elif part in (6, 8):
                    top_keys(link, M.biased[:, :, :], NE)
                elif part == 7:
                    top_one(link, M.biased[:, :, :], NE, chosen)
                elif part == 9:
                    top_other(link, NE, other, chosen)
                elif part == 10:
                    link(dve.tensor_tensor(chosen, chosen, M.score[:, :, :], ALU.mult))
                    link(dve.tensor_reduce(M.top_val[:, :], chosen, AX.X, ALU.add))
                    link(dve.tensor_scalar(M.top_val[:, :], M.top_val[:, :], 1e-20, None, ALU.add))
                else:
                    link(dve.reciprocal(M.top_val[:, :], M.top_val[:, :]))
                    dve.wait_ge(M.comb_turned, b + 1)
                    dve.tensor_tensor(M.comb[:, :, :], chosen, over(M.top_val, NE), ALU.mult
                                      ).then_inc(M.comb_ready, 1)

            def add_out(b, pair):
                dve.wait_ge(M.out_turned, 2 * b + pair + 1 + 2)
                dve.wait_ge(M.y_stored, 32 * b + 16)
                rows = entries(K.x_sb, b * TB + 2 * pair, 2)
                dve.tensor_tensor(M.y[:, pair].rearrange("p t e -> p (t e)"),
                                  rows.rearrange("p t e -> p (t e)"), M.ps_t[pair][:, :], ALU.add
                                  ).then_inc(K.y_ready, 1)

            dve.sem_inc(M.high_done, 2)
            dve.wait_ge(M.rw_high, 1)
            dve.tensor_tensor(M.rw_l[:, :, 0:NE], M.ps_x[0][:, 0:KC * NE].rearrange("p (c e) -> p c e", c=KC),
                              M.rw_h[:, :, 0:NE].bitcast(F32), ALU.subtract).then_inc(M.rw_low, 1)
            dve.wait_ge(M.order_set, NE)
            dve.wait_ge(K.router_loaded, 32)
            for part in range(12):
                route(0, part)

            def batch(b, first=False, last=False):
                def next_mix(n):
                    if n == 0:
                        mean_square(dve, D, K, M, b + 1)
                    if n == 1:
                        head_scale(dve, D, K, M, b + 1)
                    if n in (3, 4):
                        norm_heads(dve, D, K, M, b + 1, halves=(n - 3,))
                    if n == 5:
                        heads_low(dve, D, K, M, b + 1)
                    if n == 6:
                        add_rows(dve, D, K, M, b + 1)
                    if n == 7:
                        row_stats(dve, D, K, M, b + 1)
                    if n == 9:
                        norm_rows(dve, D, K, M, b + 1)
                    if n == 10:
                        rows_low(dve, D, K, M, b + 1)
                    if 13 <= n < 19:
                        route(b + 1, 2 * (n - 13))
                        route(b + 1, 2 * (n - 13) + 1)

                for n in range(NX):
                    if not (first and n + 1 < NS):
                        later(lambda b, n: low(dve, b, n), b, n + 1, last)
                    if NS <= n + 2 < NX:
                        activate(dve, b, n + 2)
                    if n in (1, 2) and not first:
                        add_out(b - 1, n - 1)
                    if not last:
                        next_mix(n)

            batch(0, first=True)
            with dve.Fori(1, B - 1) as b:
                batch(b)
            batch(B - 1, last=True)
            add_out(B - 1, 0)
            add_out(B - 1, 1)

        @block.tensor
        def _(pe):
            def logits(b):
                pe.wait_ge(K.xTl_ready, KC * b + KC)
                pe.wait_ge(K.var_ready, b + 1)
                for c in range(KC):
                    ins = matmul3(pe, M.ps_x[0][:, :], [w[:, c, :] for w in (M.rw_h, M.rw_l)],
                                  [rows_T(K, b, low, c) for low in range(2)],
                                  start=c == 0, stop=c == KC - 1)
                ins.then_inc(M.logits_done, 1)

            def turn_logits(b):
                pe.wait_ge(M.logits_copied, b + 1)
                stand(pe, M.passed)
                for t in range(TB):
                    ins = pe.transpose(M.ps_x[1][:, t * NE:(t + 1) * NE],
                                       M.logitsT[:, t * P:(t + 1) * P], K.ident[0:NE, 0:NE])
                ins.then_inc(M.logits_turned, 1)

            def turn_comb(b):
                pe.wait_ge(M.comb_ready, b + 1)
                for t in range(TB):
                    ins = pe.transpose(M.ps_x[0][0:NE, t * P:(t + 1) * P], M.comb[:, t, :], K.ident[:, :])
                ins.then_inc(M.comb_turned, 1)

            def up(b, n):
                pe.wait_ge(M.relu_done, NX * b + n + 1)
                for c in range(KC):
                    ins = matmul3(pe, M.ps_h[n % 2][:, :], [w[:, n, c * P:(c + 1) * P] for w in (K.ffn_h, K.ffn_l)],
                                  [rows_T(K, b, low, c) for low in range(2)],
                                  start=c == 0, stop=c == KC - 1)
                ins.then_inc(M.up_done, 1)

            def down(b, n):
                if n == 0:
                    pe.wait_ge(M.out_copied, KC * b + KC)
                pe.wait_ge(M.low_done, NX * b + n + 1 + 2)
                for c in range(KC):
                    ins = matmul3(pe, M.ps_o[c][:, :],
                                  [w[:, n, E + c * P:E + (c + 1) * P] for w in (K.ffn_h, K.ffn_l)],
                                  [a[:, n % 2, :] for a in (M.act_h, M.act_l)],
                                  start=n == 0, stop=n == NX - 1)
                ins.then_inc(M.down_done, 1)

            def turn_out(b, pair):
                pe.wait_ge(M.out_copied, KC * b + 2 * KC)
                for t in range(2):
                    for c in range(KC):
                        ins = pe.transpose(M.ps_t[pair][:, t * E + c * P:t * E + (c + 1) * P],
                                           M.outT[:, c, (2 * pair + t) * P:(2 * pair + t + 1) * P],
                                           K.ident[:, :])
                ins.then_inc(M.out_turned, 1)

            up(0, 0)
            pe.wait_ge(K.router_loaded, 32)
            for c in range(KC):
                ins = pe.transpose(M.ps_x[0][:, c * NE:(c + 1) * NE], K.rw_raw[:, c * P:(c + 1) * P],
                                   K.ident[0:NE, 0:NE])
            ins.then_inc(M.rw_turned, 1)
            up(0, 1)
            pe.wait_ge(M.rw_low, 1)
            logits(0)
            turn_logits(0)

            def batch(b, first=False, last=False):
                for n in range(NX):
                    later(up, b, n + 2, last)
                    if not first and n < 2:
                        turn_out(b - 1, n)
                    if first and n == 3:
                        turn_comb(0)
                    if not last:
                        if n == 5:
                            turn_heads(pe, D, K, M, b + 1)
                        if n == 6:
                            project_heads(pe, D, K, M, b + 1)
                        if n == 10:
                            turn_rows(pe, D, K, M, b + 1)
                        if n == 11:
                            logits(b + 1)
                        if n == 12:
                            turn_logits(b + 1)
                        if n == 19:
                            turn_comb(b + 1)
                    down(b, n)

            batch(0, first=True)
            with pe.Fori(1, B - 1) as b:
                batch(b)
            batch(B - 1, last=True)
            turn_out(B - 1, 0)
            turn_out(B - 1, 1)


def layer_kernel(nc, x, wq, wk, wv, wo, lq1, lk1, lq2, lk2, router_w, e_bias, w_up, w_down,
                 shared_up, shared_down, out):
    D, S = Shapes(), Tensors()
    kept = {}
    D.B, D.T, D.E = x.shape
    D.HD = lq1.shape[0]
    D.VD = 2 * D.HD
    D.VW = D.VD + 1
    D.KC = D.E // P
    D.TB = D.T // P
    D.SH = 4
    D.ROWS = D.SH * D.HD
    D.G = D.E // D.ROWS
    D.STEPS = D.B * D.G
    D.NE = router_w.shape[0]
    D.NS = shared_up.shape[1] // P
    D.NX = D.NS + D.NE
    D.SCALE = D.HD ** -0.5
    assert D.KC == 2 and D.TB == 4 and D.ROWS == 32 and w_up.shape[2] == P and D.STEPS % 4 == 0 and D.NS == 4 and D.B == 4

    S.x, S.wq, S.wk, S.wv, S.wo, S.lq1, S.lk1, S.lq2, S.lk2 = x, wq, wk, wv, wo, lq1, lk1, lq2, lk2
    S.router_w, S.e_bias, S.w_up, S.w_down = router_w, e_bias, w_up, w_down
    S.shared_up, S.shared_down, S.out = shared_up, shared_down, out
    D.MIX_STEPS = 4 + 2 * D.TB + 35
    D.RING = 4
    S.q = nc.dram_tensor("q_halves", [D.STEPS, D.SH, D.HD, 3, D.T], F32R, kind="Internal").ap()
    S.k = nc.dram_tensor("k_halves", [D.STEPS, D.SH, D.HD, 3, D.T], F32R, kind="Internal").ap()
    S.v = nc.dram_tensor("values", [D.STEPS, P, D.TB * 2 * D.VW], F32, kind="Internal").ap()
    S.comb = nc.dram_tensor("comb_rows", [D.NE, D.B * D.T], F32, kind="Internal").ap()

    with ExitStack() as ctx:
        tensor, _, _ = allocator(nc, ctx, kept)
        tensor("attn", [P, D.STEPS, D.TB * 2 * D.VD])
        tensor("ident", [P, P])
        tensor("wo_h", [P, D.KC, D.E], F32R)
        tensor("wo_l", [P, D.KC, D.E], F32R)
        tensor("ffn_h", [P, D.NX, 2 * D.E], F32R)
        tensor("ffn_l", [P, D.NX, 2 * D.E], F32R)
        tensor("eps_col", [P, 1])
        tensor("neg_lam", [P, 1])
        with ExitStack() as attention:
            tensor, _, _ = allocator(nc, attention, kept)
            tensor("k_ring", [P, D.RING, D.T], F32R)
            tensor("q_ring", [P, D.RING, D.SH, D.T], F32R)
            tensor("v_ring", [P, D.RING, D.TB, 2, D.VW])
            tensor("ident_b", [P, P], BF16)
            tensor("mask_b", [P, D.SH, P], BF16)
            tensor("zeros_b", [P, D.T], BF16)
            kept["part_h"], kept["part_l"] = (kept[w][:, 2 * D.KC:, :] for w in ("ffn_h", "ffn_l"))
            tensor("v_stage", [P, D.B, D.G, D.TB, 2, D.VW])
            kept["x_sb"] = kept["v_stage"][:].rearrange("p b g t h w -> p (b g t h w)")[
                :, 0:D.B * D.TB * D.E].rearrange("p (n e) -> p n e", e=D.E)
            for name in ("x_loaded squared mean_ready head_std_ready dve_step heads_normed heads_turned "
                         "aTh_ready aTl_ready projected var_ready std_ready rows_normed rows_turned "
                         "xTh_ready xTl_ready y_ready comb_copied router_loaded").split():
                kept[name] = attention.enter_context(nc.semaphore("mix_" + name))
            tensor("lam_sum", [P, 2])
            kept["lam_dot"] = attention.enter_context(nc.semaphore("lam_dot"))
            tensor("rw_raw", [D.NE, D.E])
            tensor("bias", [P, D.NE])
            kept["parts_stored"] = attention.enter_context(nc.semaphore("parts_stored"))
            for name in ("kq_loaded", "v_loaded"):
                kept[name] = [attention.enter_context(nc.semaphore(f"{name}{j}")) for j in range(D.RING)]
            K = named(kept)
            project(nc, D, K, S)
            attend(nc, D, K, S)
            experts(nc, D, K, S)


_INS = ['L0_attn_x', 'L0_attn_Wq', 'L0_attn_Wk', 'L0_attn_Wv', 'L0_attn_Wo', 'L0_attn_lq1', 'L0_attn_lk1',
        'L0_attn_lq2', 'L0_attn_lk2', 'L0_ffn_router_weight', 'L0_ffn_e_bias', 'L0_ffn_w_up',
        'L0_ffn_w_down', 'L0_ffn_shared_up', 'L0_ffn_shared_down']


def kernel(**inputs):
    import numpy as _np
    import concourse.bacc as _bacc
    from concourse import mybir as _mybir
    from concourse.bass_utils import run_bass_kernel_spmd as _run

    nc = _bacc.Bacc("TRN2", target_bir_lowering=False, num_devices=1)
    arrays, args = {}, []
    for name in _INS:
        a = _np.ascontiguousarray(inputs[name])
        arrays[f"in_{name}_dram"] = a
        args.append(nc.dram_tensor(f"in_{name}_dram", a.shape, _mybir.dt.from_np(a.dtype), kind="ExternalInput").ap())
    shape = inputs['L0_attn_x'].shape
    out = nc.dram_tensor("out_0_dram", shape, _mybir.dt.float32, kind="ExternalOutput").ap()
    layer_kernel(nc, *args, out)
    r = _run(nc, [arrays], core_ids=[0])
    return r.results[0]["out_0_dram"]
```
